# Optimizing a Trainium2 kernel written in Bass

```python
import numpy as np
import jax
import jax.numpy as jnp

def _softmax(x, axis=-1):
    return jax.nn.softmax(x, axis=axis)

def _gelu(x):
    return jax.nn.gelu(x, approximate=True)

def _silu(x):
    return jax.nn.silu(x)

def _sigmoid(x):
    return jax.nn.sigmoid(x)

def _layernorm(x, axis=-1, eps=1e-05):
    m = jnp.mean(x, axis=axis, keepdims=True)
    v = jnp.var(x, axis=axis, keepdims=True)
    return (x - m) / jnp.sqrt(v + eps)

def _scatter_add(tgt, idx, src, axis=0):
    return tgt.at[idx].add(src)

def _segment_sum(src, seg, n):
    return jax.ops.segment_sum(src, seg, n)
kernel_name = 'mk_adj_ffn_d2_adj_r2_53ece6'

def setup_inputs(seed: int=0):
    np.random.seed(seed)
    _w = jnp.asarray

    def _rec_inputs():
        import jax
        import jax.numpy as jnp
        _gk = jax.random.key(seed)
        x = -0.0005207 + 1.001 * jax.random.normal(jax.random.fold_in(_gk, 1), (128, 64, 128), jnp.float32)
        _a = jax.random.bernoulli(jax.random.fold_in(_gk, 2), 0.0625, (128, 64, 64))
        _a = jnp.logical_or(_a, jnp.swapaxes(_a, -1, -2))
        _a = jnp.logical_or(_a, jnp.eye(64, dtype=bool))
        _af = _a.astype(jnp.float32)
        adj = _af
        return (x, adj)
    x, adj = _rec_inputs()

    def _L0_gnn_setup():
        import jax, jax.numpy as jnp
        import numpy as np
        DIM = 128
        HEADS = 8
        BS = 8
        N = 512
        NEG = -1000000000.0
        key = jax.random.key(seed)
        ks = jax.random.split(key, 8)
        feats = jax.random.normal(ks[0], (BS, N, DIM), dtype=jnp.float32)
        adj_mat = (jax.random.uniform(ks[1], (BS, N, N)) < 0.1).astype(jnp.float32)
        s = 1.0 / np.sqrt(DIM)
        fc_w = jax.random.normal(ks[2], (DIM, DIM * HEADS), dtype=jnp.float32) * s
        fc_b = jnp.zeros((DIM * HEADS,), dtype=jnp.float32)
        q_w = jax.random.normal(ks[3], (DIM, 1), dtype=jnp.float32) * s
        q_b = jnp.zeros((1,), dtype=jnp.float32)
        k_w = jax.random.normal(ks[4], (DIM, 1), dtype=jnp.float32) * s
        k_b = jnp.zeros((1,), dtype=jnp.float32)
        fp_w = jax.random.normal(ks[5], (DIM * HEADS, DIM), dtype=jnp.float32) * (1.0 / np.sqrt(DIM * HEADS))
        fp_b = jnp.zeros((DIM,), dtype=jnp.float32)
        return {'feats': feats, 'adj_mat': adj_mat, 'fc_w': fc_w, 'fc_b': fc_b, 'q_w': q_w, 'q_b': q_b, 'k_w': k_w, 'k_b': k_b, 'fp_w': fp_w, 'fp_b': fp_b}
    _L0_gnn_all = _L0_gnn_setup()
    _L0_gnn_in = {k: v for k, v in _L0_gnn_all.items() if k in ('fc_w', 'fc_b', 'q_w', 'q_b', 'k_w', 'k_b', 'fp_w', 'fp_b')}
    del _L0_gnn_all

    def _L0_ffn_setup():
        import jax, jax.numpy as jnp
        import numpy as np
        B, T, IN_DIM = (64, 128, 128)
        HID, OUT_DIM = (256, 128)
        N_LAYERS, N_EXPERTS, N_SHARED = (2, 16, 1)
        key = jax.random.key(seed)
        ks = jax.random.split(key, 10)
        s = 0.02
        x = jax.random.normal(ks[0], (B, T, IN_DIM), dtype=jnp.float32)
        route_id = jax.random.randint(ks[1], (B,), 0, N_EXPERTS)
        Wi = jax.random.normal(ks[2], (HID, IN_DIM), dtype=jnp.float32) * s
        bi = jnp.zeros((HID,), dtype=jnp.float32)
        Wr = jax.random.normal(ks[3], (N_LAYERS, N_EXPERTS, HID, HID), dtype=jnp.float32) * s
        br = jax.random.normal(ks[4], (N_LAYERS, N_EXPERTS, HID), dtype=jnp.float32) * s
        Ws = jax.random.normal(ks[5], (N_LAYERS, N_SHARED, HID, HID), dtype=jnp.float32) * s
        bs = jax.random.normal(ks[6], (N_LAYERS, N_SHARED, HID), dtype=jnp.float32) * s
        Wo = jax.random.normal(ks[7], (OUT_DIM, HID), dtype=jnp.float32) * s
        bo = jnp.zeros((OUT_DIM,), dtype=jnp.float32)
        return {'x': x, 'route_id': route_id, 'Wi': Wi, 'bi': bi, 'Wr': Wr, 'br': br, 'Ws': Ws, 'bs': bs, 'Wo': Wo, 'bo': bo}
    _L0_ffn_all = _L0_ffn_setup()
    _L0_ffn_in = {k: v for k, v in _L0_ffn_all.items() if k in ('route_id', 'Wi', 'bi', 'Wr', 'br', 'Ws', 'bs', 'Wo', 'bo')}
    del _L0_ffn_all

    def _L1_gnn_setup():
        import jax, jax.numpy as jnp
        import numpy as np
        B, N, F_IN, F_OUT = (8, 1024, 128, 128)
        key = jax.random.key(seed)
        k1, k2, k3, k4 = jax.random.split(key, 4)
        node_features = jax.random.normal(k1, (B, N, F_IN), dtype=jnp.float32)
        adj_matrix = jax.random.uniform(k2, (B, N, N), dtype=jnp.float32)
        lim = 1.0 / np.sqrt(F_IN)
        W = jax.random.uniform(k3, (F_OUT, F_IN), minval=-lim, maxval=lim, dtype=jnp.float32)
        b = jax.random.uniform(k4, (F_OUT,), minval=-lim, maxval=lim, dtype=jnp.float32)
        return {'node_features': node_features, 'adj_matrix': adj_matrix, 'W': W, 'b': b}
    _L1_gnn_all = _L1_gnn_setup()
    _L1_gnn_in = {k: v for k, v in _L1_gnn_all.items() if k in ('W', 'b')}
    del _L1_gnn_all

    def _L1_ffn_setup():
        import jax, jax.numpy as jnp
        import numpy as np
        B, N, D = (16, 2048, 128)
        NUM_EXPERTS, TOP_K, HEADS = (4, 2, 4)
        N_EDGES = 524288
        LN_EPS = 1e-05

        def _layernorm(x, g, b):
            mu = x.mean(-1, keepdims=True)
            var = ((x - mu) ** 2).mean(-1, keepdims=True)
            return (x - mu) * jax.lax.rsqrt(var + LN_EPS) * g + b

        def _forward(x, edge_index, W_gat, att_src, att_dst, b_gat, ln_gamma, ln_beta, W1, b1, W2, b2):
            Bc, Nc, Dc = x.shape
            M = Bc * Nc
            x_flat = x.reshape(M, Dc)
            h = (x_flat @ W_gat).reshape(M, HEADS, NUM_EXPERTS)
            loops = jnp.arange(M, dtype=edge_index.dtype)
            src = jnp.concatenate([edge_index[0], loops])
            dst = jnp.concatenate([edge_index[1], loops])
            a_src = (h * att_src).sum(-1)
            a_dst = (h * att_dst).sum(-1)
            e = jax.nn.leaky_relu(a_src[src] + a_dst[dst], negative_slope=0.2)
            e_max = jax.ops.segment_max(e, dst, num_segments=M)
            ee = jnp.exp(e - e_max[dst])
            denom = jax.ops.segment_sum(ee, dst, num_segments=M)
            alpha = ee / (denom[dst] + 1e-16)
            msg = h[src] * alpha[:, :, None]
            agg = jax.ops.segment_sum(msg, dst, num_segments=M).reshape(M, HEADS * NUM_EXPERTS) + b_gat
            scores = _layernorm(agg, ln_gamma, ln_beta).reshape(M, HEADS, NUM_EXPERTS).mean(1)
            scores = scores.reshape(Bc, Nc, NUM_EXPERTS)
            topk_s, topk_i = jax.lax.top_k(scores, TOP_K)
            w = jax.nn.softmax(topk_s, axis=-1)
            out = jnp.zeros_like(x)
            for ei in range(NUM_EXPERTS):
                g = jnp.where(topk_i == ei, w, 0.0).sum(-1)
                hh = jax.nn.gelu(x @ W1[ei] + b1[ei], approximate=False)
                out = out + g[..., None] * (hh @ W2[ei] + b2[ei])
            return out
        key = jax.random.key(seed)
        ks = jax.random.split(key, 8)
        s = 0.05
        return {'x': jax.random.normal(ks[0], (B, N, D), jnp.float32), 'W_gat': jax.random.normal(ks[1], (D, HEADS * NUM_EXPERTS), jnp.float32) * s, 'att_src': jax.random.normal(ks[2], (HEADS, NUM_EXPERTS), jnp.float32) * s, 'att_dst': jax.random.normal(ks[3], (HEADS, NUM_EXPERTS), jnp.float32) * s, 'b_gat': jnp.zeros((HEADS * NUM_EXPERTS,), jnp.float32), 'ln_gamma': jnp.ones((HEADS * NUM_EXPERTS,), jnp.float32), 'ln_beta': jnp.zeros((HEADS * NUM_EXPERTS,), jnp.float32), 'W1': jax.random.normal(ks[4], (NUM_EXPERTS, D, 2 * D), jnp.float32) * s, 'b1': jnp.zeros((NUM_EXPERTS, 2 * D), jnp.float32), 'W2': jax.random.normal(ks[5], (NUM_EXPERTS, 2 * D, D), jnp.float32) * s, 'b2': jnp.zeros((NUM_EXPERTS, D), jnp.float32), 'edge_index': jax.random.randint(ks[6], (2, N_EDGES), 0, B * N, jnp.int32)}
    _L1_ffn_all = _L1_ffn_setup()
    _L1_ffn_in = {k: v for k, v in _L1_ffn_all.items() if k in ('W_gat', 'att_src', 'att_dst', 'b_gat', 'ln_gamma', 'ln_beta', 'W1', 'b1', 'W2', 'b2', 'edge_index')}
    del _L1_ffn_all
    return {'x': x, 'adj': adj, 'L0_gnn_fc_w': _L0_gnn_in['fc_w'], 'L0_gnn_fc_b': _L0_gnn_in['fc_b'], 'L0_gnn_q_w': _L0_gnn_in['q_w'], 'L0_gnn_q_b': _L0_gnn_in['q_b'], 'L0_gnn_k_w': _L0_gnn_in['k_w'], 'L0_gnn_k_b': _L0_gnn_in['k_b'], 'L0_gnn_fp_w': _L0_gnn_in['fp_w'], 'L0_gnn_fp_b': _L0_gnn_in['fp_b'], 'L0_ffn_route_id': _L0_ffn_in['route_id'], 'L0_ffn_Wi': _L0_ffn_in['Wi'], 'L0_ffn_bi': _L0_ffn_in['bi'], 'L0_ffn_Wr': _L0_ffn_in['Wr'], 'L0_ffn_br': _L0_ffn_in['br'], 'L0_ffn_Ws': _L0_ffn_in['Ws'], 'L0_ffn_bs': _L0_ffn_in['bs'], 'L0_ffn_Wo': _L0_ffn_in['Wo'], 'L0_ffn_bo': _L0_ffn_in['bo'], 'L1_gnn_W': _L1_gnn_in['W'], 'L1_gnn_b': _L1_gnn_in['b'], 'L1_ffn_W_gat': _L1_ffn_in['W_gat'], 'L1_ffn_att_src': _L1_ffn_in['att_src'], 'L1_ffn_att_dst': _L1_ffn_in['att_dst'], 'L1_ffn_b_gat': _L1_ffn_in['b_gat'], 'L1_ffn_ln_gamma': _L1_ffn_in['ln_gamma'], 'L1_ffn_ln_beta': _L1_ffn_in['ln_beta'], 'L1_ffn_W1': _L1_ffn_in['W1'], 'L1_ffn_b1': _L1_ffn_in['b1'], 'L1_ffn_W2': _L1_ffn_in['W2'], 'L1_ffn_b2': _L1_ffn_in['b2'], 'L1_ffn_edge_index': _L1_ffn_in['edge_index']}

def reference(x, adj, L0_gnn_fc_w, L0_gnn_fc_b, L0_gnn_q_w, L0_gnn_q_b, L0_gnn_k_w, L0_gnn_k_b, L0_gnn_fp_w, L0_gnn_fp_b, L0_ffn_route_id, L0_ffn_Wi, L0_ffn_bi, L0_ffn_Wr, L0_ffn_br, L0_ffn_Ws, L0_ffn_bs, L0_ffn_Wo, L0_ffn_bo, L1_gnn_W, L1_gnn_b, L1_ffn_W_gat, L1_ffn_att_src, L1_ffn_att_dst, L1_ffn_b_gat, L1_ffn_ln_gamma, L1_ffn_ln_beta, L1_ffn_W1, L1_ffn_b1, L1_ffn_W2, L1_ffn_b2, L1_ffn_edge_index):
    import jax
    import jax.numpy as jnp

    def _L0_gnn_ref(feats, adj_mat, fc_w, fc_b, q_w, q_b, k_w, k_b, fp_w, fp_b):
        import jax, jax.numpy as jnp
        import numpy as np
        DIM = 128
        HEADS = 8
        BS = 8
        N = 512
        NEG = -1000000000.0
        bs, n, dim = feats.shape
        feat_proj = (feats @ fc_w + fc_b).reshape(bs, n, HEADS, dim).transpose(0, 2, 1, 3)
        q = feat_proj @ q_w + q_b
        k = feat_proj @ k_w + k_b
        logits = q + jnp.swapaxes(k, -1, -2)
        masked = logits + (1.0 - adj_mat[:, None]) * NEG
        masked = jax.nn.leaky_relu(masked, negative_slope=0.01)
        attn = jax.nn.softmax(masked, axis=-1)
        out = attn @ feat_proj
        out = out.transpose(0, 2, 1, 3).reshape(bs, n, HEADS * dim)
        out = out @ fp_w + fp_b + feats
        return jax.nn.sigmoid(out)

    def _L0_ffn_ref(x, route_id, Wi, bi, Wr, br, Ws, bs, Wo, bo):
        import jax, jax.numpy as jnp
        import numpy as np
        B, T, IN_DIM = (64, 128, 128)
        HID, OUT_DIM = (256, 128)
        N_LAYERS, N_EXPERTS, N_SHARED = (2, 16, 1)
        flat = x.reshape(-1, x.shape[-1])
        n_tok = flat.shape[0]
        route = jnp.repeat(route_id, n_tok // route_id.shape[0])
        h = jax.nn.relu(flat @ Wi.T + bi)
        n_layers, n_experts = (Wr.shape[0], Wr.shape[1])
        for l in range(n_layers):
            shared = (jnp.einsum('nd,shd->snh', h, Ws[l]) + bs[l][:, None, :]).mean(axis=0)
            routed = jnp.zeros_like(h)
            for e in range(n_experts):
                ye = h @ Wr[l, e].T + br[l, e]
                routed = routed + jnp.where((route == e)[:, None], ye, 0.0)
            h = jax.nn.relu(shared + routed + h)
        out = h @ Wo.T + bo
        return out.reshape(*x.shape[:-1], out.shape[-1])

    def _L1_gnn_ref(node_features, adj_matrix, W, b):
        import jax, jax.numpy as jnp
        import numpy as np
        B, N, F_IN, F_OUT = (8, 1024, 128, 128)
        degree = jnp.sum(adj_matrix, axis=-1)
        d_inv_sqrt = jnp.power(degree, -0.5)
        d_inv_sqrt = jnp.where(jnp.isinf(d_inv_sqrt), 0.0, d_inv_sqrt)
        norm_adj = adj_matrix * d_inv_sqrt[:, :, None] * d_inv_sqrt[:, None, :]
        transformed = jnp.einsum('bnf,of->bno', node_features, W) + b
        output = jnp.einsum('bnm,bmo->bno', norm_adj, transformed)
        return jax.nn.relu(output)

    def _L1_ffn_ref(x, W_gat, att_src, att_dst, b_gat, ln_gamma, ln_beta, W1, b1, W2, b2, edge_index):
        import jax, jax.numpy as jnp
        import numpy as np
        B, N, D = (16, 2048, 128)
        NUM_EXPERTS, TOP_K, HEADS = (4, 2, 4)
        N_EDGES = 524288
        LN_EPS = 1e-05

        def _layernorm(x, g, b):
            mu = x.mean(-1, keepdims=True)
            var = ((x - mu) ** 2).mean(-1, keepdims=True)
            return (x - mu) * jax.lax.rsqrt(var + LN_EPS) * g + b

        def _forward(x, edge_index, W_gat, att_src, att_dst, b_gat, ln_gamma, ln_beta, W1, b1, W2, b2):
            Bc, Nc, Dc = x.shape
            M = Bc * Nc
            x_flat = x.reshape(M, Dc)
            h = (x_flat @ W_gat).reshape(M, HEADS, NUM_EXPERTS)
            loops = jnp.arange(M, dtype=edge_index.dtype)
            src = jnp.concatenate([edge_index[0], loops])
            dst = jnp.concatenate([edge_index[1], loops])
            a_src = (h * att_src).sum(-1)
            a_dst = (h * att_dst).sum(-1)
            e = jax.nn.leaky_relu(a_src[src] + a_dst[dst], negative_slope=0.2)
            e_max = jax.ops.segment_max(e, dst, num_segments=M)
            ee = jnp.exp(e - e_max[dst])
            denom = jax.ops.segment_sum(ee, dst, num_segments=M)
            alpha = ee / (denom[dst] + 1e-16)
            msg = h[src] * alpha[:, :, None]
            agg = jax.ops.segment_sum(msg, dst, num_segments=M).reshape(M, HEADS * NUM_EXPERTS) + b_gat
            scores = _layernorm(agg, ln_gamma, ln_beta).reshape(M, HEADS, NUM_EXPERTS).mean(1)
            scores = scores.reshape(Bc, Nc, NUM_EXPERTS)
            topk_s, topk_i = jax.lax.top_k(scores, TOP_K)
            w = jax.nn.softmax(topk_s, axis=-1)
            out = jnp.zeros_like(x)
            for ei in range(NUM_EXPERTS):
                g = jnp.where(topk_i == ei, w, 0.0).sum(-1)
                hh = jax.nn.gelu(x @ W1[ei] + b1[ei], approximate=False)
                out = out + g[..., None] * (hh @ W2[ei] + b2[ei])
            return out
        return _forward(x, edge_index, W_gat, att_src, att_dst, b_gat, ln_gamma, ln_beta, W1, b1, W2, b2)
    x = x + _L0_gnn_ref(_layernorm(x, axis=-1), adj, L0_gnn_fc_w, L0_gnn_fc_b, L0_gnn_q_w, L0_gnn_q_b, L0_gnn_k_w, L0_gnn_k_b, L0_gnn_fp_w, L0_gnn_fp_b)
    x = x + _L0_ffn_ref(_layernorm(x, axis=-1), L0_ffn_route_id, L0_ffn_Wi, L0_ffn_bi, L0_ffn_Wr, L0_ffn_br, L0_ffn_Ws, L0_ffn_bs, L0_ffn_Wo, L0_ffn_bo)
    x = x + _L1_gnn_ref(_layernorm(x, axis=-1), adj, L1_gnn_W, L1_gnn_b)
    x = x + _L1_ffn_ref(_layernorm(x, axis=-1), L1_ffn_W_gat, L1_ffn_att_src, L1_ffn_att_dst, L1_ffn_b_gat, L1_ffn_ln_gamma, L1_ffn_ln_beta, L1_ffn_W1, L1_ffn_b1, L1_ffn_W2, L1_ffn_b2, L1_ffn_edge_index)
    return x

_drawn_inputs = setup_inputs


def setup_inputs(seed=0):
    import zlib

    import numpy as np

    out = dict(_drawn_inputs(seed))
    spreads = {'L0_gnn_fc_b': (0.0, 0.436),
     'L0_gnn_fp_b': (0.0, 0.464),
     'L0_ffn_bi': (0.0, 0.396),
     'L0_ffn_bo': (0.0, 0.1),
     'L1_ffn_b_gat': (0.0, 0.315),
     'L1_ffn_ln_gamma': (1.0, 0.6),
     'L1_ffn_ln_beta': (0.0, 0.397),
     'L1_ffn_b1': (0.0, 0.335),
     'L1_ffn_b2': (0.0, 0.1)}
    factors = {'L0_gnn_q_w': 3.335,
     'L0_ffn_Wr': 3.507,
     'L0_ffn_br': 7.431,
     'L0_ffn_Ws': 3.336,
     'L0_ffn_bs': 6.825,
     'L1_ffn_att_src': 8.0,
     'L1_ffn_att_dst': 23.753}
    for name, (base, spread) in spreads.items():
        noise = np.random.default_rng([zlib.crc32(name.encode()), seed]).standard_normal(out[name].shape)
        drawn = base * np.exp(spread * noise) if base else spread * noise
        out[name] = jnp.asarray(drawn.astype(out[name].dtype))
    for name, factor in factors.items():
        out[name] = (out[name] * factor).astype(out[name].dtype)
    return out
```

```python
from contextlib import ExitStack
import concourse.bass as bass
from concourse import mybir
F32 = mybir.dt.float32
BF16 = mybir.dt.bfloat16
I32 = mybir.dt.int32
U32 = mybir.dt.uint32
ALU = mybir.AluOpType
ACT = mybir.ActivationFunctionType
AX = mybir.AxisListType
P = 128

NODES = 8192
HI = NODES // P
EDGES = 524288
EPP = EDGES // P
SEGS = 4
SEG = EPP // SEGS
ROUNDS = 11
SLOTS = 8 * ROUNDS
COLS = SEGS * SLOTS
EPOCHS = -(-SEG // SLOTS)
LIST = EPOCHS * COLS
BATCH = 8
BPE = COLS // BATCH
HB = 16
TAG = 0x20000000
K = 16
SB = 13


def sort_edges(nc, edge_index, hist_keys, lists, counts_out):
    with ExitStack() as ctx:
        def sb(name, shape, dt=F32):
            return ctx.enter_context(nc.sbuf_tensor("e_" + name, shape, dt))

        def ps(name, shape, dt=F32):
            return ctx.enter_context(nc.psum_tensor("e_" + name, shape, dt))

        def sem(name):
            return ctx.enter_context(nc.semaphore("e_" + name))

        src = sb("src", [P, SEG], I32)
        dst = sb("dst", [P, SEG], I32)
        key = sb("key", [P, EPP])
        keyi = key[:, :].bitcast(I32)
        mask = sb("mask", [P, SEG])
        lo = sb("lo", [P, EPP], BF16)
        hi = sb("hi", [P, EPP], BF16)
        tmp = sb("tmp", [P, SEG], I32)
        counts = sb("counts", [P, SEGS])
        countmax = sb("countmax", [P, SEGS])
        edge_steps = sb("edge_steps", [P, EPOCHS])
        top = sb("top", [P, 1])
        n_epochs_f = sb("n_epochs_f", [P, 1])
        n_epochs = sb("n_epochs", [P, 4], I32)
        top_rank = sb("top_rank", [P, 2])
        rounds_i = sb("rounds_i", [P, 2], I32)
        iota_i = sb("iota_i", [P, P], I32)
        iota = sb("iota", [P, P], BF16)
        ident = sb("ident", [P, P], BF16)
        ident_hi = sb("ident_hi", [P, P], BF16)
        later = sb("later", [P, P], BF16)
        zeros = sb("zeros", [P, P], BF16)
        oh_lo = sb("oh_lo", [P, 2, BATCH, P], BF16)
        oh_hi = sb("oh_hi", [P, 2, BATCH, HI], BF16)
        picked = sb("picked", [P, COLS])
        picked_i = picked[:, :].bitcast(I32)
        dec = sb("dec", [P, COLS], I32)
        dec2 = sb("dec2", [P, COLS], I32)
        node_d = sb("node_d", [P, LIST])
        node_s = sb("node_s", [P, LIST], I32)
        rank = sb("rank", [P, LIST])
        slotf = sb("slotf", [P, LIST])
        d8 = sb("d8", [P, 2, BATCH])
        d8i = sb("d8i", [P, 2, BATCH], I32)
        lo8 = sb("lo8", [P, 2, BATCH], I32)
        hi8 = sb("hi8", [P, 2, BATCH], I32)
        lo8b = sb("lo8b", [P, 2, BATCH], BF16)
        hi8b = sb("hi8b", [P, 2, BATCH], BF16)
        same = sb("same", [P, 2, BATCH, P], BF16)
        loT = sb("loT", [P, 2, BATCH, P])
        hist = sb("hist", [P, 2, HI])
        before = sb("before", [P, 2, BATCH])
        inside = sb("inside", [P, 2, BATCH])
        masked = sb("masked", [P, 2, BATCH, HI])

        ps_hist = ps("ps_hist", [P, 512])
        ps_row = ps("ps_row", [P, 2, BATCH, P])
        ps_base = ps("ps_base", [P, 2, BATCH, HI])
        ps_loT = ps("ps_loT", [P, BATCH, P], BF16)

        loaded = [sem(f"loaded{s}") for s in range(SEGS)]
        consts = sem("consts")
        decoded = sem("decoded")
        chain = sem("chain")
        counted = sem("counted")
        maxed = sem("maxed")
        stored = sem("stored")
        steps = [0]

        with nc.Block() as block:
            @block.sync
            def _(sp):
                for s in range(SEGS):
                    if s:
                        sp.wait_ge(decoded, s)
                    e = edge_index.rearrange("two (p e) -> two p e", p=P)
                    sp.dma_start(src[:, :], e[0, :, s * SEG:(s + 1) * SEG]).then_inc(loaded[s], 16)
                    sp.dma_start(dst[:, :], e[1, :, s * SEG:(s + 1) * SEG]).then_inc(loaded[s], 16)
                sp.wait_ge(decoded, SEGS)
                sp.dma_start(hist_keys[0], lo[:, :]).then_inc(stored, 16)
                sp.dma_start(hist_keys[1], hi[:, :]).then_inc(stored, 16)
                sp.wait_ge(stored, 32)

            @block.gpsimd
            def _(pool):
                nc.gpsimd.iota(iota_i[:, :], pattern=[[1, P]], base=0, channel_multiplier=0).then_inc(consts, 1)
                nc.gpsimd.iota(edge_steps[:, :], pattern=[[SLOTS, EPOCHS]], base=0, channel_multiplier=0,
                               allow_small_or_imprecise_dtypes=True).then_inc(consts, 1)
                nc.gpsimd.memset(ident[:, :], 0.0).then_inc(consts, 1)
                nc.gpsimd.memset(ident_hi[:, :], 0.0).then_inc(consts, 1)
                nc.gpsimd.memset(later[:, :], 0.0).then_inc(consts, 1)
                nc.gpsimd.memset(zeros[:, :], 0.0).then_inc(consts, 1)
                nc.gpsimd.memset(rank[:, :], 0.0).then_inc(consts, 1)
                pool.wait_ge(consts, 7)
                nc.gpsimd.tensor_copy(iota[:, :], iota_i[:, :]).then_inc(consts, 1)
                for m, v in ((ident, 1.0), (ident_hi, float(P))):
                    nc.gpsimd.affine_select(out=m[:, :], in_=m[:, :], compare_op=ALU.not_equal, fill=v, base=0,
                                            pattern=[[-1, P]], channel_multiplier=1).then_inc(consts, 1)
                nc.gpsimd.affine_select(out=later[:, :], in_=later[:, :], compare_op=ALU.is_gt, fill=16384.0,
                                        base=0, pattern=[[1, P]], channel_multiplier=-1).then_inc(consts, 1)
                pool.wait_ge(counted, 1)
                nc.gpsimd.partition_all_reduce(countmax[:, :], counts[:, :], P, bass.bass_isa.ReduceOp.max).then_inc(maxed, 1)

            @block.vector
            def _(dve):
                def link(ins):
                    steps[0] += 1
                    ins.then_inc(chain, 1)
                    dve.wait_ge(chain, steps[0])

                for s in range(SEGS):
                    q = slice(s * SEG, (s + 1) * SEG)
                    dve.wait_ge(loaded[s], 32)
                    link(nc.vector.tensor_scalar(dst[:, :], dst[:, :], float(NODES), None, ALU.min))
                    link(nc.vector.tensor_scalar(src[:, :], src[:, :], float(NODES - 1), None, ALU.min))
                    link(nc.vector.tensor_scalar(mask[:, :], dst[:, :], float(NODES), None, ALU.is_lt))
                    link(nc.vector.scalar_tensor_tensor(out=mask[:, :], in0=src[:, :], scalar=float(NODES - 1),
                                                        in1=mask[:, :], op0=ALU.is_lt, op1=ALU.mult))
                    link(nc.vector.tensor_reduce(counts[:, s:s + 1], mask[:, :], AX.X, ALU.add))
                    link(nc.vector.tensor_scalar(tmp[:, :], dst[:, :], SB, TAG, ALU.logical_shift_left, ALU.bitwise_or))
                    link(nc.vector.tensor_tensor(keyi[:, q], tmp[:, :], src[:, :], ALU.bitwise_or))
                    link(nc.vector.tensor_tensor(key[:, q], key[:, q], mask[:, :], ALU.mult))
                    link(nc.vector.tensor_scalar(tmp[:, :], dst[:, :], P - 1, None, ALU.bitwise_and))
                    link(nc.vector.tensor_copy(lo[:, q], tmp[:, :]))
                    link(nc.vector.tensor_scalar(tmp[:, :], dst[:, :], 7, None, ALU.logical_shift_right))
                    link(nc.vector.tensor_scalar(mask[:, :], src[:, :], float(NODES - 1), 256.0, ALU.is_lt, ALU.mult))
                    link(nc.vector.tensor_tensor(hi[:, q], tmp[:, :], mask[:, :], ALU.add))
                    dve.sem_inc(decoded, 1)
                dve.sem_inc(counted, 1)
                dve.wait_ge(consts, 11)
                dve.wait_ge(maxed, 1)
                link(nc.vector.tensor_reduce(top[:, :], countmax[:, :], AX.X, ALU.max))
                link(nc.vector.tensor_scalar(edge_steps[:, :], edge_steps[:, :], top[:, 0:1], None, ALU.is_lt))
                link(nc.vector.tensor_reduce(n_epochs_f[:, :], edge_steps[:, :], AX.X, ALU.add))
                link(nc.vector.tensor_scalar(n_epochs_f[:, :], n_epochs_f[:, :], 1.0, None, ALU.max))
                link(nc.vector.tensor_copy(n_epochs[:, 0:1], n_epochs_f[:, :]))
                link(nc.vector.tensor_scalar(n_epochs[:, 1:2], n_epochs_f[:, :], float(BPE // 2), None, ALU.mult))
        carrier = sem("carrier")
        chain2 = sem("chain2")
        with nc.Block() as block:
            @block.vector
            def _(dve):
                ne = dve.value_load(n_epochs[0:1, 0:1], min_val=1, max_val=EPOCHS)
                N2 = 2 * ROUNDS + 7
                nc.vector.memset(node_d[:, :], float(NODES)).then_inc(chain2, 1)
                nc.vector.memset(node_s[:, :], 0).then_inc(chain2, 1)
                dve.wait_ge(chain2, 2)
                with dve.Fori(0, ne) as ep:
                    k = 2
                    for r in range(ROUNDS):
                        for s in range(SEGS):
                            m8 = picked[:, s * SLOTS + 8 * r:s * SLOTS + 8 * r + 8]
                            ins = nc.vector.max(out=m8, in_=key[:, s * SEG:(s + 1) * SEG])
                        ins.then_inc(chain2, 1)
                        k += 1
                        dve.wait_ge(chain2, ep * N2 + k)
                        dve.sem_inc(carrier, 1)
                        for s in range(SEGS):
                            m8 = picked[:, s * SLOTS + 8 * r:s * SLOTS + 8 * r + 8]
                            sl = key[:, s * SEG:(s + 1) * SEG]
                            ins = nc.vector.match_replace(out=sl, in_to_replace=m8, in_values=sl, imm_value=0.0)
                        ins.then_inc(chain2, 1)
                        k += 1
                        dve.wait_ge(chain2, ep * N2 + k)
                        dve.sem_inc(carrier, 1)
                    q = bass.ds(ep * COLS, COLS)

                    def link(ins):
                        nonlocal k
                        k += 1
                        ins.then_inc(chain2, 1)
                        dve.wait_ge(chain2, ep * N2 + k)
                    link(nc.vector.tensor_scalar(node_s[:, q], picked_i, NODES - 1, None, ALU.bitwise_and))
                    link(nc.vector.tensor_scalar(dec[:, :], picked_i, SB, NODES - 1, ALU.logical_shift_right,
                                                 ALU.bitwise_and))
                    link(nc.vector.tensor_scalar(dec2[:, :], picked[:, :], 0.0, float(NODES), ALU.is_equal, ALU.mult))
                    link(nc.vector.tensor_tensor(node_d[:, q], dec[:, :], dec2[:, :], ALU.add))
                    link(nc.vector.tensor_copy(dec[:, 0:8], dec[:, 0:8]))
                    link(nc.vector.tensor_copy(dec[:, 0:8], dec[:, 0:8]))
                    link(nc.vector.tensor_copy(dec[:, 0:8], dec[:, 0:8]))
                    assert k == N2 + 2

        d_ready = sem("d_ready")
        dchain = sem("dchain")
        oh_ready = sem("oh_ready")
        oh_free = sem("oh_free")
        loT_ps = sem("loT_ps")
        loT_sb = sem("loT_sb")
        rows = sem("rows")
        rows_free = sem("rows_free")
        hist_sb = sem("hist_sb")
        hist_up = sem("hist_up")
        base_ready = sem("base_ready")
        base_free = sem("base_free")
        ranked = sem("ranked")
        rchain = sem("rchain")
        lstored = sem("lstored")
        rstored = sem("rstored")
        topped = sem("topped")
        last_steps = sem("last_steps")
        with nc.Block() as block:
            @block.sync
            def _(sp):
                sp.dma_start(lists[1], node_s[:, :].bitcast(F32)).then_inc(lstored, 16)
                sp.wait_ge(ranked, 1)
                sp.dma_start(lists[2], rank[:, :]).then_inc(rstored, 16)
                sp.dma_start(lists[0], slotf[:, :]).then_inc(rstored, 16)
                sp.wait_ge(ranked, 2)
                sp.dma_start(counts_out, n_epochs[:, :]).then_inc(rstored, 16)
                sp.wait_ge(lstored, 16)
                sp.wait_ge(rstored, 48)

            @block.gpsimd
            def _(pool):
                pool.wait_ge(topped, 1)
                nc.gpsimd.partition_all_reduce(top_rank[:, 1:2], top_rank[:, 0:1], P,
                                               bass.bass_isa.ReduceOp.max).then_inc(topped, 1)

            @block.tensor
            def _(pe):
                n = pe.value_load(n_epochs[0:1, 1:2], min_val=1, max_val=EPOCHS * BPE // 2)
                nc.tensor.matmul(ps_hist[:, 0:HI], zeros[:, :], zeros[:, 0:HI], start=True, stop=False,
                                 skip_group_check=True).then_inc(hist_up, 1)
                with pe.Fori(0, n) as i:
                    for u in (0, 1):
                        g = 2 * i + u
                        pe.wait_ge(oh_ready, g + 1)
                        pe.wait_ge(loT_sb, g + 1)
                        for k in range(BATCH):
                            mm = nc.tensor.transpose(ps_loT[:, k], oh_lo[:, u, k], ident[:, :])
                        mm.then_inc(loT_ps, 1)
                        pe.wait_ge(rows_free, g + 1)
                        for k in range(BATCH):
                            nc.tensor.matmul(ps_row[:, u, k], lo8b[:, u, k:k + 1].to_broadcast([P, P]), ident[:, :],
                                             start=True, stop=False)
                            nc.tensor.matmul(ps_row[:, u, k], hi8b[:, u, k:k + 1].to_broadcast([P, P]),
                                             ident_hi[:, :], start=False, stop=False)
                            mm = nc.tensor.matmul(ps_row[:, u, k], later[:, :], ident[:, :], start=False, stop=True)
                        mm.then_inc(rows, 1)
                        pe.wait_ge(loT_sb, g + 2)
                        pe.wait_ge(base_free, g + 1)
                        for k in range(BATCH):
                            pe.wait_ge(hist_sb, g * BATCH + k + 1)
                            bm = nc.tensor.matmul(ps_base[:, u, k], loT[:, u, k], hist[:, k % 2], start=True, stop=True)
                            mm = nc.tensor.matmul(ps_hist[:, 0:HI], oh_lo[:, u, k], oh_hi[:, u, k], start=False,
                                                  stop=False, skip_group_check=True)
                            mm.then_inc(hist_up, 1)
                            if k == BATCH - 1:
                                bm.then_inc(base_ready, 1)
                        pe.wait_ge(hist_up, (g + 1) * BATCH + 1)
                        pe.sem_inc(oh_free, 1)

            @block.scalar
            def _(act):
                act.sem_inc(loT_sb, 1)
                n = act.value_load(n_epochs[0:1, 1:2], min_val=1, max_val=EPOCHS * BPE // 2)
                with act.Fori(0, n) as i:
                    for u in (0, 1):
                        g = 2 * i + u
                        act.wait_ge(loT_ps, g + 1)
                        nc.scalar.copy(loT[:, u], ps_loT[:, :, :]).then_inc(loT_sb, 1)
                        for k in range(BATCH):
                            act.wait_ge(hist_up, g * BATCH + k + 1)
                            nc.scalar.copy(hist[:, k % 2], ps_hist[:, 0:HI]).then_inc(hist_sb, 1)

            @block.vector
            def _(dve):
                n = dve.value_load(n_epochs[0:1, 1:2], min_val=1, max_val=EPOCHS * BPE // 2)
                dve.sem_inc(rows_free, 2)
                dve.sem_inc(oh_free, 2)
                dve.sem_inc(base_free, 2)
                NC = 6 * 2
                NR = 5 * 2

                def onehots(i, u, kk):
                    g = 2 * i + u
                    k = kk * 6
                    dve.wait_ge(oh_free, g + 1)

                    def link(ins):
                        nonlocal k
                        k += 1
                        ins.then_inc(dchain, 1)
                        dve.wait_ge(dchain, i * NC + k)
                    link(nc.vector.tensor_copy(d8[:, u], node_d[:, bass.ds(g * BATCH, BATCH)]))
                    link(nc.vector.tensor_copy(d8i[:, u], d8[:, u]))
                    link(nc.vector.tensor_scalar(lo8[:, u], d8i[:, u], P - 1, None, ALU.bitwise_and))
                    link(nc.vector.tensor_scalar(hi8[:, u], d8i[:, u], 7, None, ALU.logical_shift_right))
                    link(nc.vector.tensor_copy(lo8b[:, u], lo8[:, u]))
                    link(nc.vector.tensor_copy(hi8b[:, u], hi8[:, u]))
                    nc.vector.tensor_tensor(oh_lo[:, u, 0:BATCH], lo8b[:, u].unsqueeze(2).to_broadcast([P, BATCH, P]),
                                            iota[:, :].unsqueeze(1).to_broadcast([P, BATCH, P]), ALU.is_equal)
                    nc.vector.tensor_tensor(oh_hi[:, u, 0:BATCH], hi8b[:, u].unsqueeze(2).to_broadcast([P, BATCH, HI]),
                                            iota[:, 0:HI].unsqueeze(1).to_broadcast([P, BATCH, HI]),
                                            ALU.is_equal).then_inc(oh_ready, 1)

                def ranks(i, u):
                    g = 2 * i + u
                    k = u * 5

                    def link(ins):
                        nonlocal k
                        k += 1
                        ins.then_inc(rchain, 1)
                        dve.wait_ge(rchain, i * NR + k)
                    dve.wait_ge(rows, g + 1)
                    link(nc.vector.tensor_tensor(same[:, u], ps_row[:, u], d8[:, u].unsqueeze(2).to_broadcast([P, BATCH, P]),
                                                 ALU.is_equal))
                    dve.sem_inc(rows_free, 1)
                    link(nc.vector.tensor_reduce(inside[:, u], same[:, u], AX.X, ALU.add))
                    dve.wait_ge(base_ready, g + 1)
                    link(nc.vector.tensor_tensor(masked[:, u], ps_base[:, u], oh_hi[:, u, 0:BATCH], ALU.mult))
                    dve.sem_inc(base_free, 1)
                    link(nc.vector.tensor_reduce(before[:, u], masked[:, u], AX.X, ALU.add))
                    link(nc.vector.tensor_tensor(rank[:, bass.ds(g * BATCH, BATCH)], before[:, u], inside[:, u], ALU.add))

                with dve.Fori(0, n) as i:
                    onehots(i, 0, 0)
                    onehots(i, 1, 1)
                    ranks(i, 0)
                    ranks(i, 1)
                valid = node_d
                seq = [0]

                def link(ins):
                    seq[0] += 1
                    ins.then_inc(last_steps, 1)
                    dve.wait_ge(last_steps, seq[0])
                link(nc.vector.scalar_tensor_tensor(out=slotf[:, :], in0=node_d[:, :], scalar=float(K), in1=rank[:, :],
                                                    op0=ALU.mult, op1=ALU.add))
                dve.sem_inc(ranked, 1)
                link(nc.vector.tensor_scalar(valid[:, :], node_d[:, :], float(NODES), None, ALU.is_lt))
                link(nc.vector.tensor_tensor(valid[:, :], valid[:, :], rank[:, :], ALU.mult))
                link(nc.vector.tensor_reduce(top_rank[:, 0:1], valid[:, :], AX.X, ALU.max))
                dve.sem_inc(topped, 1)
                dve.wait_ge(topped, 2)
                link(nc.vector.tensor_copy(rounds_i[:, 0:1], top_rank[:, 1:2]))
                link(nc.vector.tensor_scalar(rounds_i[:, 1:2], rounds_i[:, 0:1], 4, None, ALU.logical_shift_right))
                link(nc.vector.tensor_scalar(n_epochs[:, 2:3], rounds_i[:, 1:2], 1.0, None, ALU.add))
                link(nc.vector.tensor_copy(n_epochs[:, 3:4], rounds_i[:, 0:1]))
                dve.sem_inc(ranked, 1)

TILES = NODES // P
DIM = 128
HEADS = 8
NB = 64
HID = 256
EXP0 = 16
LAYERS = 2
WROW = LAYERS * 2 * HID + LAYERS * 2
EPS = 1e-5
NEG = 1e9
SLOPE = 0.01
GH = 4
GE = 4
GAT = GH * GE
ROW = GAT + GH
COLS24 = GAT + 2 * GH


def node_layers(nc, w, x_all, hg_all, xT_dram, table):
    with ExitStack() as ctx:
        def sb(name, shape, dt=F32):
            return ctx.enter_context(nc.sbuf_tensor("n_" + name, shape, dt))

        def ps(name, shape, dt=F32):
            return ctx.enter_context(nc.psum_tensor("n_" + name, shape, dt))

        def sem(name):
            return ctx.enter_context(nc.semaphore("n_" + name))

        M = sb("M", [P, HEADS, DIM])
        kw = sb("kw", [P, 32])
        qw = sb("qw", [P, 32])
        cb = sb("cb", [1, DIM])
        head_c = sb("head_c", [1, HEADS])
        wiT = sb("wiT", [P, HID])
        bi = sb("bi", [P, 2])
        woT = sb("woT", [P, 2, DIM])
        bo = sb("bo", [1, DIM])
        gW = sb("gW", [P, DIM])
        gb = sb("gb", [1, DIM])
        w24 = sb("w24", [P, COLS24])
        ident = sb("ident", [P, P])
        ones = sb("ones", [1, P])
        half = sb("half", [P, 2])
        route = sb("route", [1, TILES], I32)
        adj = sb("adj", [P, TILES, NB])
        BD = sb("BD", [P, TILES, P])
        deg = sb("deg", [P, TILES])
        dinv = sb("dinv", [P, TILES])
        ps_all = [[ps(f"b{u}{k}", [P, 512]) for k in range(4)] for u in (0, 1)]
        A = [ps_all[u][0] for u in (0, 1)]
        Z = [ps_all[u][1] for u in (0, 1)]
        U = [[ps_all[u][2], ps_all[u][3]] for u in (0, 1)]
        wdram = nc.dram_tensor("n_weff", [EXP0, P, WROW], F32).ap()

        with ExitStack() as tctx:
            def tsb(name, shape, dt=F32):
                return tctx.enter_context(nc.sbuf_tensor("s_" + name, shape, dt))

            def tsem(name):
                return tctx.enter_context(nc.semaphore("s_" + name))
            fcT = tsb("fcT", [P, HEADS, DIM])
            fp = tsb("fp", [P, HEADS, DIM])
            fcb = tsb("fcb", [P, HEADS])
            qk = tsb("qk", [P, 4])
            small = tsb("small", [1, 2 * DIM])
            wsI = tsb("wsI", [P, WROW])
            wr = tsb("wr", [P, 2, WROW])
            att = tsb("att", [P, 2, GAT])
            attw = tsb("attw", [P, 2, GAT])
            pos = tsb("pos", [P, TILES])
            pos_mask = tsb("pos_mask", [P, TILES])
            ld = tsem("ld")
            ldb = tsem("ldb")
            chain = tsem("chain")
            consts = tsem("consts")
            summed = tsem("summed")
            folded = tsem("folded")
            powed = tsem("powed")
            wl = [tsem("wl0"), tsem("wl1")]
            wadd = tsem("wadd")
            wst = [tsem("wst0"), tsem("wst1")]
            k = [0]
            NLD = 21

            with nc.Block() as block:
                @block.sync
                def _(sp):
                    for dst, src in (
                        (fcT[:, :, :], w["fcT"].rearrange("(h c) d -> c h d", c=DIM)),
                        (fp[:, :, :], w["fp"].rearrange("(h c) d -> c h d", c=DIM)),
                        (fcb[:, :], w["fcbT"]),
                        (qk[:, 0:1], w["q_w"]), (qk[:, 1:2], w["k_w"]),
                        (small[:, 0:DIM], w["fp_b"].unsqueeze(0)),
                        (small[:, DIM:DIM + 1], w["q_b"].unsqueeze(0)),
                        (small[:, DIM + 1:DIM + 2], w["k_b"].unsqueeze(0)),
                        (wiT[:, :], w["WiT"]), (bi[:, :], w["biT"]),
                        (woT[:, :, :], w["WoT"].rearrange("(c p) o -> p c o", p=P)),
                        (bo[:, :], w["bo"].unsqueeze(0)),
                        (gW[:, :], w["gWT"]), (gb[:, :], w["gb"].unsqueeze(0)),
                        (w24[:, 0:GAT], w["Wgat"]),
                        (att[:, 0], w["att_src"].partition_broadcast(P)),
                        (att[:, 1], w["att_dst"].partition_broadcast(P)),
                        (route[:, :], w["route"].unsqueeze(0)),
                        (wsI[:, 0:LAYERS * 2 * HID], w["WsT"]),
                        (wsI[:, LAYERS * 2 * HID:WROW], w["bsT"]),
                        (adj[:, :, :], w["adj"].rearrange("(t b) i j -> (b i) t j", b=2)),
                    ):
                        sp.dma_start(dst, src).then_inc(ld, 16)
                    sp.wait_ge(consts, 8)
                    for b in (0, 1):
                        sp.dma_start(BD[b * NB:(b + 1) * NB, :, b * NB:(b + 1) * NB],
                                     w["adjT"].rearrange("(t b) m i -> b m t i", b=2)[b]).then_inc(ldb, 16)
                    sp.dma_start(x_all[:, :, :], w["x"].rearrange("(t b) n d -> (b n) t d", b=2)).then_inc(ldb, 16)
                    for e in range(EXP0 + 1):
                        if e < EXP0:
                            u = e % 2
                            if e >= 2:
                                sp.wait_ge(wst[u], 16 * (e // 2))
                            sp.dma_start(wr[:, u, 0:LAYERS * 2 * HID], w["WrT"][e]).then_inc(wl[u], 16)
                            sp.dma_start(wr[:, u, LAYERS * 2 * HID:WROW], w["brT"][e]).then_inc(wl[u], 16)
                        if e >= 1:
                            v = (e - 1) % 2
                            sp.wait_ge(wadd, e)
                            sp.dma_start(wdram[e - 1], wr[:, v, :]).then_inc(wst[v], 16)
                    for v in (0, 1):
                        sp.wait_ge(wst[v], 16 * (EXP0 // 2))
                    sp.wait_ge(ldb, 48)

                @block.gpsimd
                def _(pool):
                    nc.gpsimd.memset(ident[:, :], 0.0).then_inc(consts, 1)
                    nc.gpsimd.memset(ones[:, :], 1.0).then_inc(consts, 1)
                    nc.gpsimd.memset(half[:, :], -0.5).then_inc(consts, 1)
                    nc.gpsimd.memset(pos[:, :], -0.5).then_inc(consts, 1)
                    nc.gpsimd.memset(kw[:, :], 0.0).then_inc(consts, 1)
                    nc.gpsimd.memset(qw[:, :], 0.0).then_inc(consts, 1)
                    nc.gpsimd.memset(BD[:, :, :], 0.0).then_inc(consts, 1)
                    pool.wait_ge(consts, 7)
                    nc.gpsimd.affine_select(out=ident[:, :], in_=ident[:, :], compare_op=ALU.not_equal, fill=1.0,
                                            base=0, pattern=[[-1, P]], channel_multiplier=1).then_inc(consts, 1)
                    pool.wait_ge(summed, 1)
                    nc.gpsimd.tensor_tensor(dinv[:, :], deg[:, :], pos[:, :], ALU.pow).then_inc(powed, 1)

                @block.vector
                def _(dve):
                    def link(ins):
                        k[0] += 1
                        ins.then_inc(chain, 1)
                        dve.wait_ge(chain, k[0])
                    dve.wait_ge(ld, 16 * NLD)
                    dve.wait_ge(consts, 8)
                    link(nc.vector.tensor_reduce(dinv[:, :], adj[:, :, :], AX.X, ALU.add))
                    link(nc.vector.tensor_scalar(deg[:, :], dinv[:, :], 1e-30, None, ALU.max))
                    link(nc.vector.tensor_scalar(pos_mask[:, :], dinv[:, :], 0.0, None, ALU.not_equal))
                    dve.sem_inc(summed, 1)
                    dve.wait_ge(powed, 1)
                    link(nc.vector.tensor_tensor(dinv[:, :], dinv[:, :], pos_mask[:, :], ALU.mult))
                    link(nc.vector.tensor_scalar(adj[:, :, :], adj[:, :, :], 1.0, NEG, ALU.subtract, ALU.mult))
                    link(nc.vector.tensor_tensor(qk[:, 2:3], qk[:, 0:1], qk[:, 1:2], ALU.add))
                    link(nc.vector.tensor_tensor(small[:, DIM + 2:DIM + 3], small[:, DIM:DIM + 1],
                                                 small[:, DIM + 1:DIM + 2], ALU.add))
                    for s in (0, 1):
                        link(nc.vector.tensor_tensor(attw[:, s], w24[:, 0:GAT], att[:, s], ALU.mult))
                        link(nc.vector.tensor_reduce(w24[:, GAT + s * GH:GAT + (s + 1) * GH],
                                                     attw[:, s].rearrange("p (h e) -> p h e", h=GH), AX.X, ALU.add))
                    for l in range(LAYERS):
                        for c in (0, 1):
                            q = (l * 2 + c) * HID + c * P
                            link(nc.vector.tensor_tensor(wsI[:, q:q + P], wsI[:, q:q + P], ident[:, :], ALU.add))
                    dve.sem_inc(folded, 1)
                    dve.wait_ge(folded, 2)
                    link(nc.vector.tensor_copy(M[:, 0:4], A[0][:, :].rearrange("p (h d) -> p h d", h=4)))
                    link(nc.vector.tensor_copy(M[:, 4:8], A[1][:, :].rearrange("p (h d) -> p h d", h=4)))
                    qkp = Z[0][:, 0:16].rearrange("p (h s) -> p h s", s=2)
                    link(nc.vector.tensor_copy(qw[:, 0:HEADS], qkp[:, :, 0]))
                    link(nc.vector.tensor_copy(kw[:, 0:HEADS], qkp[:, :, 1]))
                    link(nc.vector.tensor_tensor(cb[:, :], Z[1][0:1, 0:DIM], small[:, 0:DIM], ALU.add))
                    link(nc.vector.tensor_scalar(head_c[:, :], Z[1][0:1, DIM:DIM + HEADS], small[:, DIM + 2:DIM + 3],
                                                 None, ALU.add))
                    for e in range(EXP0):
                        u = e % 2
                        dve.wait_ge(wl[u], 32 * (e // 2 + 1))
                        nc.vector.tensor_tensor(wr[:, u, :], wr[:, u, :], wsI[:, :], ALU.add).then_inc(wadd, 1)

                @block.tensor
                def _(pe):
                    pe.wait_ge(folded, 1)
                    for h in range(HEADS):
                        nc.tensor.matmul(A[h // 4][:, (h % 4) * DIM:(h % 4 + 1) * DIM], fcT[:, h], fp[:, h],
                                         start=True, stop=True)
                        nc.tensor.matmul(Z[0][:, 2 * h:2 * h + 2], fcT[:, h], qk[:, 0:2], start=True, stop=True)
                    for h in range(HEADS):
                        nc.tensor.matmul(Z[1][0:1, 0:DIM], fcb[:, h:h + 1], fp[:, h], start=(h == 0),
                                         stop=(h == HEADS - 1))
                    nc.tensor.matmul(Z[1][0:1, DIM:DIM + HEADS], qk[:, 2:3], fcb[:, :], start=True,
                                     stop=True).then_inc(folded, 1)

        f = sb("f", [P, 2, DIM])
        fT = sb("fT", [P, 2, P])
        stats = sb("stats", [P, 2, 6])
        mv = sb("mv", [P, 2, 2])
        ve = sb("ve", [P, 2])
        rstd = sb("rstd", [P, 2])
        delta = sb("delta", [64, HEADS])
        kd = sb("kd", [P, 2, HEADS, NB])
        sel = sb("sel", [P, 2, P])
        z = sb("z", [P, 2, HEADS, NB])
        z2 = sb("z2", [P, 2, HEADS, NB])
        zmax = sb("zmax", [P, 2, HEADS])
        zsum = sb("zsum", [P, 2, HEADS])
        atT = sb("atT", [P, 2, HEADS, NB])
        UT = sb("UT", [P, 2, HEADS, 2, NB])
        s_ = sb("s_", [P, 2, DIM])
        h1 = sb("h1", [P, 2, 2, P])
        h2 = sb("h2", [P, 2, 2, P])
        wbuf = sb("wbuf", [P, 2, WROW])
        dcol = sb("dcol", [P, 2])
        srow = sb("srow", [1, 2, P])
        prime = sb("prime", [1, 2, TILES], I32)
        VT = sb("VT", [P, 2, P])
        NCH = 42

        S = {n: sem(n) for n in (
            "dve", "init", "consts2", "ve_ready", "rstd_ready", "f_ready", "tr", "fT_ready", "kq", "q_in_sel", "kd_ready",
            "z_ready", "sub", "exp", "attn", "atT_ps", "atT_sb", "U_ps", "UT0", "UT1", "y", "neg", "sig",
            "H1", "h1r", "L1", "h2r", "L2", "h3r", "fo", "w_ready0", "w_ready1", "L2free", "fd", "V", "Vsb",
            "gnn", "carrier", "hg", "hg_sb", "xT0", "xT1", "stored")}
        wr_s = [S["w_ready0"], S["w_ready1"]]
        xT_s = [S["xT0"], S["xT1"]]

        def n1(i, u):
            return 2 * i + u + 1

        with nc.Block() as block:
            @block.sync
            def _(sp):
                for u in (0, 1):
                    sp.dma_start(prime[:, u], w["route"].unsqueeze(0)).then_inc(xT_s[u], 16)
                with sp.Fori(0, TILES // 2) as i:
                    for u in (0, 1):
                        sp.wait_ge(S["L2free"], n1(i, u))
                        e = sp.value_load(route[0:1, bass.ds(2 * i + u, 1)], min_val=0, max_val=EXP0 - 1)
                        sp.dma_start(wbuf[:, u, :], wdram[bass.ds(e, 1)].squeeze(0)).then_inc(wr_s[u], 16)
                    for u in (0, 1):
                        sp.wait_ge(S["fT_ready"], 3 * n1(i, u) if u else 6 * i + 5)
                        sp.dma_start(xT_dram[:, bass.ds((2 * i + u) * P, P)], fT[:, u]).then_inc(xT_s[u], 16)
                for u in (0, 1):
                    sp.wait_ge(xT_s[u], 16 * (TILES // 2) + 16)
                sp.wait_ge(S["hg_sb"], TILES)
                sp.dma_start(table.rearrange("(t p) c -> p t c", p=P), hg_all[:, :, 0:ROW]).then_inc(S["stored"], 16)
                sp.wait_ge(S["stored"], 16)

            @block.gpsimd
            def _(pool):
                nc.gpsimd.memset(kd[:, :, :, :], 0.0).then_inc(S["consts2"], 1)
                nc.gpsimd.memset(sel[:, :, :], 0.0).then_inc(S["consts2"], 1)
                nc.gpsimd.memset(delta[:, :], 0.0).then_inc(S["consts2"], 1)
                pool.wait_ge(S["consts2"], 3)
                for b in (0, 1):
                    nc.gpsimd.affine_select(out=delta[32 * b:32 * b + 32, :], in_=delta[32 * b:32 * b + 32, :],
                                            compare_op=ALU.not_equal, fill=1.0, base=0, pattern=[[-1, HEADS]],
                                            channel_multiplier=1).then_inc(S["consts2"], 1)
                for u in (0, 1):
                    nc.gpsimd.affine_select(out=kd[64:96, u], in_=kd[64:96, u], compare_op=ALU.not_equal, fill=1.0,
                                            base=0, pattern=[[-1, HEADS], [0, NB]],
                                            channel_multiplier=1).then_inc(S["consts2"], 1)
                    for b in (0, 1):
                        nc.gpsimd.memset(sel[32 * b:32 * b + 32, u, b * NB:(b + 1) * NB], 1.0).then_inc(S["consts2"], 1)
                    nc.gpsimd.memset(sel[96:97, u, :], 1.0).then_inc(S["consts2"], 1)
                with pool.Fori(0, TILES // 2) as i:
                    for ln in range(4):
                        for u in (0, 1):
                            pool.wait_ge(S["ve_ready"], 8 * i + 2 * ln + u + 1)
                            nc.gpsimd.tensor_tensor(rstd[:, u:u + 1], ve[:, u:u + 1], half[:, u:u + 1],
                                                    ALU.pow).then_inc(S["rstd_ready"], 1)

            @block.vector
            def _(dve):
                dve.wait_ge(S["consts2"], 13)
                for u in (0, 1):
                    nc.vector.tensor_copy(kd[96:97, u], head_c[:, :].unsqueeze(2).to_broadcast([1, HEADS, NB])
                                          ).then_inc(S["init"], 1)
                dve.wait_ge(S["init"], 2)
                with dve.Fori(0, TILES // 2) as i:
                    cnt = 0

                    def link(ins):
                        nonlocal cnt
                        cnt += 1
                        ins.then_inc(S["dve"], 1)
                        dve.wait_ge(S["dve"], i * NCH + cnt)

                    def norm_stats(ln):
                        for u in (0, 1):
                            xt = x_all[:, bass.ds(2 * i + u, 1), :].squeeze(1)
                            dve.sem_inc(S["carrier"], 1)
                            link(nc.vector.bn_stats(stats[:, u], xt))
                            dve.sem_inc(S["carrier"], 1)
                            link(nc.vector.bn_aggr(mv[:, u], stats[:, u]))
                            nc.vector.tensor_scalar(ve[:, u:u + 1], mv[:, u, 1:2], EPS, None,
                                                    ALU.add).then_inc(S["ve_ready"], 1)

                    def norm(ln, scaled=False):
                        norm_stats(ln)
                        for u in (0, 1):
                            xt = x_all[:, bass.ds(2 * i + u, 1), :].squeeze(1)
                            dve.wait_ge(S["rstd_ready"], 8 * i + 2 * ln + u + 1)
                            r = rstd[:, u:u + 1]
                            if scaled:
                                dt = dinv[:, bass.ds(2 * i + u, 1)]
                                link(nc.vector.tensor_copy(dcol[:, u:u + 1], dt))
                                link(nc.vector.tensor_tensor(ve[:, u:u + 1], r, dcol[:, u:u + 1], ALU.mult))
                                r = ve[:, u:u + 1]
                            nc.vector.tensor_scalar(f[:, u], xt, mv[:, u, 0:1], r, ALU.subtract,
                                                    ALU.mult).then_inc(S["fd"] if scaled else S["f_ready"], 1)

                    def bc(ap, n=NB):
                        return ap.unsqueeze(2).to_broadcast([P, HEADS, n])
                    norm(0)
                    for u in (0, 1):
                        dve.wait_ge(S["kq"], n1(i, u))
                        nc.vector.tensor_tensor(kd[0:64, u], A[u][0:64, 256:256 + NB].unsqueeze(1).to_broadcast([64, HEADS, NB]),
                                                delta[:, :].unsqueeze(2).to_broadcast([64, HEADS, NB]),
                                                ALU.mult).then_inc(S["kd_ready"], 1)
                    for u in (0, 1):
                        dve.wait_ge(S["z_ready"], n1(i, u))
                        m = adj[:, bass.ds(2 * i + u, 1), :].to_broadcast([P, HEADS, NB])
                        link(nc.vector.tensor_tensor(z[:, u], Z[u][:, :].rearrange("p (h j) -> p h j", h=HEADS), m, ALU.add))
                        link(nc.vector.scalar_tensor_tensor(out=z2[:, u], in0=z[:, u], scalar=SLOPE, in1=z[:, u],
                                                            op0=ALU.mult, op1=ALU.max))
                        link(nc.vector.tensor_reduce(zmax[:, u], z2[:, u], AX.X, ALU.max))
                        nc.vector.tensor_tensor(z[:, u], z2[:, u], bc(zmax[:, u]), ALU.subtract).then_inc(S["sub"], 1)
                    for u in (0, 1):
                        dve.wait_ge(S["exp"], n1(i, u))
                        link(nc.vector.tensor_reduce(zsum[:, u], z2[:, u], AX.X, ALU.add))
                        link(nc.vector.reciprocal(zsum[:, u], zsum[:, u]))
                        nc.vector.tensor_tensor(z[:, u], z2[:, u], bc(zsum[:, u]), ALU.mult).then_inc(S["attn"], 1)
                    for u in (0, 1):
                        dve.wait_ge(S["U_ps"], n1(i, u))
                        nc.vector.tensor_copy(UT[:, u, :, 1, :], U[u][1][:, :].rearrange("p (h j) -> p h j", h=HEADS)
                                              ).then_inc(S["UT1"], 1)
                    for u in (0, 1):
                        dve.wait_ge(S["y"], n1(i, u))
                        nc.vector.tensor_tensor(s_[:, u], A[u][:, 0:DIM], f[:, u], ALU.add).then_inc(S["neg"], 1)
                    for u in (0, 1):
                        xt = x_all[:, bass.ds(2 * i + u, 1), :].squeeze(1)
                        dve.wait_ge(S["sig"], n1(i, u))
                        link(nc.vector.tensor_scalar(s_[:, u], s_[:, u], 1.0, None, ALU.add))
                        link(nc.vector.reciprocal(s_[:, u], s_[:, u]))
                        link(nc.vector.tensor_tensor(xt, xt, s_[:, u], ALU.add))
                    norm(1)
                    for u in (0, 1):
                        xt = x_all[:, bass.ds(2 * i + u, 1), :].squeeze(1)
                        dve.wait_ge(S["fo"], n1(i, u))
                        link(nc.vector.tensor_tensor(xt, xt, A[u][:, 0:DIM], ALU.add))
                    norm(2, scaled=True)
                    for u in (0, 1):
                        xt = x_all[:, bass.ds(2 * i + u, 1), :].squeeze(1)
                        dve.wait_ge(S["gnn"], n1(i, u))
                        link(nc.vector.tensor_scalar(s_[:, u], A[u][:, 384:512], dcol[:, u:u + 1], 0.0, ALU.mult, ALU.max))
                        link(nc.vector.tensor_tensor(xt, xt, s_[:, u], ALU.add))
                    norm(3)
                    for u in (0, 1):
                        dve.wait_ge(S["hg"], n1(i, u))
                        nc.vector.tensor_copy(hg_all[:, bass.ds(2 * i + u, 1), :].squeeze(1), A[u][:, 0:COLS24]
                                              ).then_inc(S["hg_sb"], 1)

                    assert cnt == NCH, cnt

            @block.scalar
            def _(act):
                with act.Fori(0, TILES // 2) as i:
                    def evacT(k, wait_store=False):
                        for u in (0, 1):
                            act.wait_ge(S["tr"], 6 * i + 2 * k + u + 1)
                            if k == 0:
                                act.wait_ge(xT_s[u], 16 * i + 16)
                            nc.scalar.copy(fT[:, u], A[u][:, 0:P]).then_inc(S["fT_ready"], 1)
                    evacT(0)
                    for u in (0, 1):
                        act.wait_ge(S["kq"], n1(i, u))
                        nc.scalar.copy(sel[64:96, u], A[u][64:96, 256:384]).then_inc(S["q_in_sel"], 1)
                    for u in (0, 1):
                        act.wait_ge(S["sub"], n1(i, u))
                        nc.scalar.activation(z2[:, u], z[:, u], ACT.Exp).then_inc(S["exp"], 1)
                    for u in (0, 1):
                        act.wait_ge(S["atT_ps"], n1(i, u))
                        nc.scalar.copy(atT[:, u], Z[u][:, :].rearrange("p (h j) -> p h j", h=HEADS)).then_inc(S["atT_sb"], 1)
                    for u in (0, 1):
                        act.wait_ge(S["U_ps"], n1(i, u))
                        nc.scalar.copy(UT[:, u, :, 0, :], U[u][0][:, :].rearrange("p (h j) -> p h j", h=HEADS)
                                       ).then_inc(S["UT0"], 1)
                    for u in (0, 1):
                        act.wait_ge(S["neg"], n1(i, u))
                        nc.scalar.activation(s_[:, u], s_[:, u], ACT.Exp, scale=-1.0).then_inc(S["sig"], 1)
                    evacT(1)
                    for u in (0, 1):
                        act.wait_ge(S["H1"], n1(i, u))
                        for c in (0, 1):
                            ins = nc.scalar.activation(h1[:, u, c], Z[u][:, c * P:(c + 1) * P], ACT.Relu, bias=bi[:, c:c + 1])
                        ins.then_inc(S["h1r"], 1)
                    for l, (src, dst, a, b) in enumerate(((2, h2, "L1", "h2r"), (3, h1, "L2", "h3r"))):
                        for u in (0, 1):
                            act.wait_ge(S[a], n1(i, u))
                            act.wait_ge(wr_s[u], 16 * (i + 1))
                            for c in (0, 1):
                                q = LAYERS * 2 * HID + l * 2 + c
                                ins = nc.scalar.activation(dst[:, u, c], ps_all[u][src][:, c * P:(c + 1) * P], ACT.Relu,
                                                           bias=wbuf[:, u, q:q + 1])
                            ins.then_inc(S[b], 1)
                    for u in (0, 1):
                        act.wait_ge(S["V"], n1(i, u))
                        nc.scalar.copy(VT[:, u], A[u][:, 128:256])
                        nc.scalar.copy(srow[:, u], A[u][0:1, 256:384]).then_inc(S["Vsb"], 1)
                    evacT(2)

            @block.tensor
            def _(pe):
                pe.sem_inc(S["L2free"], 2)
                pe.wait_ge(S["init"], 2)
                pe.wait_ge(S["consts2"], 13)
                with pe.Fori(0, TILES // 2) as i:
                    def tr(k, waited):
                        for u in (0, 1):
                            pe.wait_ge(*waited(u))
                            nc.tensor.transpose(A[u][:, 0:P], f[:, u], ident[:, :]).then_inc(S["tr"], 1)
                    tr(0, lambda u: (S["f_ready"], 6 * i + u + 1))
                    for u in (0, 1):
                        pe.wait_ge(S["fT_ready"], 6 * i + u + 1)
                        for b in (0, 1):
                            nc.tensor.matmul(A[u][32 * b:32 * b + 32, 256:256 + NB], kw[:, :],
                                             fT[:, u, b * NB:(b + 1) * NB], start=True, stop=True)
                        nc.tensor.matmul(A[u][64:96, 256:384], qw[:, :], fT[:, u], start=True,
                                         stop=True).then_inc(S["kq"], 1)
                    for u in (0, 1):
                        pe.wait_ge(S["kd_ready"], n1(i, u))
                        pe.wait_ge(S["q_in_sel"], n1(i, u))
                        nc.tensor.matmul(Z[u][:, :], sel[:, u], kd[:, u].rearrange("p h j -> p (h j)"), start=True,
                                         stop=True).then_inc(S["z_ready"], 1)
                    for u in (0, 1):
                        pe.wait_ge(S["attn"], n1(i, u))
                        pe.sem_inc(S["carrier"], 1)
                        for h in range(HEADS):
                            for b in (0, 1):
                                q = slice(b * NB, (b + 1) * NB)
                                mm = nc.tensor.matmul(Z[u][q, h * NB:(h + 1) * NB], z[q, u, h], ident[q, q], start=True,
                                                      stop=True)
                        mm.then_inc(S["atT_ps"], 1)
                    for u in (0, 1):
                        pe.wait_ge(S["atT_sb"], n1(i, u))
                        for b in (0, 1):
                            q = slice(b * NB, (b + 1) * NB)
                            mm = nc.tensor.matmul(U[u][b][:, :], f[q, u], atT[q, u].rearrange("p h j -> p (h j)"),
                                                  start=True, stop=True)
                        mm.then_inc(S["U_ps"], 1)
                    for u in (0, 1):
                        pe.wait_ge(S["UT0"], n1(i, u))
                        pe.wait_ge(S["UT1"], n1(i, u))
                        nc.tensor.matmul(A[u][:, 0:DIM], ones[:, :], cb[:, :], start=True, stop=False)
                        for h in range(HEADS):
                            mm = nc.tensor.matmul(A[u][:, 0:DIM], UT[:, u, h].rearrange("p b j -> p (b j)"), M[:, h],
                                                  start=False, stop=(h == HEADS - 1))
                        mm.then_inc(S["y"], 1)
                    tr(1, lambda u: (S["f_ready"], 6 * i + 2 + u + 1))
                    for u in (0, 1):
                        pe.wait_ge(S["fT_ready"], 6 * i + 2 + u + 1)
                        for c in (0, 1):
                            mm = nc.tensor.matmul(Z[u][:, c * P:(c + 1) * P], wiT[:, c * P:(c + 1) * P], fT[:, u],
                                                  start=True, stop=True)
                        mm.then_inc(S["H1"], 1)
                    for l, (dst, src, a, b) in enumerate(((2, h1, "h1r", "L1"), (3, h2, "h2r", "L2"))):
                        for u in (0, 1):
                            pe.wait_ge(S[a], n1(i, u))
                            pe.wait_ge(wr_s[u], 16 * (i + 1))
                            for m in (0, 1):
                                for k in (0, 1):
                                    q = (l * 2 + k) * HID + m * P
                                    mm = nc.tensor.matmul(ps_all[u][dst][:, m * P:(m + 1) * P], wbuf[:, u, q:q + P],
                                                          src[:, u, k], start=(k == 0), stop=(k == 1))
                            mm.then_inc(S[b], 1)
                    for u in (0, 1):
                        pe.wait_ge(S["h3r"], n1(i, u))
                        pe.sem_inc(S["L2free"], 1)
                        nc.tensor.matmul(A[u][:, 0:DIM], ones[:, :], bo[:, :], start=True, stop=False)
                        for c in (0, 1):
                            mm = nc.tensor.matmul(A[u][:, 0:DIM], h1[:, u, c], woT[:, c], start=False, stop=(c == 1))
                        mm.then_inc(S["fo"], 1)
                    for u in (0, 1):
                        pe.wait_ge(S["fd"], n1(i, u))
                        bd = BD[:, bass.ds(2 * i + u, 1), :].squeeze(1)
                        nc.tensor.matmul(A[u][:, 128:256], f[:, u], bd, start=True, stop=True)
                        nc.tensor.matmul(A[u][0:1, 256:384], dcol[:, u:u + 1], bd, start=True,
                                         stop=True).then_inc(S["V"], 1)
                    for u in (0, 1):
                        pe.wait_ge(S["Vsb"], n1(i, u))
                        nc.tensor.matmul(A[u][:, 384:512], VT[:, u], gW[:, :], start=True, stop=False)
                        nc.tensor.matmul(A[u][:, 384:512], srow[:, u], gb[:, :], start=False,
                                         stop=True).then_inc(S["gnn"], 1)
                    tr(2, lambda u: (S["f_ready"], 6 * i + 4 + u + 1))
                    for u in (0, 1):
                        pe.wait_ge(S["fT_ready"], 6 * i + 4 + u + 1)
                        nc.tensor.matmul(A[u][:, 0:COLS24], fT[:, u], w24[:, :], start=True, stop=True).then_inc(S["hg"], 1)

CAP = NODES * K
OUTSIDE = float(4 * CAP)
EMPTY = -1e30
GT = 8
GROUPS = TILES // GT
NBUF = 4
MG = 512
GAT_SLOPE = 0.2


def edge_and_expert_layers(nc, w, x_all, hg_all, xT_dram, table, hist_keys, lists, counts_dram, out):
    with ExitStack() as ctx:
        def sb(name, shape, dt=F32):
            return ctx.enter_context(nc.sbuf_tensor("m_" + name, shape, dt))

        def sem(name):
            return ctx.enter_context(nc.semaphore("m_" + name))

        slots = nc.dram_tensor("m_slots", [CAP, ROW], F32).ap()
        Y = nc.dram_tensor("m_Y", [TILES, P, GE * DIM], F32).ap()
        counts = sb("counts", [P, 4], I32)
        m0 = sb("m0", [P, TILES, GH])
        den = sb("den", [P, TILES, GH])
        num = sb("num", [P, TILES, GAT])
        t4 = sb("t4", [P, TILES, GH])
        t4b = sb("t4b", [P, TILES, GH])
        asrc = hg_all[:, :, GAT:GAT + GH]
        adst = hg_all[:, :, GAT + GH:GAT + 2 * GH]
        cload = sem("cload")
        with nc.Block() as block:
            @block.sync
            def _(sp):
                sp.dma_start(counts[:, :], counts_dram).then_inc(cload, 16)
                sp.wait_ge(cload, 16)

        with ExitStack() as c1:
            def sb1(name, shape, dt=F32):
                return c1.enter_context(nc.sbuf_tensor("m1_" + name, shape, dt))

            ps1 = [c1.enter_context(nc.psum_tensor(f"m1_p{k}", [P, 512], F32)) for k in range(4)]
            ps2 = [c1.enter_context(nc.psum_tensor(f"m1_q{k}", [P, 512], F32)) for k in range(2)]
            ps_hist = c1.enter_context(nc.psum_tensor("m1_hist", [P, 512], F32))
            slotf = sb1("slotf", [P, COLS])
            node_s = sb1("node_s", [P, COLS])
            rank = sb1("rank", [P, COLS])
            ok = sb1("ok", [P, COLS])
            ok2 = sb1("ok2", [P, COLS])
            slot_i = sb1("slot_i", [P, COLS], I32)
            lo = sb1("lo", [P, EPP], BF16)
            hi = sb1("hi", [P, EPP], BF16)
            bins_i = sb1("bins_i", [P, P, HB], I32)
            bins = sb1("bins", [P, P, HB], BF16)
            oh_lo = sb1("oh_lo", [P, 2, P, HB], BF16)
            oh_hi = sb1("oh_hi", [P, 2, HI, HB], BF16)
            zeros = sb1("zeros", [P, P], BF16)
            w1 = sb1("w1", [P, GE, HID])
            b1 = sb1("b1", [P, GE * 2])
            w2 = sb1("w2", [P, GE, 2, DIM])
            b2 = sb1("b2", [1, GE * DIM])
            ones = sb1("ones", [1, P])
            xg = sb1("xg", [P, 2, MG])
            hh = sb1("hh", [P, GE * 2, MG])
            yb = sb1("yb", [P, 4, GE * DIM])
            prime = sb1("prime", [1, 4 + NBUF, 4], I32)
            fill = sb1("fill", [P, K, ROW])
            nclamp = sb1("nclamp", [P, TILES])
            last = sb1("last", [P, ROW])
            has = sb1("has", [P, TILES])
            round_lo = sb1("round_lo", [P, 1])
            src8 = sb1("src8", [P, NBUF, 8], I32)
            slot8 = sb1("slot8", [P, NBUF, 8], I32)
            rows = sb1("rows", [P, NBUF, 8, ROW])
            ell = sb1("ell", [P, 2, GT * K * ROW])
            zk = sb1("zk", [P, GT * K * GH])
            zl = sb1("zl", [P, GT * K * GH])
            mx = sb1("mx", [P, GT, GH])
            m1 = sb1("m1", [P, GT, GH])
            sc = sb1("sc", [P, GT, GH])
            prod = sb1("prod", [P, GT * K * GAT])
            part = sb1("part", [P, GT, GAT])

            S = {n: c1.enter_context(nc.semaphore("m1_" + n)) for n in (
                "wl", "small", "consts", "xl0", "xl1", "xfree", "l1", "gelu", "l2", "ysb", "yst0", "yst1", "yst2", "yst3",
                "filled", "keys", "lists", "lists_free", "pool", "pidx", "gat0", "gat1", "gat2", "gat3", "sca0", "sca1", "sca2", "sca3", "scattered", "made", "free", "hist", "ell0", "ell1", "ellfree", "round_done",
                "dve", "dvc", "dvg", "carrier", "ex_in", "ex_out", "init", "epochs")}
            gat = [S[f"gat{u}"] for u in range(NBUF)]
            sca = [S[f"sca{u}"] for u in range(NBUF)]
            els = [S["ell0"], S["ell1"]]
            xls = [S["xl0"], S["xl1"]]
            yst = [S[f"yst{t}"] for t in range(4)]
            HALF = "(t p k) c -> p t (k c)"

            with nc.Block() as block:
                @block.sync
                def _(sp):
                    for dst, src in ((lo[:, :], hist_keys[0]), (hi[:, :], hist_keys[1])):
                        sp.dma_start(dst, src).then_inc(S["keys"], 16)
                    sp.dma_start(last[:, :], table[NODES - 1].partition_broadcast(P)).then_inc(S["small"], 16)
                    nr = sp.value_load(counts[0:1, 2:3], min_val=1, max_val=EDGES // K)
                    ne = sp.value_load(counts[0:1, 0:1], min_val=1, max_val=EPOCHS)
                    sp.wait_ge(S["consts"], 3)
                    sl = slots.rearrange(HALF, p=P, k=K)
                    with sp.Fori(0, nr) as ro:
                        for g in range(GROUPS):
                            sp.dma_start(sl[:, g * GT:(g + 1) * GT],
                                         fill[:, :, :].rearrange("p k c -> p (k c)").unsqueeze(1).to_broadcast([P, GT, K * ROW])
                                         ).then_inc(S["filled"], 16)
                        with sp.Fori(0, ne) as ep:
                            sp.wait_ge(S["lists_free"], ro * ne + ep + 1)
                            sp.sem_inc(S["carrier"], 1)
                            for dst, src in ((slotf, lists[0]), (node_s, lists[1]), (rank, lists[2])):
                                sp.dma_start(dst[:, :], src[:, bass.ds(ep * COLS, COLS)]).then_inc(S["lists"], 16)
                        sp.wait_ge(S["scattered"], ro + 1)
                        for g in range(GROUPS):
                            u = g % 2
                            sp.wait_ge(S["ellfree"], ro * GROUPS + g + 1)
                            sp.dma_start(ell[:, u].rearrange("p (t n) -> p t n", t=GT),
                                         sl[:, g * GT:(g + 1) * GT]).then_inc(els[u], 16)
                        sp.wait_ge(S["ellfree"], ro * GROUPS + GROUPS + 2)
                        sp.sem_inc(S["carrier"], 1)

                @block.gpsimd
                def _(pool):
                    nc.gpsimd.memset(ones[:, :], 1.0).then_inc(S["consts"], 1)
                    nc.gpsimd.memset(fill[:, :, 0:GAT], 0.0).then_inc(S["consts"], 1)
                    nc.gpsimd.memset(fill[:, :, GAT:ROW], EMPTY).then_inc(S["consts"], 1)
                    nc.gpsimd.memset(zeros[:, :], 0.0).then_inc(S["consts"], 1)
                    nc.gpsimd.iota(bins_i[:, :, :], pattern=[[1, P], [0, HB]], base=0,
                                   channel_multiplier=0).then_inc(S["consts"], 1)
                    nc.gpsimd.memset(round_lo[:, :], 0.0).then_inc(S["consts"], 1)
                    pool.sem_inc(S["lists_free"], 1)
                    nr = pool.value_load(counts[0:1, 2:3], min_val=1, max_val=EDGES // K)
                    ne = pool.value_load(counts[0:1, 0:1], min_val=1, max_val=EPOCHS)
                    IT = COLS // 8 // NBUF
                    NPE = 9
                    NPR = 1
                    first = sca[0].num

                    def gathers(u):
                        for k in range(8):
                            nc.gpsimd.indirect_dma_start(
                                out=rows[:, u, k], out_offset=None, in_=table,
                                in_offset=bass.IndirectOffsetOnAxis(ap=src8[:, u, k:k + 1].bitcast(U32), axis=0)
                            ).then_inc(gat[u], 16)

                    def scatters(u):
                        for k in range(8):
                            nc.gpsimd.indirect_dma_start(
                                out=slots, out_offset=bass.IndirectOffsetOnAxis(ap=slot8[:, u, k:k + 1].bitcast(U32), axis=0),
                                in_=rows[:, u, k], in_offset=None, bounds_check=CAP - 1, oob_is_err=False
                            ).then_inc(sca[u], 16)

                    pool.wait_ge(S["consts"], 6)
                    with pool.Fori(0, nr) as ro:
                        with pool.Fori(0, ne) as ep:
                            q = ro * ne + ep
                            k = 0

                            def link(ins):
                                nonlocal k
                                k += 1
                                ins.then_inc(S["pool"], 1)
                                pool.wait_ge(S["pool"], q * NPE + ro + k)
                                pool.sem_inc(S["carrier"], 1)
                            for u in range(NBUF):
                                pool.dma_start(prime[:, u], counts_dram[0:1, :]).then_inc(sca[u], 16)
                            pool.wait_ge(S["lists"], 48 * (q + 1))
                            pool.sem_inc(S["carrier"], 1)
                            g_ts, g_tt = nc.gpsimd.tensor_scalar, nc.gpsimd.tensor_tensor
                            link(g_ts(rank[:, :], rank[:, :], round_lo[:, 0:1], None, ALU.subtract))
                            link(g_ts(ok[:, :], rank[:, :], 0.0, None, ALU.is_ge))
                            link(g_ts(ok2[:, :], rank[:, :], float(K), None, ALU.is_lt))
                            link(g_tt(ok[:, :], ok[:, :], ok2[:, :], ALU.mult))
                            link(g_ts(slotf[:, :], slotf[:, :], round_lo[:, 0:1], None, ALU.subtract))
                            link(g_tt(slotf[:, :], slotf[:, :], ok[:, :], ALU.mult))
                            link(g_ts(ok[:, :], ok[:, :], -OUTSIDE, OUTSIDE, ALU.mult, ALU.add))
                            link(g_tt(slotf[:, :], slotf[:, :], ok[:, :], ALU.add))
                            link(nc.gpsimd.tensor_copy(slot_i[:, :], slotf[:, :]))
                            assert k == NPE
                            pool.wait_ge(S["filled"], (ro + 1) * 16 * GROUPS)
                            pool.sem_inc(S["carrier"], 1)
                            with pool.Fori(0, IT) as it:
                                for u in range(NBUF):
                                    pool.wait_ge(sca[u], 128 * it + 16)
                                    pool.sem_inc(S["carrier"], 1)
                                    c8 = bass.ds((it * NBUF + u) * 8, 8)
                                    nc.gpsimd.tensor_copy(src8[:, u], node_s[:, c8].bitcast(I32)).then_inc(S["pidx"], 1)
                                    nc.gpsimd.tensor_copy(slot8[:, u], slot_i[:, c8]).then_inc(S["pidx"], 1)
                                    pool.wait_ge(S["pidx"], (q * IT + it) * 2 * NBUF + 2 * u + 2)
                                    pool.sem_inc(S["carrier"], 1)
                                    gathers(u)
                                    if u:
                                        pool.wait_ge(gat[u - 1], 128 * it + 128)
                                        pool.sem_inc(S["carrier"], 1)
                                        scatters(u - 1)
                                pool.wait_ge(gat[NBUF - 1], 128 * it + 128)
                                pool.sem_inc(S["carrier"], 1)
                                scatters(NBUF - 1)
                            for u in range(NBUF):
                                pool.wait_ge(sca[u], 128 * IT + 16)
                            pool.sem_inc(S["carrier"], 1)
                            pool.dma_reset(range(gat[0].num, gat[0].num + 2 * NBUF))
                            pool.sem_clear(range(gat[0].num, gat[0].num + 2 * NBUF))
                            pool.sem_inc(S["lists_free"], 1)
                        nc.gpsimd.tensor_scalar(round_lo[:, :], round_lo[:, :], float(K), None, ALU.add).then_inc(S["pool"], 1)
                        pool.wait_ge(S["pool"], (ro * ne + ne) * NPE + ro + 1)
                        pool.sem_inc(S["scattered"], 1)

                @block.vector
                def _(dve):
                    cnt = [0]

                    def link(ins):
                        cnt[0] += 1
                        ins.then_inc(S["dve"], 1)
                        dve.wait_ge(S["dve"], cnt[0])

                    def bt(ap):
                        return ap.unsqueeze(2).to_broadcast([P, TILES, GH])

                    def lrelu(dst, src):
                        return nc.vector.scalar_tensor_tensor(out=dst, in0=src, scalar=GAT_SLOPE, in1=src,
                                                              op0=ALU.mult, op1=ALU.max)

                    dve.wait_ge(S["consts"], 6)
                    link(nc.vector.tensor_copy(bins[:, :, :], bins_i[:, :, :]))
                    dve.wait_ge(S["keys"], 32)
                    with dve.Fori(0, EPP // HB // 2) as i:
                        for u in (0, 1):
                            c = bass.ds((2 * i + u) * HB, HB)
                            dve.wait_ge(S["free"], 2 * i + u + 1)
                            nc.vector.tensor_tensor(oh_lo[:, u], lo[:, c].unsqueeze(1).to_broadcast([P, P, HB]),
                                                    bins[:, :, :], ALU.is_equal).then_inc(S["made"], 1)
                            nc.vector.tensor_tensor(oh_hi[:, u], hi[:, c].unsqueeze(1).to_broadcast([P, HI, HB]),
                                                    bins[:, 0:HI, :], ALU.is_equal).then_inc(S["made"], 1)
                    dve.wait_ge(S["hist"], 1)
                    link(nc.vector.tensor_copy(nclamp[:, :], ps_hist[:, 0:HI]))
                    dve.wait_ge(S["small"], 16)
                    zc = t4b
                    link(nc.vector.tensor_tensor(t4[:, :, :], asrc, adst, ALU.add))
                    link(lrelu(t4[:, :, :], t4[:, :, :]))
                    link(nc.vector.tensor_tensor(zc[:, :, :], adst,
                                                 last[:, GAT:ROW].unsqueeze(1).to_broadcast([P, TILES, GH]), ALU.add))
                    link(lrelu(zc[:, :, :], zc[:, :, :]))
                    link(nc.vector.tensor_scalar(has[:, :], nclamp[:, :], 0.0, None, ALU.is_gt))
                    link(nc.vector.tensor_tensor(m0[:, :, :], zc[:, :, :], bt(has[:, :]), ALU.mult))
                    link(nc.vector.tensor_scalar(has[:, :], has[:, :], 1.0, -EMPTY, ALU.subtract, ALU.mult))
                    link(nc.vector.tensor_tensor(m0[:, :, :], m0[:, :, :], bt(has[:, :]), ALU.add))
                    link(nc.vector.tensor_tensor(m0[:, :, :], m0[:, :, :], t4[:, :, :], ALU.max))
                    link(nc.vector.tensor_tensor(t4[:, :, :], t4[:, :, :], m0[:, :, :], ALU.subtract))
                    link(nc.vector.tensor_tensor(zc[:, :, :], zc[:, :, :], m0[:, :, :], ALU.subtract))
                    link(nc.vector.tensor_scalar(zc[:, :, :], zc[:, :, :], 0.0, None, ALU.min))
                    dve.sem_inc(S["init"], 1)
                    dve.wait_ge(S["init"], 3)
                    link(nc.vector.tensor_tensor(zc[:, :, :], zc[:, :, :], bt(nclamp[:, :]), ALU.mult))
                    link(nc.vector.tensor_tensor(den[:, :, :], zc[:, :, :], t4[:, :, :], ALU.add))
                    for h in range(GH):
                        q = slice(h * GE, (h + 1) * GE)
                        link(nc.vector.tensor_tensor(num[:, :, q], hg_all[:, :, q], t4[:, :, h:h + 1].to_broadcast([P, TILES, GE]), ALU.mult))
                        link(nc.vector.tensor_tensor(prod[:, 0:TILES * GE].rearrange("p (t e) -> p t e", t=TILES),
                                                     last[:, q].unsqueeze(1).to_broadcast([P, TILES, GE]),
                                                     zc[:, :, h:h + 1].to_broadcast([P, TILES, GE]), ALU.mult))
                        link(nc.vector.tensor_tensor(num[:, :, q], num[:, :, q],
                                                     prod[:, 0:TILES * GE].rearrange("p (t e) -> p t e", t=TILES), ALU.add))
                    nr = dve.value_load(counts[0:1, 2:3], min_val=1, max_val=EDGES // K)
                    dve.sem_inc(S["ellfree"], 2)
                    NG = 14 * GROUPS
                    with dve.Fori(0, nr) as ro:
                        gk = 0

                        def link(ins):
                            nonlocal gk
                            gk += 1
                            ins.then_inc(S["dvg"], 1)
                            dve.wait_ge(S["dvg"], ro * NG + gk)
                        for g in range(GROUPS):
                            u = g % 2
                            gt = slice(g * GT, (g + 1) * GT)
                            E3 = ell[:, u].rearrange("p (t k c) -> p t k c", t=GT, k=K)
                            Ef = ell[:, u].rearrange("p (n c) -> p n c", c=ROW)
                            zk4 = zk[:, :].rearrange("p (t k h) -> p t k h", t=GT, k=K)
                            zl4 = zl[:, :].rearrange("p (t k h) -> p t k h", t=GT, k=K)

                            def over_k(ap):
                                return ap.unsqueeze(2).to_broadcast([P, GT, K, GH])
                            dve.wait_ge(els[u], ro * (16 * GROUPS // 2) + 16 * (g // 2 + 1))
                            link(nc.vector.tensor_tensor(zk4, E3[:, :, :, GAT:ROW], over_k(adst[:, gt]), ALU.add))
                            link(lrelu(zl[:, :], zk[:, :]))
                            link(nc.vector.tensor_reduce(mx[:, :, :], zl4.rearrange("p t k h -> p t h k"), AX.X, ALU.max))
                            link(nc.vector.tensor_tensor(m1[:, :, :], mx[:, :, :], m0[:, gt], ALU.max))
                            link(nc.vector.tensor_tensor(sc[:, :, :], m0[:, gt], m1[:, :, :], ALU.subtract))
                            link(nc.vector.tensor_copy(m0[:, gt], m1[:, :, :]))
                            link(nc.vector.tensor_tensor(zk4, zl4, over_k(m1[:, :, :]), ALU.subtract))
                            dve.sem_inc(S["ex_in"], 1)
                            dve.wait_ge(S["ex_out"], ro * GROUPS + g + 1)
                            link(nc.vector.tensor_reduce(mx[:, :, :], zk4.rearrange("p t k h -> p t h k"), AX.X, ALU.add))
                            link(nc.vector.tensor_tensor(den[:, gt], den[:, gt], sc[:, :, :], ALU.mult))
                            link(nc.vector.tensor_tensor(den[:, gt], den[:, gt], mx[:, :, :], ALU.add))
                            link(nc.vector.tensor_tensor(prod[:, :].rearrange("p (n h e) -> p n h e", h=GH, e=GE),
                                                         Ef[:, :, 0:GAT].rearrange("p n (h e) -> p n h e", h=GH),
                                                         zk[:, :].rearrange("p (n h) -> p n h", h=GH).unsqueeze(3)
                                                         .to_broadcast([P, GT * K, GH, GE]), ALU.mult))
                            dve.sem_inc(S["ellfree"], 1)
                            link(nc.vector.tensor_reduce(part[:, :, :], prod[:, :].rearrange("p (t k f) -> p t f k", t=GT, k=K),
                                                         AX.X, ALU.add))
                            n4 = num[:, gt].rearrange("p t (h e) -> p t h e", h=GH)
                            link(nc.vector.tensor_tensor(n4, n4, sc[:, :, :].unsqueeze(3).to_broadcast([P, GT, GH, GE]), ALU.mult))
                            link(nc.vector.tensor_tensor(num[:, gt], num[:, gt], part[:, :, :], ALU.add))
                        assert gk == NG, gk

                @block.tensor
                def _(pe):
                    pe.sem_inc(S["free"], 2)
                    pe.wait_ge(S["consts"], 6)
                    nc.tensor.matmul(ps_hist[:, 0:HI], zeros[:, :], zeros[:, 0:HI], start=True, stop=False,
                                     skip_group_check=True)
                    pe.wait_ge(S["wl"], 64)
                    HPG = EPP // HB // (NODES // MG)

                    def hist_batch(g, n):
                        u = n % 2
                        pe.wait_ge(S["made"], 2 * (g * HPG + n + 1))
                        for c in range(HB):
                            mm = nc.tensor.matmul(ps_hist[:, 0:HI], oh_lo[:, u, :, c], oh_hi[:, u, :, c], start=False,
                                                  stop=False, skip_group_check=True)
                        mm.then_inc(S["free"], 1)

                    with pe.Fori(0, NODES // MG // 2) as i:
                        for u in (0, 1):
                            g = 2 * i + u
                            pe.wait_ge(xls[u], 16 * (i + 1))
                            for c in range(GE * 2):
                                pe.wait_ge(S["gelu"], g * 8 + c + 1)
                                mm = nc.tensor.matmul(ps1[c % 4][:, :], w1[:, c // 2, (c % 2) * P:(c % 2 + 1) * P], xg[:, u],
                                                      start=True, stop=True)
                                mm.then_inc(S["l1"], 1)
                                hist_batch(g, c)
                            pe.wait_ge(S["gelu"], g * 8 + 8 + 4)
                            for t in range(4):
                                pe.wait_ge(S["ysb"], g * 4 + t + 1)
                                for e in range(GE):
                                    nc.tensor.matmul(ps2[t % 2][:, e * DIM:(e + 1) * DIM], ones[:, :],
                                                     b2[:, e * DIM:(e + 1) * DIM], start=True, stop=False)
                                    for c in (0, 1):
                                        mm = nc.tensor.matmul(ps2[t % 2][:, e * DIM:(e + 1) * DIM], hh[:, 2 * e + c, t * P:(t + 1) * P],
                                                              w2[:, e, c], start=False, stop=(c == 1))
                                mm.then_inc(S["l2"], 1)
                                hist_batch(g, 8 + 2 * t)
                                hist_batch(g, 9 + 2 * t)
                    nc.tensor.matmul(ps_hist[:, 0:HI], zeros[:, :], zeros[:, 0:HI], start=False, stop=True,
                                     skip_group_check=True).then_inc(S["hist"], 1)

                @block.scalar
                def _(act):
                    for dst, src in ((w1[:, :, :], w["W1"].rearrange("e d h -> d e h")), (b1[:, :], w["b1T"]),
                                     (w2[:, :, :, :].rearrange("p e c o -> p (e c) o"),
                                      w["W2"].rearrange("e (c p) o -> p (e c) o", p=P)),
                                     (b2[:, :], w["b2"].rearrange("e o -> (e o)").unsqueeze(0))):
                        act.dma_start(dst, src).then_inc(S["wl"], 16)
                    for t in range(4):
                        act.dma_start(prime[:, NBUF + t], counts_dram[0:1, :]).then_inc(yst[t], 16)
                    act.sem_inc(S["gelu"], 4)
                    act.sem_inc(S["l2"], 4)
                    act.sem_inc(S["ysb"], 2)
                    for u in (0, 1):
                        act.dma_start(xg[:, u], xT_dram[:, u * MG:(u + 1) * MG]).then_inc(xls[u], 16)
                    act.wait_ge(S["wl"], 64)
                    def groups(i, more):
                        for u in (0, 1):
                            g = 2 * i + u
                            for c in range(GE * 2):
                                act.wait_ge(S["l1"], g * 8 + c + 1)
                                if c == 0:
                                    act.wait_ge(S["l2"], g * 4 + 4)
                                nc.scalar.activation(hh[:, c], ps1[c % 4][:, :], ACT.Gelu, bias=b1[:, c:c + 1]).then_inc(S["gelu"], 1)
                            if more:
                                act.dma_start(xg[:, u], xT_dram[:, bass.ds((g + 2) * MG, MG)]).then_inc(xls[u], 16)
                            for t in range(4):
                                act.wait_ge(S["l2"], g * 4 + t + 5)
                                act.wait_ge(yst[t], 16 * g + 16)
                                nc.scalar.copy(yb[:, t], ps2[t % 2][:, :]).then_inc(S["ysb"], 1)
                                act.wait_ge(S["ysb"], g * 4 + t + 3)
                                act.dma_start(Y[bass.ds(g * 4 + t, 1)].squeeze(0) if more else Y[g * 4 + t],
                                              yb[:, t]).then_inc(yst[t], 16)

                    pairs = NODES // MG // 2
                    with act.Fori(0, pairs - 1) as i:
                        groups(i, True)
                    groups(pairs - 1, False)
                    act.wait_ge(S["init"], 1)
                    nc.scalar.activation(t4[:, :, :], t4[:, :, :], ACT.Exp).then_inc(S["init"], 1)
                    nc.scalar.activation(t4b[:, :, :], t4b[:, :, :], ACT.Exp).then_inc(S["init"], 1)
                    for t in range(4):
                        act.wait_ge(yst[t], 16 * (NODES // MG) + 16)
                    nr = act.value_load(counts[0:1, 2:3], min_val=1, max_val=EDGES // K)
                    with act.Fori(0, nr) as ro:
                        for g in range(GROUPS):
                            act.wait_ge(S["ex_in"], ro * GROUPS + g + 1)
                            nc.scalar.activation(sc[:, :, :], sc[:, :, :], ACT.Exp)
                            nc.scalar.activation(zk[:, :], zk[:, :], ACT.Exp).then_inc(S["ex_out"], 1)

        with ExitStack() as c2:
            def sb2(name, shape, dt=F32):
                return c2.enter_context(nc.sbuf_tensor("m2_" + name, shape, dt))
            bg = sb2("bg", [P, GAT])
            gam = sb2("gam", [P, GAT])
            bet = sb2("bet", [P, GAT])
            a1 = sb2("a1", [P, TILES, GAT])
            a2 = sb2("a2", [P, TILES, GAT])
            r1 = sb2("r1", [P, TILES])
            r2 = sb2("r2", [P, TILES])
            hf = sb2("hf", [P, TILES])
            s4 = sb2("s4", [P, TILES, GE])
            rk = sb2("rk", [P, TILES, GE])
            cmp = sb2("cmp", [P, TILES])
            g4 = sb2("g4", [P, TILES, GE])
            NY = 4
            yl = sb2("yl", [P, NY, GE * DIM])
            S2 = {n: c2.enter_context(nc.semaphore("m2_" + n)) for n in
                  ("ld", "carrier", "dve", "pw", "pwd", "ex", "exd", "y0", "y1", "y2", "y3", "yfree", "comb", "od", "stored")}
            ys = [S2[f"y{t}"] for t in range(NY)]
            xo = out.rearrange("(t b) n d -> (b n) t d", b=2)
            OG = 8
            with nc.Block() as block:
                @block.sync
                def _(sp):
                    for dst, src in ((bg, w["b_gat"]), (gam, w["gamma"]), (bet, w["beta"])):
                        sp.dma_start(dst[:, :], src.partition_broadcast(P)).then_inc(S2["ld"], 16)
                    with sp.Fori(0, TILES // NY) as i:
                        for t in range(NY):
                            sp.wait_ge(S2["yfree"], i * NY + t + 1)
                            sp.sem_inc(S2["carrier"], 1)
                            sp.dma_start(yl[:, t], Y[bass.ds(i * NY + t, 1)].squeeze(0)).then_inc(ys[t], 16)
                    for t in range(NY):
                        sp.wait_ge(ys[t], 16 * (TILES // NY))

                @block.gpsimd
                def _(pool):
                    nc.gpsimd.memset(hf[:, :], -0.5).then_inc(S2["pw"], 1)
                    pool.wait_ge(S2["pw"], 2)
                    nc.gpsimd.tensor_tensor(r2[:, :], r1[:, :], hf[:, :], ALU.pow).then_inc(S2["pwd"], 1)

                @block.scalar
                def _(act):
                    act.wait_ge(S2["ex"], 1)
                    nc.scalar.activation(g4[:, :, :], g4[:, :, :], ACT.Exp).then_inc(S2["exd"], 1)
                    with act.Fori(0, TILES // OG) as i:
                        act.wait_ge(S2["comb"], OG * i + OG)
                        act.dma_start(xo[:, bass.ds(i * OG, OG)], x_all[:, bass.ds(i * OG, OG)]).then_inc(S2["stored"], 16)
                    act.wait_ge(S2["stored"], 16 * (TILES // OG))

                @block.vector
                def _(dve):
                    cnt = [0]

                    def link(ins):
                        cnt[0] += 1
                        ins.then_inc(S2["dve"], 1)
                        dve.wait_ge(S2["dve"], cnt[0])
                    tt, ts, red = nc.vector.tensor_tensor, nc.vector.tensor_scalar, nc.vector.tensor_reduce

                    def f16(ap):
                        return ap.unsqueeze(2).to_broadcast([P, TILES, GAT])

                    def row(ap):
                        return ap[:, :].unsqueeze(1).to_broadcast([P, TILES, GAT])
                    dve.wait_ge(S2["ld"], 48)
                    link(ts(den[:, :, :], den[:, :, :], 1e-16, None, ALU.add))
                    link(nc.vector.reciprocal(den[:, :, :], den[:, :, :]))
                    for h in range(GH):
                        q = slice(h * GE, (h + 1) * GE)
                        link(tt(a1[:, :, q], num[:, :, q], den[:, :, h:h + 1].to_broadcast([P, TILES, GE]), ALU.mult))
                    link(tt(a1[:, :, :], a1[:, :, :], row(bg), ALU.add))
                    link(red(r1[:, :], a1[:, :, :], AX.X, ALU.add))
                    link(ts(r1[:, :], r1[:, :], 1.0 / GAT, None, ALU.mult))
                    link(tt(a1[:, :, :], a1[:, :, :], f16(r1[:, :]), ALU.subtract))
                    link(tt(a2[:, :, :], a1[:, :, :], a1[:, :, :], ALU.mult))
                    link(red(r1[:, :], a2[:, :, :], AX.X, ALU.add))
                    link(ts(r1[:, :], r1[:, :], 1.0 / GAT, EPS, ALU.mult, ALU.add))
                    dve.sem_inc(S2["pw"], 1)
                    dve.wait_ge(S2["pwd"], 1)
                    link(tt(a1[:, :, :], a1[:, :, :], f16(r2[:, :]), ALU.mult))
                    link(tt(a1[:, :, :], a1[:, :, :], row(gam), ALU.mult))
                    link(tt(a1[:, :, :], a1[:, :, :], row(bet), ALU.add))
                    link(red(s4[:, :, :], a1[:, :, :].rearrange("p t (h e) -> p t e h", h=GH), AX.X, ALU.add))
                    link(ts(s4[:, :, :], s4[:, :, :], 1.0 / GH, None, ALU.mult))
                    link(nc.vector.memset(rk[:, :, :], 0.0))
                    for e in range(GE):
                        for o in range(GE):
                            if o != e:
                                link(tt(cmp[:, :], s4[:, :, o], s4[:, :, e], ALU.is_ge if o < e else ALU.is_gt))
                                link(tt(rk[:, :, e], rk[:, :, e], cmp[:, :], ALU.add))
                    link(red(r1[:, :], s4[:, :, :], AX.X, ALU.max))
                    link(tt(g4[:, :, :], s4[:, :, :], r1[:, :].unsqueeze(2).to_broadcast([P, TILES, GE]), ALU.subtract))
                    dve.sem_inc(S2["ex"], 1)
                    dve.wait_ge(S2["exd"], 1)
                    link(nc.vector.scalar_tensor_tensor(out=g4[:, :, :], in0=rk[:, :, :], scalar=2.0, in1=g4[:, :, :],
                                                        op0=ALU.is_lt, op1=ALU.mult))
                    link(red(r1[:, :], g4[:, :, :], AX.X, ALU.add))
                    link(nc.vector.reciprocal(r1[:, :], r1[:, :]))
                    link(tt(g4[:, :, :], g4[:, :, :], r1[:, :].unsqueeze(2).to_broadcast([P, TILES, GE]), ALU.mult))
                    base = cnt[0]
                    dve.sem_inc(S2["yfree"], NY)
                    with dve.Fori(0, TILES // NY) as i:
                        for t in range(NY):
                            dve.wait_ge(ys[t], 16 * (i + 1))
                            xt = x_all[:, bass.ds(i * NY + t, 1), :].squeeze(1)
                            for e in range(GE):
                                gs = g4[:, bass.ds(i * NY + t, 1), e:e + 1].squeeze(1)
                                ins = nc.vector.scalar_tensor_tensor(out=xt, in0=yl[:, t, e * DIM:(e + 1) * DIM], scalar=gs,
                                                                     in1=xt, op0=ALU.mult, op1=ALU.add)
                                ins.then_inc(S2["od"] if e < GE - 1 else S2["comb"], 1)
                                if e < GE - 1:
                                    dve.wait_ge(S2["od"], (i * NY + t) * (GE - 1) + e + 1)
                            dve.wait_ge(S2["comb"], i * NY + t + 1)
                            dve.sem_inc(S2["yfree"], 1)


_ARGS = ("x", "adj", "adjT", "fcT", "fp", "fcbT", "q_w", "k_w", "q_b", "k_b", "fp_b", "WiT", "biT", "WoT", "bo", "gWT",
         "gb", "Wgat", "att_src", "att_dst", "route", "WsT", "bsT", "WrT", "brT", "b_gat", "gamma", "beta", "W1", "b1T",
         "W2", "b2", "edges")


def program(nc, w, out):
    lists = nc.dram_tensor("edge_lists", [3, P, LIST], F32).ap()
    hist_keys = nc.dram_tensor("hist_keys", [2, P, EPP], BF16).ap()
    counts = nc.dram_tensor("loop_counts", [P, 4], I32).ap()
    xT = nc.dram_tensor("features_T", [P, NODES], F32).ap()
    table = nc.dram_tensor("gat_table", [NODES, ROW], F32).ap()
    sort_edges(nc, w["edges"], hist_keys, lists, counts)
    with ExitStack() as ctx:
        x_all = ctx.enter_context(nc.sbuf_tensor("x_all", [P, TILES, DIM], F32))
        hg_all = ctx.enter_context(nc.sbuf_tensor("hg_all", [P, TILES, COLS24], F32))
        node_layers(nc, w, x_all, hg_all, xT, table)
        edge_and_expert_layers(nc, w, x_all, hg_all, xT, table, hist_keys, lists, counts, out)


def kernel(**inputs):
    import numpy as np
    import concourse.bacc as bacc
    from concourse.bass_utils import run_bass_kernel_spmd

    g = {k: np.asarray(v) for k, v in inputs.items()}

    def lay(a):
        return np.ascontiguousarray(a)

    C = HID // P
    host = {
        "x": g["x"], "adj": g["adj"], "adjT": lay(g["adj"].transpose(0, 2, 1)),
        "fcT": lay(g["L0_gnn_fc_w"].T), "fp": g["L0_gnn_fp_w"],
        "fcbT": lay(g["L0_gnn_fc_b"].reshape(HEADS, DIM).T),
        "q_w": g["L0_gnn_q_w"], "k_w": g["L0_gnn_k_w"], "q_b": g["L0_gnn_q_b"], "k_b": g["L0_gnn_k_b"],
        "fp_b": g["L0_gnn_fp_b"],
        "WiT": lay(g["L0_ffn_Wi"].T), "biT": lay(g["L0_ffn_bi"].reshape(C, P).T),
        "WoT": lay(g["L0_ffn_Wo"].T), "bo": g["L0_ffn_bo"],
        "gWT": lay(g["L1_gnn_W"].T), "gb": g["L1_gnn_b"], "Wgat": g["L1_ffn_W_gat"],
        "att_src": lay(g["L1_ffn_att_src"].reshape(-1)), "att_dst": lay(g["L1_ffn_att_dst"].reshape(-1)),
        "route": g["L0_ffn_route_id"],
        "WsT": lay(g["L0_ffn_Ws"][:, 0].transpose(0, 2, 1).reshape(LAYERS, C, P, HID).transpose(2, 0, 1, 3)
                   .reshape(P, LAYERS * C * HID)),
        "bsT": lay(g["L0_ffn_bs"].reshape(LAYERS, C, P).transpose(2, 0, 1).reshape(P, LAYERS * C)),
        "WrT": lay(g["L0_ffn_Wr"].transpose(1, 0, 3, 2).reshape(EXP0, LAYERS, C, P, HID).transpose(0, 3, 1, 2, 4)
                   .reshape(EXP0, P, LAYERS * C * HID)),
        "brT": lay(g["L0_ffn_br"].reshape(LAYERS, EXP0, C, P).transpose(1, 3, 0, 2).reshape(EXP0, P, LAYERS * C)),
        "b_gat": g["L1_ffn_b_gat"], "gamma": g["L1_ffn_ln_gamma"], "beta": g["L1_ffn_ln_beta"],
        "W1": g["L1_ffn_W1"], "b1T": lay(g["L1_ffn_b1"].reshape(GE * C, P).T), "W2": g["L1_ffn_W2"],
        "b2": g["L1_ffn_b2"], "edges": g["L1_ffn_edge_index"],
    }
    nc = bacc.Bacc("TRN2", target_bir_lowering=False, num_devices=1)
    arrays, w = {}, {}
    for name in _ARGS:
        arrays["in_" + name] = host[name]
        w[name] = nc.dram_tensor("in_" + name, host[name].shape, mybir.dt.from_np(host[name].dtype),
                                 kind="ExternalInput").ap()
    out = nc.dram_tensor("out_x", (TILES * 2, NB, DIM), F32, kind="ExternalOutput").ap()
    program(nc, w, out)
    got = run_bass_kernel_spmd(nc, [arrays], core_ids=[0])
    return got.results[0]["out_x"]
```

```python
from contextlib import ExitStack
import concourse.bass as bass
from concourse import mybir
F32 = mybir.dt.float32
BF16 = mybir.dt.bfloat16
I32 = mybir.dt.int32
U32 = mybir.dt.uint32
ALU = mybir.AluOpType
ACT = mybir.ActivationFunctionType
AX = mybir.AxisListType
P = 128

NODES = 8192
HI = NODES // P
EDGES = 524288
EPP = EDGES // P
SEGS = 4
SEG = EPP // SEGS
ROUNDS = 11
SLOTS = 8 * ROUNDS
COLS = SEGS * SLOTS
EPOCHS = -(-SEG // SLOTS)
LIST = EPOCHS * COLS
BATCH = 8
BPE = COLS // BATCH
HALF = BATCH // 2
PAIRS = BATCH // 2
QB = 4
HB = 16
TAG = 0x20000000
K = 16
SB = 13


def sort_edges(nc, edge_index, hist_keys, lists, counts_out):
    with ExitStack() as ctx:
        def sb(name, shape, dt=F32):
            return ctx.enter_context(nc.sbuf_tensor("e_" + name, shape, dt))

        def ps(name, shape, dt=F32):
            return ctx.enter_context(nc.psum_tensor("e_" + name, shape, dt))

        def sem(name):
            return ctx.enter_context(nc.semaphore("e_" + name))

        src = sb("src", [P, SEG], I32)
        dst = sb("dst", [P, SEG], I32)
        key = sb("key", [P, EPP])
        keyi = key[:, :].bitcast(I32)
        mask = sb("mask", [P, SEG])
        lo = sb("lo", [P, EPP], BF16)
        hi = sb("hi", [P, EPP], BF16)
        tmp = sb("tmp", [P, SEG], I32)
        counts = sb("counts", [P, SEGS])
        countmax = sb("countmax", [P, SEGS])
        edge_steps = sb("edge_steps", [P, EPOCHS])
        top = sb("top", [P, 1])
        n_epochs_f = sb("n_epochs_f", [P, 1])
        n_epochs = sb("n_epochs", [P, 4], I32)
        top_rank = sb("top_rank", [P, 2])
        rounds_i = sb("rounds_i", [P, 2], I32)
        iota_i = sb("iota_i", [P, P], I32)
        iota = sb("iota", [P, P], BF16)
        ident = sb("ident", [P, P], BF16)
        ident_hi = sb("ident_hi", [P, P], BF16)
        later = sb("later", [P, P], BF16)
        zeros = sb("zeros", [P, P], BF16)
        bins = sb("bins", [P, P, BATCH], BF16)
        ones = sb("ones", [P, HI], BF16)
        oh_lo = sb("oh_lo", [P, QB, P, BATCH], BF16)
        oh_hi = sb("oh_hi", [P, QB, HI, BATCH], BF16)
        picked = sb("picked", [P, COLS])
        picked_i = picked[:, :].bitcast(I32)
        dec = sb("dec", [P, COLS], I32)
        dec2 = sb("dec2", [P, COLS], I32)
        node_d = sb("node_d", [P, LIST + 2 * BATCH])
        node_lo = sb("node_lo", [P, LIST + 2 * BATCH], BF16)
        node_hi = sb("node_hi", [P, LIST + 2 * BATCH], BF16)
        node_s = sb("node_s", [P, LIST], I32)
        rank = sb("rank", [P, LIST])
        slotf = sb("slotf", [P, LIST])
        lo8 = sb("lo8", [P, QB, BATCH], BF16)
        hi8 = sb("hi8", [P, QB, BATCH], BF16)
        same = sb("same", [P, 2, BATCH, P], BF16)
        loT = sb("loT", [P, 2, BATCH, P])
        loTb = sb("loTb", [P, 2, PAIRS, P], BF16)
        hist = sb("hist", [P, 2, HI])
        first = sb("first", [P, 2, PAIRS, HI], BF16)
        masked = sb("masked", [P, 2, BATCH, HI])

        ps_hist = ps("ps_hist", [P, 512])
        ps_row = ps("ps_row", [P, 2, BATCH, P])
        ps_base = ps("ps_base", [P, 2, BATCH, HI])
        ps_turn = ps("ps_turn", [P, 512])
        ps_loT = ps_turn[:, 0:256].bitcast(BF16).rearrange("p (k e) -> p k e", k=HALF)
        ps_first = ps_turn[:, 256:512].rearrange("p (j h) -> p j h", j=PAIRS)

        loaded = [sem(f"loaded{s}") for s in range(SEGS)]
        consts = sem("consts")
        decoded = sem("decoded")
        chain = sem("chain")
        counted = sem("counted")
        maxed = sem("maxed")
        stored = sem("stored")
        steps = [0]

        with nc.Block() as block:
            @block.sync
            def _(sp):
                for s in range(SEGS):
                    if s:
                        sp.wait_ge(decoded, s)
                    e = edge_index.rearrange("two (p e) -> two p e", p=P)
                    sp.dma_start(src[:, :], e[0, :, s * SEG:(s + 1) * SEG]).then_inc(loaded[s], 16)
                    sp.dma_start(dst[:, :], e[1, :, s * SEG:(s + 1) * SEG]).then_inc(loaded[s], 16)
                sp.wait_ge(decoded, SEGS)
                sp.dma_start(hist_keys[0], lo[:, :]).then_inc(stored, 16)
                sp.dma_start(hist_keys[1], hi[:, :]).then_inc(stored, 16)
                sp.wait_ge(stored, 32)

            @block.gpsimd
            def _(pool):
                nc.gpsimd.iota(iota_i[:, :], pattern=[[1, P]], base=0, channel_multiplier=0).then_inc(consts, 1)
                nc.gpsimd.iota(edge_steps[:, :], pattern=[[SLOTS, EPOCHS]], base=0, channel_multiplier=0,
                               allow_small_or_imprecise_dtypes=True).then_inc(consts, 1)
                nc.gpsimd.memset(ident[:, :], 0.0).then_inc(consts, 1)
                nc.gpsimd.memset(ident_hi[:, :], 0.0).then_inc(consts, 1)
                nc.gpsimd.memset(later[:, :], 1.0).then_inc(consts, 1)
                nc.gpsimd.memset(zeros[:, :], 0.0).then_inc(consts, 1)
                nc.gpsimd.memset(rank[:, :], 0.0).then_inc(consts, 1)
                nc.gpsimd.memset(ones[:, :], 1.0).then_inc(consts, 1)
                pool.wait_ge(consts, 8)
                nc.gpsimd.tensor_copy(iota[:, :], iota_i[:, :]).then_inc(consts, 1)
                for m, v in ((ident, 1.0), (ident_hi, float(P))):
                    nc.gpsimd.affine_select(out=m[:, :], in_=m[:, :], compare_op=ALU.not_equal, fill=v, base=0,
                                            pattern=[[-1, P]], channel_multiplier=1).then_inc(consts, 1)
                nc.gpsimd.affine_select(out=later[:, :], in_=later[:, :], compare_op=ALU.is_gt, fill=0.0,
                                        base=0, pattern=[[1, P]], channel_multiplier=-1).then_inc(consts, 1)
                pool.wait_ge(consts, 12)
                nc.gpsimd.tensor_copy(bins[:, :, :], iota[:, :].unsqueeze(2).to_broadcast([P, P, BATCH])
                                      ).then_inc(consts, 1)
                pool.wait_ge(counted, 1)
                nc.gpsimd.partition_all_reduce(countmax[:, :], counts[:, :], P, bass.bass_isa.ReduceOp.max).then_inc(maxed, 1)

            @block.vector
            def _(dve):
                def link(ins):
                    steps[0] += 1
                    ins.then_inc(chain, 1)
                    dve.wait_ge(chain, steps[0])

                for s in range(SEGS):
                    q = slice(s * SEG, (s + 1) * SEG)
                    dve.wait_ge(loaded[s], 32)
                    link(nc.vector.tensor_scalar(dst[:, :], dst[:, :], float(NODES), None, ALU.min))
                    link(nc.vector.tensor_scalar(src[:, :], src[:, :], float(NODES - 1), None, ALU.min))
                    link(nc.vector.tensor_scalar(mask[:, :], dst[:, :], float(NODES), None, ALU.is_lt))
                    link(nc.vector.scalar_tensor_tensor(out=mask[:, :], in0=src[:, :], scalar=float(NODES - 1),
                                                        in1=mask[:, :], op0=ALU.is_lt, op1=ALU.mult))
                    link(nc.vector.tensor_reduce(counts[:, s:s + 1], mask[:, :], AX.X, ALU.add))
                    link(nc.vector.tensor_scalar(tmp[:, :], dst[:, :], SB, TAG, ALU.logical_shift_left, ALU.bitwise_or))
                    link(nc.vector.tensor_tensor(keyi[:, q], tmp[:, :], src[:, :], ALU.bitwise_or))
                    link(nc.vector.tensor_tensor(key[:, q], key[:, q], mask[:, :], ALU.mult))
                    link(nc.vector.tensor_scalar(tmp[:, :], dst[:, :], P - 1, None, ALU.bitwise_and))
                    link(nc.vector.tensor_copy(lo[:, q], tmp[:, :]))
                    link(nc.vector.tensor_scalar(tmp[:, :], dst[:, :], 7, None, ALU.logical_shift_right))
                    link(nc.vector.tensor_scalar(mask[:, :], src[:, :], float(NODES - 1), 256.0, ALU.is_lt, ALU.mult))
                    link(nc.vector.tensor_tensor(hi[:, q], tmp[:, :], mask[:, :], ALU.add))
                    dve.sem_inc(decoded, 1)
                dve.sem_inc(counted, 1)
                dve.wait_ge(consts, 13)
                dve.wait_ge(maxed, 1)
                link(nc.vector.tensor_reduce(top[:, :], countmax[:, :], AX.X, ALU.max))
                link(nc.vector.tensor_scalar(edge_steps[:, :], edge_steps[:, :], top[:, 0:1], None, ALU.is_lt))
                link(nc.vector.tensor_reduce(n_epochs_f[:, :], edge_steps[:, :], AX.X, ALU.add))
                link(nc.vector.tensor_scalar(n_epochs_f[:, :], n_epochs_f[:, :], 1.0, None, ALU.max))
                link(nc.vector.tensor_copy(n_epochs[:, 0:1], n_epochs_f[:, :]))
                link(nc.vector.tensor_scalar(n_epochs[:, 1:2], n_epochs_f[:, :], float(BPE // QB), None, ALU.mult))
        carrier = sem("carrier")
        chain2 = sem("chain2")
        with nc.Block() as block:
            @block.vector
            def _(dve):
                ne = dve.value_load(n_epochs[0:1, 0:1], min_val=1, max_val=EPOCHS)
                N2 = 2 * ROUNDS + 9
                nc.vector.memset(node_d[:, :], float(NODES)).then_inc(chain2, 1)
                nc.vector.memset(node_s[:, :], 0).then_inc(chain2, 1)
                nc.vector.memset(node_lo[:, :], 0.0).then_inc(chain2, 1)
                nc.vector.memset(node_hi[:, :], float(HI)).then_inc(chain2, 1)
                dve.wait_ge(chain2, 4)
                with dve.Fori(0, ne) as ep:
                    k = 4
                    for r in range(ROUNDS):
                        for s in range(SEGS):
                            m8 = picked[:, s * SLOTS + 8 * r:s * SLOTS + 8 * r + 8]
                            ins = nc.vector.max(out=m8, in_=key[:, s * SEG:(s + 1) * SEG])
                        ins.then_inc(chain2, 1)
                        k += 1
                        dve.wait_ge(chain2, ep * N2 + k)
                        dve.sem_inc(carrier, 1)
                        for s in range(SEGS):
                            m8 = picked[:, s * SLOTS + 8 * r:s * SLOTS + 8 * r + 8]
                            sl = key[:, s * SEG:(s + 1) * SEG]
                            ins = nc.vector.match_replace(out=sl, in_to_replace=m8, in_values=sl, imm_value=0.0)
                        ins.then_inc(chain2, 1)
                        k += 1
                        dve.wait_ge(chain2, ep * N2 + k)
                        dve.sem_inc(carrier, 1)
                    q = bass.ds(ep * COLS, COLS)

                    def link(ins):
                        nonlocal k
                        k += 1
                        ins.then_inc(chain2, 1)
                        dve.wait_ge(chain2, ep * N2 + k)
                    link(nc.vector.tensor_scalar(node_s[:, q], picked_i, NODES - 1, None, ALU.bitwise_and))
                    link(nc.vector.tensor_scalar(dec[:, :], picked_i, SB, NODES - 1, ALU.logical_shift_right,
                                                 ALU.bitwise_and))
                    link(nc.vector.tensor_scalar(dec2[:, :], picked[:, :], 0.0, float(NODES), ALU.is_equal, ALU.mult))
                    link(nc.vector.tensor_tensor(node_d[:, q], dec[:, :], dec2[:, :], ALU.add))
                    dve.sem_inc(carrier, 1)
                    link(nc.vector.tensor_copy(dec[:, :], node_d[:, q]))
                    link(nc.vector.tensor_scalar(dec2[:, :], dec[:, :], P - 1, None, ALU.bitwise_and))
                    link(nc.vector.tensor_copy(node_lo[:, q], dec2[:, :]))
                    link(nc.vector.tensor_scalar(dec2[:, :], dec[:, :], 7, None, ALU.logical_shift_right))
                    nc.vector.tensor_copy(node_hi[:, q], dec2[:, :]).then_inc(chain2, 1)
                    dve.wait_ge(chain2, ep * N2 + N2 + 4)
                    assert k + 1 == N2 + 4, k

        d_ready = sem("d_ready")
        dchain = sem("dchain")
        oh_ready = sem("oh_ready")
        same_ready = sem("same_ready")
        AHEAD = 2 * PAIRS
        loT_ps = sem("loT_ps")
        loT_sb = sem("loT_sb")
        rows = sem("rows")
        rows_free = sem("rows_free")
        hist_sb = sem("hist_sb")
        hist_up = sem("hist_up")
        base_ready = sem("base_ready")
        base_free = sem("base_free")
        ranked = sem("ranked")
        rchain = sem("rchain")
        lstored = sem("lstored")
        rstored = sem("rstored")
        topped = sem("topped")
        last_steps = sem("last_steps")
        with nc.Block() as block:
            @block.sync
            def _(sp):
                sp.dma_start(lists[1], node_s[:, :].bitcast(F32)).then_inc(lstored, 16)
                sp.wait_ge(ranked, 1)
                sp.dma_start(lists[2], rank[:, :]).then_inc(rstored, 16)
                sp.dma_start(lists[0], slotf[:, :]).then_inc(rstored, 16)
                sp.wait_ge(ranked, 2)
                sp.dma_start(counts_out, n_epochs[:, :]).then_inc(rstored, 16)
                sp.wait_ge(lstored, 16)
                sp.wait_ge(rstored, 48)

            @block.gpsimd
            def _(pool):
                pool.wait_ge(topped, 1)
                nc.gpsimd.partition_all_reduce(top_rank[:, 1:2], top_rank[:, 0:1], P,
                                               bass.bass_isa.ReduceOp.max).then_inc(topped, 1)

            @block.tensor
            def _(pe):
                n = pe.value_load(n_epochs[0:1, 1:2], min_val=1, max_val=EPOCHS * BPE // QB)
                pe.sem_inc(hist_up, AHEAD)
                nc.tensor.matmul(ps_hist[:, 0:HI], zeros[:, :], zeros[:, 0:HI], start=True, stop=False,
                                 skip_group_check=True).then_inc(hist_up, 1)

                def transposed(b, h):
                    if h == 0:
                        for j in range(PAIRS):
                            nc.tensor.matmul(ps_first[:, j], oh_lo[:, b, :, 2 * j], oh_hi[:, b, :, 2 * j], start=True,
                                             stop=True)
                    for k in range(HALF):
                        mm = nc.tensor.transpose(ps_loT[:, k], oh_lo[:, b, :, h * HALF + k], ident[:, :])
                    mm.then_inc(loT_ps, 1)

                def row(b, q, k):
                    nc.tensor.matmul(ps_row[:, q, k], lo8[:, b, k:k + 1].to_broadcast([P, P]), ident[:, :],
                                     start=True, stop=False)
                    return nc.tensor.matmul(ps_row[:, q, k], hi8[:, b, k:k + 1].to_broadcast([P, P]), ident_hi[:, :],
                                            start=False, stop=True)

                pe.wait_ge(oh_ready, 1)
                for h in (0, 1):
                    if h:
                        pe.wait_ge(loT_sb, 1)
                    transposed(0, h)
                for k in range(BATCH):
                    mm = row(0, 0, k)
                mm.then_inc(rows, 1)
                with pe.Fori(0, n) as i:
                    for b in range(QB):
                        g = QB * i + b
                        u = b % 2
                        pe.wait_ge(oh_ready, g + 2)
                        pe.wait_ge(rows_free, g + 2)
                        pe.wait_ge(base_free, g + 1)
                        for k in range(BATCH):
                            if k % HALF == 0:
                                pe.wait_ge(loT_sb, 2 * g + 2 + k // HALF)
                                transposed((b + 1) % QB, k // HALF)
                            nm = row((b + 1) % QB, 1 - u, k)
                            if k == BATCH - 1:
                                nm.then_inc(rows, 1)
                            j = k // 2
                            if k % 2 == 0:
                                pe.wait_ge(hist_sb, g * PAIRS + j + 1)
                            nc.tensor.matmul(ps_base[:, u, k], loT[:, u, k], hist[:, j % 2], start=(k == 0), stop=False,
                                             skip_group_check=True)
                            mm = nc.tensor.matmul(ps_hist[:, 0:HI], oh_lo[:, b, :, k], oh_hi[:, b, :, k], start=False,
                                                  stop=False, skip_group_check=True)
                            if k % 2:
                                mm.then_inc(hist_up, 1)
                                nc.tensor.matmul(ps_base[:, u, k], loTb[:, u, j], first[:, u, j], start=False, stop=False,
                                                 skip_group_check=True)
                        pe.wait_ge(same_ready, g + 1)
                        for k in range(BATCH):
                            mm = nc.tensor.matmul(ps_base[:, u, k], same[:, u, k], ones[:, :], start=False, stop=True,
                                                  skip_group_check=True)
                        mm.then_inc(base_ready, 1)

            @block.scalar
            def _(act):
                n = act.value_load(n_epochs[0:1, 1:2], min_val=1, max_val=EPOCHS * BPE // QB)

                def transposed_copy(q, h):
                    half = slice(h * HALF, (h + 1) * HALF)
                    nc.scalar.copy(loT[:, q, half], ps_loT)

                def second_copy(q, h):
                    if h == 0:
                        nc.scalar.copy(first[:, q], ps_first)
                    nc.scalar.copy(loTb[:, q, h * HALF // 2:(h + 1) * HALF // 2],
                                   ps_loT.rearrange("p (j two) e -> p j two e", two=2)[:, :, 1]).then_inc(loT_sb, 1)

                for h in (0, 1):
                    act.wait_ge(loT_ps, h + 1)
                    transposed_copy(0, h)
                    second_copy(0, h)
                with act.Fori(0, n) as i:
                    for b in range(QB):
                        g = QB * i + b
                        for j in range(PAIRS):
                            act.wait_ge(hist_up, g * PAIRS + j + 1 + AHEAD)
                            nc.scalar.copy(hist[:, j % 2], ps_hist[:, 0:HI]).then_inc(hist_sb, 1)
                            h = j // 2
                            if j % 2 == 0:
                                act.wait_ge(loT_ps, 2 * (g + 1) + h + 1)
                                transposed_copy(1 - b % 2, h)
                            else:
                                second_copy(1 - b % 2, h)

            @block.vector
            def _(dve):
                n = dve.value_load(n_epochs[0:1, 1:2], min_val=1, max_val=EPOCHS * BPE // QB)
                dve.sem_inc(rows_free, 2)
                dve.sem_inc(base_free, 2)
                NR = 4 * QB

                def onehots(g, b):
                    c = bass.ds(g * BATCH, BATCH)
                    nc.vector.tensor_tensor(oh_lo[:, b], node_lo[:, c].unsqueeze(1).to_broadcast([P, P, BATCH]),
                                            bins[:, :, :], ALU.is_equal)
                    nc.vector.tensor_copy(lo8[:, b], node_lo[:, c])
                    nc.vector.tensor_copy(hi8[:, b], node_hi[:, c])
                    nc.vector.tensor_tensor(oh_hi[:, b], node_hi[:, c].unsqueeze(1).to_broadcast([P, HI, BATCH]),
                                            bins[:, 0:HI], ALU.is_equal).then_inc(oh_ready, 1)

                onehots(0, 0)
                onehots(1, 1)
                with dve.Fori(0, n) as i:
                    for b in range(QB):
                        g = QB * i + b
                        u = b % 2
                        k = b * 4

                        def link(ins):
                            nonlocal k
                            k += 1
                            ins.then_inc(rchain, 1)
                            dve.wait_ge(rchain, i * NR + k)
                        c = bass.ds(g * BATCH, BATCH)
                        dve.wait_ge(rows, g + 1)
                        link(nc.vector.tensor_tensor(same[:, u], ps_row[:, u],
                                                     node_d[:, c].unsqueeze(2).to_broadcast([P, BATCH, P]), ALU.is_equal))
                        dve.sem_inc(rows_free, 1)
                        link(nc.vector.tensor_tensor(same[:, u], same[:, u],
                                                     later[:, :].unsqueeze(1).to_broadcast([P, BATCH, P]), ALU.mult))
                        dve.sem_inc(same_ready, 1)
                        dve.wait_ge(hist_up, g * PAIRS + AHEAD - PAIRS + 1)
                        onehots(g + 2, (b + 2) % QB)
                        dve.wait_ge(base_ready, g + 1)
                        link(nc.vector.tensor_tensor(masked[:, u], ps_base[:, u],
                                                     oh_hi[:, b].rearrange("p h k -> p k h"), ALU.mult))
                        dve.sem_inc(base_free, 1)
                        link(nc.vector.tensor_reduce(rank[:, c], masked[:, u], AX.X, ALU.add))
                valid = node_d[:, 0:LIST]
                seq = [0]

                def link(ins):
                    seq[0] += 1
                    ins.then_inc(last_steps, 1)
                    dve.wait_ge(last_steps, seq[0])
                link(nc.vector.scalar_tensor_tensor(out=slotf[:, :], in0=node_d[:, 0:LIST], scalar=float(K), in1=rank[:, :],
                                                    op0=ALU.mult, op1=ALU.add))
                dve.sem_inc(ranked, 1)
                link(nc.vector.tensor_scalar(valid, node_d[:, 0:LIST], float(NODES), None, ALU.is_lt))
                link(nc.vector.tensor_tensor(valid, valid, rank[:, :], ALU.mult))
                link(nc.vector.tensor_reduce(top_rank[:, 0:1], valid, AX.X, ALU.max))
                dve.sem_inc(topped, 1)
                dve.wait_ge(topped, 2)
                link(nc.vector.tensor_copy(rounds_i[:, 0:1], top_rank[:, 1:2]))
                link(nc.vector.tensor_scalar(rounds_i[:, 1:2], rounds_i[:, 0:1], 4, None, ALU.logical_shift_right))
                link(nc.vector.tensor_scalar(n_epochs[:, 2:3], rounds_i[:, 1:2], 1.0, None, ALU.add))
                link(nc.vector.tensor_copy(n_epochs[:, 3:4], rounds_i[:, 0:1]))
                dve.sem_inc(ranked, 1)

TILES = NODES // P
UN = 4
DIM = 128
HEADS = 8
NB = 64
HID = 256
EXP0 = 16
LAYERS = 2
WROW = LAYERS * 2 * HID + LAYERS * 2
EPS = 1e-5
NEG = 1e9
SLOPE = 0.01
GH = 4
GE = 4
GAT = GH * GE
ROW = GAT + GH
COLS24 = GAT + 2 * GH


def node_layers(nc, w, x_all, hg_all, xT_dram, table):
    with ExitStack() as ctx:
        def sb(name, shape, dt=F32):
            return ctx.enter_context(nc.sbuf_tensor("n_" + name, shape, dt))

        def ps(name, shape, dt=F32):
            return ctx.enter_context(nc.psum_tensor("n_" + name, shape, dt))

        def sem(name):
            return ctx.enter_context(nc.semaphore("n_" + name))

        M = sb("M", [P, HEADS, DIM])
        kw = sb("kw", [P, 32])
        qw = sb("qw", [P, 32])
        cb = sb("cb", [1, DIM])
        head_c = sb("head_c", [1, HEADS])
        wiT = sb("wiT", [P, HID])
        bi = sb("bi", [P, 2])
        woT = sb("woT", [P, 2, DIM])
        bo = sb("bo", [1, DIM])
        gW = sb("gW", [P, DIM])
        gb = sb("gb", [1, DIM])
        w24 = sb("w24", [P, COLS24])
        ident = sb("ident", [P, P])
        ones = sb("ones", [1, P])
        half = sb("half", [P, UN])
        route = sb("route", [1, TILES], I32)
        adj = sb("adj", [P, TILES, NB])
        BD = sb("BD", [P, TILES, P])
        deg = sb("deg", [P, TILES])
        dinv = sb("dinv", [P, TILES])
        A = [ps(f"A{u}", [P, 512]) for u in range(UN)]
        Z = [ps(f"Z{u}", [P, 512]) for u in range(UN)]
        wdram = nc.dram_tensor("n_weff", [EXP0, P, WROW], F32).ap()

        with ExitStack() as tctx:
            def tsb(name, shape, dt=F32):
                return tctx.enter_context(nc.sbuf_tensor("s_" + name, shape, dt))

            def tsem(name):
                return tctx.enter_context(nc.semaphore("s_" + name))
            fcT = tsb("fcT", [P, HEADS, DIM])
            fp = tsb("fp", [P, HEADS, DIM])
            fcb = tsb("fcb", [P, HEADS])
            qk = tsb("qk", [P, 4])
            small = tsb("small", [1, 2 * DIM])
            wsI = tsb("wsI", [P, WROW])
            wr = tsb("wr", [P, 2, WROW])
            att = tsb("att", [P, 2, GAT])
            attw = tsb("attw", [P, 2, GAT])
            pos = tsb("pos", [P, TILES])
            pos_mask = tsb("pos_mask", [P, TILES])
            ld = tsem("ld")
            ldb = tsem("ldb")
            chain = tsem("chain")
            consts = tsem("consts")
            summed = tsem("summed")
            folded = tsem("folded")
            powed = tsem("powed")
            wl = [tsem("wl0"), tsem("wl1")]
            wadd = tsem("wadd")
            wst = [tsem("wst0"), tsem("wst1")]
            k = [0]
            NLD = 21

            with nc.Block() as block:
                @block.sync
                def _(sp):
                    for dst, src in (
                        (fcT[:, :, :], w["fcT"].rearrange("(h c) d -> c h d", c=DIM)),
                        (fp[:, :, :], w["fp"].rearrange("(h c) d -> c h d", c=DIM)),
                        (fcb[:, :], w["fcbT"]),
                        (qk[:, 0:1], w["q_w"]), (qk[:, 1:2], w["k_w"]),
                        (small[:, 0:DIM], w["fp_b"].unsqueeze(0)),
                        (small[:, DIM:DIM + 1], w["q_b"].unsqueeze(0)),
                        (small[:, DIM + 1:DIM + 2], w["k_b"].unsqueeze(0)),
                        (wiT[:, :], w["WiT"]), (bi[:, :], w["biT"]),
                        (woT[:, :, :], w["WoT"].rearrange("(c p) o -> p c o", p=P)),
                        (bo[:, :], w["bo"].unsqueeze(0)),
                        (gW[:, :], w["gWT"]), (gb[:, :], w["gb"].unsqueeze(0)),
                        (w24[:, 0:GAT], w["Wgat"]),
                        (att[:, 0], w["att_src"].partition_broadcast(P)),
                        (att[:, 1], w["att_dst"].partition_broadcast(P)),
                        (route[:, :], w["route"].unsqueeze(0)),
                        (wsI[:, 0:LAYERS * 2 * HID], w["WsT"]),
                        (wsI[:, LAYERS * 2 * HID:WROW], w["bsT"]),
                        (adj[:, :, :], w["adj"].rearrange("(t b) i j -> (b i) t j", b=2)),
                    ):
                        sp.dma_start(dst, src).then_inc(ld, 16)
                    sp.wait_ge(consts, 8)
                    for b in (0, 1):
                        sp.dma_start(BD[b * NB:(b + 1) * NB, :, b * NB:(b + 1) * NB],
                                     w["adjT"].rearrange("(t b) m i -> b m t i", b=2)[b]).then_inc(ldb, 16)
                    sp.dma_start(x_all[:, :, :], w["x"].rearrange("(t b) n d -> (b n) t d", b=2)).then_inc(ldb, 16)
                    for e in range(EXP0 + 1):
                        if e < EXP0:
                            u = e % 2
                            if e >= 2:
                                sp.wait_ge(wst[u], 16 * (e // 2))
                            sp.dma_start(wr[:, u, 0:LAYERS * 2 * HID], w["WrT"][e]).then_inc(wl[u], 16)
                            sp.dma_start(wr[:, u, LAYERS * 2 * HID:WROW], w["brT"][e]).then_inc(wl[u], 16)
                        if e >= 1:
                            v = (e - 1) % 2
                            sp.wait_ge(wadd, e)
                            sp.dma_start(wdram[e - 1], wr[:, v, :]).then_inc(wst[v], 16)
                    for v in (0, 1):
                        sp.wait_ge(wst[v], 16 * (EXP0 // 2))
                    sp.wait_ge(ldb, 48)

                @block.gpsimd
                def _(pool):
                    nc.gpsimd.memset(ident[:, :], 0.0).then_inc(consts, 1)
                    nc.gpsimd.memset(ones[:, :], 1.0).then_inc(consts, 1)
                    nc.gpsimd.memset(half[:, :], -0.5).then_inc(consts, 1)
                    nc.gpsimd.memset(pos[:, :], -0.5).then_inc(consts, 1)
                    nc.gpsimd.memset(kw[:, :], 0.0).then_inc(consts, 1)
                    nc.gpsimd.memset(qw[:, :], 0.0).then_inc(consts, 1)
                    nc.gpsimd.memset(BD[:, :, :], 0.0).then_inc(consts, 1)
                    pool.wait_ge(consts, 7)
                    nc.gpsimd.affine_select(out=ident[:, :], in_=ident[:, :], compare_op=ALU.not_equal, fill=1.0,
                                            base=0, pattern=[[-1, P]], channel_multiplier=1).then_inc(consts, 1)
                    pool.wait_ge(summed, 1)
                    nc.gpsimd.tensor_tensor(dinv[:, :], deg[:, :], pos[:, :], ALU.pow).then_inc(powed, 1)

                @block.vector
                def _(dve):
                    def link(ins):
                        k[0] += 1
                        ins.then_inc(chain, 1)
                        dve.wait_ge(chain, k[0])
                    dve.wait_ge(ld, 16 * NLD)
                    dve.wait_ge(consts, 8)
                    link(nc.vector.tensor_reduce(dinv[:, :], adj[:, :, :], AX.X, ALU.add))
                    link(nc.vector.tensor_scalar(deg[:, :], dinv[:, :], 1e-30, None, ALU.max))
                    link(nc.vector.tensor_scalar(pos_mask[:, :], dinv[:, :], 0.0, None, ALU.not_equal))
                    dve.sem_inc(summed, 1)
                    dve.wait_ge(powed, 1)
                    link(nc.vector.tensor_tensor(dinv[:, :], dinv[:, :], pos_mask[:, :], ALU.mult))
                    link(nc.vector.tensor_scalar(adj[:, :, :], adj[:, :, :], 1.0, NEG, ALU.subtract, ALU.mult))
                    link(nc.vector.tensor_tensor(qk[:, 2:3], qk[:, 0:1], qk[:, 1:2], ALU.add))
                    link(nc.vector.tensor_tensor(small[:, DIM + 2:DIM + 3], small[:, DIM:DIM + 1],
                                                 small[:, DIM + 1:DIM + 2], ALU.add))
                    for s in (0, 1):
                        link(nc.vector.tensor_tensor(attw[:, s], w24[:, 0:GAT], att[:, s], ALU.mult))
                        link(nc.vector.tensor_reduce(w24[:, GAT + s * GH:GAT + (s + 1) * GH],
                                                     attw[:, s].rearrange("p (h e) -> p h e", h=GH), AX.X, ALU.add))
                    for l in range(LAYERS):
                        for c in (0, 1):
                            q = (l * 2 + c) * HID + c * P
                            link(nc.vector.tensor_tensor(wsI[:, q:q + P], wsI[:, q:q + P], ident[:, :], ALU.add))
                    dve.sem_inc(folded, 1)
                    dve.wait_ge(folded, 2)
                    link(nc.vector.tensor_copy(M[:, 0:4], A[0][:, :].rearrange("p (h d) -> p h d", h=4)))
                    link(nc.vector.tensor_copy(M[:, 4:8], A[1][:, :].rearrange("p (h d) -> p h d", h=4)))
                    qkp = Z[0][:, 0:16].rearrange("p (h s) -> p h s", s=2)
                    link(nc.vector.tensor_copy(qw[:, 0:HEADS], qkp[:, :, 0]))
                    link(nc.vector.tensor_copy(kw[:, 0:HEADS], qkp[:, :, 1]))
                    link(nc.vector.tensor_tensor(cb[:, :], Z[1][0:1, 0:DIM], small[:, 0:DIM], ALU.add))
                    link(nc.vector.tensor_scalar(head_c[:, :], Z[1][0:1, DIM:DIM + HEADS], small[:, DIM + 2:DIM + 3],
                                                 None, ALU.add))
                    for e in range(EXP0):
                        u = e % 2
                        dve.wait_ge(wl[u], 32 * (e // 2 + 1))
                        nc.vector.tensor_tensor(wr[:, u, :], wr[:, u, :], wsI[:, :], ALU.add).then_inc(wadd, 1)

                @block.tensor
                def _(pe):
                    pe.wait_ge(folded, 1)
                    for h in range(HEADS):
                        nc.tensor.matmul(A[h // 4][:, (h % 4) * DIM:(h % 4 + 1) * DIM], fcT[:, h], fp[:, h],
                                         start=True, stop=True)
                        nc.tensor.matmul(Z[0][:, 2 * h:2 * h + 2], fcT[:, h], qk[:, 0:2], start=True, stop=True)
                    for h in range(HEADS):
                        nc.tensor.matmul(Z[1][0:1, 0:DIM], fcb[:, h:h + 1], fp[:, h], start=(h == 0),
                                         stop=(h == HEADS - 1))
                    nc.tensor.matmul(Z[1][0:1, DIM:DIM + HEADS], qk[:, 2:3], fcb[:, :], start=True,
                                     stop=True).then_inc(folded, 1)

        f = sb("f", [P, UN, DIM])
        fT = sb("fT", [P, UN, P])
        stats = sb("stats", [P, UN, 6])
        mv = sb("mv", [P, UN, 2])
        ve = sb("ve", [P, UN])
        rstd = sb("rstd", [P, UN])
        delta = sb("delta", [64, HEADS])
        kd = sb("kd", [P, UN, HEADS, NB])
        sel = sb("sel", [P, UN, P])
        z = sb("z", [P, UN, HEADS, NB])
        z2 = sb("z2", [P, UN, HEADS, NB])
        zmax = sb("zmax", [P, UN, HEADS])
        zsum = sb("zsum", [P, UN, HEADS])
        atT = sb("atT", [P, UN, HEADS, NB])
        UT = sb("UT", [P, UN, HEADS, 2, NB])
        s_ = sb("s_", [P, UN, DIM])
        h1 = sb("h1", [P, UN, 2, P])
        h2 = sb("h2", [P, UN, 2, P])
        wbuf = sb("wbuf", [P, UN, WROW])
        dcol = sb("dcol", [P, UN])
        srow = sb("srow", [1, UN, P])
        prime = sb("prime", [1, UN, TILES], I32)
        VT = sb("VT", [P, UN, P])
        NCH = 21 * UN

        S = {n: sem(n) for n in (
            "dve", "init", "consts2", "ve_ready", "rstd_ready", "f_ready", "tr", "fT_ready", "kq", "q_in_sel", "kd_ready",
            "z_ready", "sub", "exp", "attn", "atT_ps", "atT_sb", "U_ps", "UT0", "UT1", "y", "neg", "sig",
            "H1", "h1r", "L1", "h2r", "L2", "h3r", "fo", "L2free", "fd", "V", "Vsb",
            "gnn", "carrier", "hg", "hg_sb", "stored")}
        wr_s = [sem(f"w_ready{u}") for u in range(UN)]
        xT_s = [sem(f"xT{u}") for u in range(UN)]

        def n1(i, u):
            return UN * i + u + 1

        with nc.Block() as block:
            @block.sync
            def _(sp):
                for u in range(UN):
                    sp.dma_start(prime[:, u], w["route"].unsqueeze(0)).then_inc(xT_s[u], 16)
                with sp.Fori(0, TILES // UN) as i:
                    for u in range(UN):
                        sp.wait_ge(S["L2free"], n1(i, u))
                        e = sp.value_load(route[0:1, bass.ds(UN * i + u, 1)], min_val=0, max_val=EXP0 - 1)
                        sp.dma_start(wbuf[:, u, :], wdram[bass.ds(e, 1)].squeeze(0)).then_inc(wr_s[u], 16)
                    for u in range(UN):
                        sp.wait_ge(S["fT_ready"], 3 * UN * i + 2 * UN + u + 1)
                        sp.dma_start(xT_dram[:, bass.ds((UN * i + u) * P, P)], fT[:, u]).then_inc(xT_s[u], 16)
                for u in range(UN):
                    sp.wait_ge(xT_s[u], 16 * (TILES // UN) + 16)
                sp.wait_ge(S["hg_sb"], TILES)
                sp.dma_start(table.rearrange("(t p) c -> p t c", p=P), hg_all[:, :, 0:ROW]).then_inc(S["stored"], 16)
                sp.wait_ge(S["stored"], 16)

            @block.gpsimd
            def _(pool):
                nc.gpsimd.memset(kd[:, :, :, :], 0.0).then_inc(S["consts2"], 1)
                nc.gpsimd.memset(sel[:, :, :], 0.0).then_inc(S["consts2"], 1)
                nc.gpsimd.memset(delta[:, :], 0.0).then_inc(S["consts2"], 1)
                pool.wait_ge(S["consts2"], 3)
                for b in (0, 1):
                    nc.gpsimd.affine_select(out=delta[32 * b:32 * b + 32, :], in_=delta[32 * b:32 * b + 32, :],
                                            compare_op=ALU.not_equal, fill=1.0, base=0, pattern=[[-1, HEADS]],
                                            channel_multiplier=1).then_inc(S["consts2"], 1)
                for u in range(UN):
                    nc.gpsimd.affine_select(out=kd[64:96, u], in_=kd[64:96, u], compare_op=ALU.not_equal, fill=1.0,
                                            base=0, pattern=[[-1, HEADS], [0, NB]],
                                            channel_multiplier=1).then_inc(S["consts2"], 1)
                    for b in (0, 1):
                        nc.gpsimd.memset(sel[32 * b:32 * b + 32, u, b * NB:(b + 1) * NB], 1.0).then_inc(S["consts2"], 1)
                    nc.gpsimd.memset(sel[96:97, u, :], 1.0).then_inc(S["consts2"], 1)
                with pool.Fori(0, TILES // UN) as i:
                    for ln in range(4):
                        for u in range(UN):
                            pool.wait_ge(S["ve_ready"], 4 * UN * i + UN * ln + u + 1)
                            nc.gpsimd.tensor_tensor(rstd[:, u:u + 1], ve[:, u:u + 1], half[:, u:u + 1],
                                                    ALU.pow).then_inc(S["rstd_ready"], 1)

            @block.vector
            def _(dve):
                dve.wait_ge(S["consts2"], 5 + 4 * UN)
                for u in range(UN):
                    nc.vector.tensor_copy(kd[96:97, u], head_c[:, :].unsqueeze(2).to_broadcast([1, HEADS, NB])
                                          ).then_inc(S["init"], 1)
                dve.wait_ge(S["init"], UN)
                with dve.Fori(0, TILES // UN) as i:
                    cnt = 0

                    def link(ins):
                        nonlocal cnt
                        cnt += 1
                        ins.then_inc(S["dve"], 1)
                        dve.wait_ge(S["dve"], i * NCH + cnt)

                    def norm_stats(ln):
                        for u in range(UN):
                            xt = x_all[:, bass.ds(UN * i + u, 1), :].squeeze(1)
                            dve.sem_inc(S["carrier"], 1)
                            link(nc.vector.bn_stats(stats[:, u], xt))
                            dve.sem_inc(S["carrier"], 1)
                            link(nc.vector.bn_aggr(mv[:, u], stats[:, u]))
                            nc.vector.tensor_scalar(ve[:, u:u + 1], mv[:, u, 1:2], EPS, None,
                                                    ALU.add).then_inc(S["ve_ready"], 1)

                    def norm(ln, scaled=False):
                        norm_stats(ln)
                        for u in range(UN):
                            xt = x_all[:, bass.ds(UN * i + u, 1), :].squeeze(1)
                            dve.wait_ge(S["rstd_ready"], 4 * UN * i + UN * ln + u + 1)
                            r = rstd[:, u:u + 1]
                            if scaled:
                                dt = dinv[:, bass.ds(UN * i + u, 1)]
                                link(nc.vector.tensor_copy(dcol[:, u:u + 1], dt))
                                link(nc.vector.tensor_tensor(ve[:, u:u + 1], r, dcol[:, u:u + 1], ALU.mult))
                                r = ve[:, u:u + 1]
                            nc.vector.tensor_scalar(f[:, u], xt, mv[:, u, 0:1], r, ALU.subtract,
                                                    ALU.mult).then_inc(S["fd"] if scaled else S["f_ready"], 1)

                    def bc(ap, n=NB):
                        return ap.unsqueeze(2).to_broadcast([P, HEADS, n])
                    norm(0)
                    for u in range(UN):
                        dve.wait_ge(S["kq"], n1(i, u))
                        nc.vector.tensor_tensor(kd[0:64, u], A[u][0:64, 256:256 + NB].unsqueeze(1).to_broadcast([64, HEADS, NB]),
                                                delta[:, :].unsqueeze(2).to_broadcast([64, HEADS, NB]),
                                                ALU.mult).then_inc(S["kd_ready"], 1)
                    for u in range(UN):
                        dve.wait_ge(S["z_ready"], n1(i, u))
                        m = adj[:, bass.ds(UN * i + u, 1), :].to_broadcast([P, HEADS, NB])
                        link(nc.vector.tensor_tensor(z[:, u], Z[u][:, :].rearrange("p (h j) -> p h j", h=HEADS), m, ALU.add))
                        link(nc.vector.scalar_tensor_tensor(out=z2[:, u], in0=z[:, u], scalar=SLOPE, in1=z[:, u],
                                                            op0=ALU.mult, op1=ALU.max))
                        link(nc.vector.tensor_reduce(zmax[:, u], z2[:, u], AX.X, ALU.max))
                        nc.vector.tensor_tensor(z[:, u], z2[:, u], bc(zmax[:, u]), ALU.subtract).then_inc(S["sub"], 1)
                    for u in range(UN):
                        dve.wait_ge(S["exp"], n1(i, u))
                        link(nc.vector.tensor_reduce(zsum[:, u], z2[:, u], AX.X, ALU.add))
                        link(nc.vector.reciprocal(zsum[:, u], zsum[:, u]))
                        nc.vector.tensor_tensor(z[:, u], z2[:, u], bc(zsum[:, u]), ALU.mult).then_inc(S["attn"], 1)
                    for u in range(UN):
                        dve.wait_ge(S["U_ps"], n1(i, u))
                        nc.vector.tensor_copy(UT[:, u, :, 1, :], A[u][:, :].rearrange("p (h j) -> p h j", h=HEADS)
                                              ).then_inc(S["UT1"], 1)
                    for u in range(UN):
                        dve.wait_ge(S["y"], n1(i, u))
                        nc.vector.tensor_tensor(s_[:, u], A[u][:, 0:DIM], f[:, u], ALU.add).then_inc(S["neg"], 1)
                    for u in range(UN):
                        xt = x_all[:, bass.ds(UN * i + u, 1), :].squeeze(1)
                        dve.wait_ge(S["sig"], n1(i, u))
                        link(nc.vector.tensor_scalar(s_[:, u], s_[:, u], 1.0, None, ALU.add))
                        link(nc.vector.reciprocal(s_[:, u], s_[:, u]))
                        link(nc.vector.tensor_tensor(xt, xt, s_[:, u], ALU.add))
                    norm(1)
                    for u in range(UN):
                        xt = x_all[:, bass.ds(UN * i + u, 1), :].squeeze(1)
                        dve.wait_ge(S["fo"], n1(i, u))
                        link(nc.vector.tensor_tensor(xt, xt, A[u][:, 0:DIM], ALU.add))
                    norm(2, scaled=True)
                    for u in range(UN):
                        xt = x_all[:, bass.ds(UN * i + u, 1), :].squeeze(1)
                        dve.wait_ge(S["gnn"], n1(i, u))
                        link(nc.vector.tensor_scalar(s_[:, u], A[u][:, 384:512], dcol[:, u:u + 1], 0.0, ALU.mult, ALU.max))
                        link(nc.vector.tensor_tensor(xt, xt, s_[:, u], ALU.add))
                    norm(3)
                    for u in range(UN):
                        dve.wait_ge(S["hg"], n1(i, u))
                        nc.vector.tensor_copy(hg_all[:, bass.ds(UN * i + u, 1), :].squeeze(1), A[u][:, 0:COLS24]
                                              ).then_inc(S["hg_sb"], 1)

                    assert cnt == NCH, cnt

            @block.scalar
            def _(act):
                with act.Fori(0, TILES // UN) as i:
                    def evacT(k, wait_store=False):
                        for u in range(UN):
                            act.wait_ge(S["tr"], 3 * UN * i + UN * k + u + 1)
                            if k == 0:
                                act.wait_ge(xT_s[u], 16 * i + 16)
                            nc.scalar.copy(fT[:, u], A[u][:, 0:P]).then_inc(S["fT_ready"], 1)
                    evacT(0)
                    for u in range(UN):
                        act.wait_ge(S["kq"], n1(i, u))
                        nc.scalar.copy(sel[64:96, u], A[u][64:96, 256:384]).then_inc(S["q_in_sel"], 1)
                    for u in range(UN):
                        act.wait_ge(S["sub"], n1(i, u))
                        nc.scalar.activation(z2[:, u], z[:, u], ACT.Exp).then_inc(S["exp"], 1)
                    for u in range(UN):
                        act.wait_ge(S["atT_ps"], n1(i, u))
                        nc.scalar.copy(atT[:, u], Z[u][:, :].rearrange("p (h j) -> p h j", h=HEADS)).then_inc(S["atT_sb"], 1)
                    for u in range(UN):
                        act.wait_ge(S["U_ps"], n1(i, u))
                        nc.scalar.copy(UT[:, u, :, 0, :], Z[u][:, :].rearrange("p (h j) -> p h j", h=HEADS)
                                       ).then_inc(S["UT0"], 1)
                    for u in range(UN):
                        act.wait_ge(S["neg"], n1(i, u))
                        nc.scalar.activation(s_[:, u], s_[:, u], ACT.Exp, scale=-1.0).then_inc(S["sig"], 1)
                    evacT(1)
                    for u in range(UN):
                        act.wait_ge(S["H1"], n1(i, u))
                        for c in (0, 1):
                            ins = nc.scalar.activation(h1[:, u, c], Z[u][:, c * P:(c + 1) * P], ACT.Relu, bias=bi[:, c:c + 1])
                        ins.then_inc(S["h1r"], 1)
                    for l, (src, dst, a, b) in enumerate(((A, h2, "L1", "h2r"), (Z, h1, "L2", "h3r"))):
                        for u in range(UN):
                            act.wait_ge(S[a], n1(i, u))
                            act.wait_ge(wr_s[u], 16 * (i + 1))
                            for c in (0, 1):
                                q = LAYERS * 2 * HID + l * 2 + c
                                ins = nc.scalar.activation(dst[:, u, c], src[u][:, c * P:(c + 1) * P], ACT.Relu,
                                                           bias=wbuf[:, u, q:q + 1])
                            ins.then_inc(S[b], 1)
                    for u in range(UN):
                        act.wait_ge(S["V"], n1(i, u))
                        nc.scalar.copy(VT[:, u], A[u][:, 128:256])
                        nc.scalar.copy(srow[:, u], A[u][0:1, 256:384]).then_inc(S["Vsb"], 1)
                    evacT(2)

            @block.tensor
            def _(pe):
                pe.sem_inc(S["L2free"], UN)
                pe.wait_ge(S["init"], UN)
                pe.wait_ge(S["consts2"], 5 + 4 * UN)
                with pe.Fori(0, TILES // UN) as i:
                    def tr(k, waited):
                        for u in range(UN):
                            pe.wait_ge(*waited(u))
                            nc.tensor.transpose(A[u][:, 0:P], f[:, u], ident[:, :]).then_inc(S["tr"], 1)
                    tr(0, lambda u: (S["f_ready"], 3 * UN * i + u + 1))
                    for u in range(UN):
                        pe.wait_ge(S["fT_ready"], 3 * UN * i + u + 1)
                        for b in (0, 1):
                            nc.tensor.matmul(A[u][32 * b:32 * b + 32, 256:256 + NB], kw[:, :],
                                             fT[:, u, b * NB:(b + 1) * NB], start=True, stop=True)
                        nc.tensor.matmul(A[u][64:96, 256:384], qw[:, :], fT[:, u], start=True,
                                         stop=True).then_inc(S["kq"], 1)
                    for u in range(UN):
                        pe.wait_ge(S["kd_ready"], n1(i, u))
                        pe.wait_ge(S["q_in_sel"], n1(i, u))
                        nc.tensor.matmul(Z[u][:, :], sel[:, u], kd[:, u].rearrange("p h j -> p (h j)"), start=True,
                                         stop=True).then_inc(S["z_ready"], 1)
                    for u in range(UN):
                        pe.wait_ge(S["attn"], n1(i, u))
                        pe.sem_inc(S["carrier"], 1)
                        for h in range(HEADS):
                            for b in (0, 1):
                                q = slice(b * NB, (b + 1) * NB)
                                mm = nc.tensor.matmul(Z[u][q, h * NB:(h + 1) * NB], z[q, u, h], ident[q, q], start=True,
                                                      stop=True)
                        mm.then_inc(S["atT_ps"], 1)
                    for u in range(UN):
                        pe.wait_ge(S["atT_sb"], n1(i, u))
                        for b in (0, 1):
                            q = slice(b * NB, (b + 1) * NB)
                            mm = nc.tensor.matmul((Z, A)[b][u][:, :], f[q, u], atT[q, u].rearrange("p h j -> p (h j)"),
                                                  start=True, stop=True)
                        mm.then_inc(S["U_ps"], 1)
                    for u in range(UN):
                        pe.wait_ge(S["UT0"], n1(i, u))
                        pe.wait_ge(S["UT1"], n1(i, u))
                        nc.tensor.matmul(A[u][:, 0:DIM], ones[:, :], cb[:, :], start=True, stop=False)
                        for h in range(HEADS):
                            mm = nc.tensor.matmul(A[u][:, 0:DIM], UT[:, u, h].rearrange("p b j -> p (b j)"), M[:, h],
                                                  start=False, stop=(h == HEADS - 1))
                        mm.then_inc(S["y"], 1)
                    tr(1, lambda u: (S["f_ready"], 3 * UN * i + UN + u + 1))
                    for u in range(UN):
                        pe.wait_ge(S["fT_ready"], 3 * UN * i + UN + u + 1)
                        for c in (0, 1):
                            mm = nc.tensor.matmul(Z[u][:, c * P:(c + 1) * P], wiT[:, c * P:(c + 1) * P], fT[:, u],
                                                  start=True, stop=True)
                        mm.then_inc(S["H1"], 1)
                    for l, (dst, src, a, b) in enumerate(((A, h1, "h1r", "L1"), (Z, h2, "h2r", "L2"))):
                        for u in range(UN):
                            pe.wait_ge(S[a], n1(i, u))
                            pe.wait_ge(wr_s[u], 16 * (i + 1))
                            for m in (0, 1):
                                for k in (0, 1):
                                    q = (l * 2 + k) * HID + m * P
                                    mm = nc.tensor.matmul(dst[u][:, m * P:(m + 1) * P], wbuf[:, u, q:q + P],
                                                          src[:, u, k], start=(k == 0), stop=(k == 1))
                            mm.then_inc(S[b], 1)
                    for u in range(UN):
                        pe.wait_ge(S["h3r"], n1(i, u))
                        pe.sem_inc(S["L2free"], 1)
                        nc.tensor.matmul(A[u][:, 0:DIM], ones[:, :], bo[:, :], start=True, stop=False)
                        for c in (0, 1):
                            mm = nc.tensor.matmul(A[u][:, 0:DIM], h1[:, u, c], woT[:, c], start=False, stop=(c == 1))
                        mm.then_inc(S["fo"], 1)
                    for u in range(UN):
                        pe.wait_ge(S["fd"], n1(i, u))
                        bd = BD[:, bass.ds(UN * i + u, 1), :].squeeze(1)
                        nc.tensor.matmul(A[u][:, 128:256], f[:, u], bd, start=True, stop=True)
                        nc.tensor.matmul(A[u][0:1, 256:384], dcol[:, u:u + 1], bd, start=True,
                                         stop=True).then_inc(S["V"], 1)
                    for u in range(UN):
                        pe.wait_ge(S["Vsb"], n1(i, u))
                        nc.tensor.matmul(A[u][:, 384:512], VT[:, u], gW[:, :], start=True, stop=False)
                        nc.tensor.matmul(A[u][:, 384:512], srow[:, u], gb[:, :], start=False,
                                         stop=True).then_inc(S["gnn"], 1)
                    tr(2, lambda u: (S["f_ready"], 3 * UN * i + 2 * UN + u + 1))
                    for u in range(UN):
                        pe.wait_ge(S["fT_ready"], 3 * UN * i + 2 * UN + u + 1)
                        nc.tensor.matmul(A[u][:, 0:COLS24], fT[:, u], w24[:, :], start=True, stop=True).then_inc(S["hg"], 1)

CAP = NODES * K
OUTSIDE = float(4 * CAP)
EMPTY = -1e30
GT = 8
GROUPS = TILES // GT
NBUF = 4
MG = 512
GAT_SLOPE = 0.2


def edge_and_expert_layers(nc, w, x_all, hg_all, xT_dram, table, hist_keys, lists, counts_dram, out):
    with ExitStack() as ctx:
        def sb(name, shape, dt=F32):
            return ctx.enter_context(nc.sbuf_tensor("m_" + name, shape, dt))

        def sem(name):
            return ctx.enter_context(nc.semaphore("m_" + name))

        slots = nc.dram_tensor("m_slots", [CAP, ROW], F32).ap()
        Y = nc.dram_tensor("m_Y", [TILES, P, GE * DIM], F32).ap()
        counts = sb("counts", [P, 4], I32)
        m0 = sb("m0", [P, TILES, GH])
        den = sb("den", [P, TILES, GH])
        num = sb("num", [P, TILES, GAT])
        t4 = sb("t4", [P, TILES, GH])
        t4b = sb("t4b", [P, TILES, GH])
        asrc = hg_all[:, :, GAT:GAT + GH]
        adst = hg_all[:, :, GAT + GH:GAT + 2 * GH]
        cload = sem("cload")
        with nc.Block() as block:
            @block.sync
            def _(sp):
                sp.dma_start(counts[:, :], counts_dram).then_inc(cload, 16)
                sp.wait_ge(cload, 16)

        with ExitStack() as c1:
            def sb1(name, shape, dt=F32):
                return c1.enter_context(nc.sbuf_tensor("m1_" + name, shape, dt))

            ps1 = [c1.enter_context(nc.psum_tensor(f"m1_p{k}", [P, 512], F32)) for k in range(4)]
            ps2 = [c1.enter_context(nc.psum_tensor(f"m1_q{k}", [P, 512], F32)) for k in range(2)]
            ps_hist = c1.enter_context(nc.psum_tensor("m1_hist", [P, 512], F32))
            slotf = sb1("slotf", [P, COLS])
            node_s = sb1("node_s", [P, COLS])
            rank = sb1("rank", [P, COLS])
            ok = sb1("ok", [P, COLS])
            ok2 = sb1("ok2", [P, COLS])
            slot_i = sb1("slot_i", [P, COLS], I32)
            lo = sb1("lo", [P, EPP], BF16)
            hi = sb1("hi", [P, EPP], BF16)
            bins_i = sb1("bins_i", [P, P, HB], I32)
            bins = sb1("bins", [P, P, HB], BF16)
            oh_lo = sb1("oh_lo", [P, 2, P, HB], BF16)
            oh_hi = sb1("oh_hi", [P, 2, HI, HB], BF16)
            zeros = sb1("zeros", [P, P], BF16)
            w1 = sb1("w1", [P, GE, HID])
            b1 = sb1("b1", [P, GE * 2])
            w2 = sb1("w2", [P, GE, 2, DIM])
            b2 = sb1("b2", [1, GE * DIM])
            ones = sb1("ones", [1, P])
            xg = sb1("xg", [P, 2, MG])
            hh = sb1("hh", [P, GE * 2, MG])
            yb = sb1("yb", [P, 4, GE * DIM])
            prime = sb1("prime", [1, 4 + NBUF, 4], I32)
            fill = sb1("fill", [P, K, ROW])
            nclamp = sb1("nclamp", [P, TILES])
            last = sb1("last", [P, ROW])
            has = sb1("has", [P, TILES])
            round_lo = sb1("round_lo", [P, 1])
            src8 = sb1("src8", [P, NBUF, 8], I32)
            slot8 = sb1("slot8", [P, NBUF, 8], I32)
            rows = sb1("rows", [P, NBUF, 8, ROW])
            ell = sb1("ell", [P, 2, GT * K * ROW])
            zk = sb1("zk", [P, GT * K * GH])
            zl = sb1("zl", [P, GT * K * GH])
            mx = sb1("mx", [P, GT, GH])
            m1 = sb1("m1", [P, GT, GH])
            sc = sb1("sc", [P, GT, GH])
            prod = sb1("prod", [P, GT * K * GAT])
            part = sb1("part", [P, GT, GAT])

            S = {n: c1.enter_context(nc.semaphore("m1_" + n)) for n in (
                "wl", "small", "consts", "xl0", "xl1", "xfree", "l1", "gelu", "l2", "ysb", "yst0", "yst1", "yst2", "yst3",
                "filled", "keys", "lists", "lists_free", "pool", "pidx", "gat0", "gat1", "gat2", "gat3", "sca0", "sca1", "sca2", "sca3", "scattered", "made", "free", "hist", "ell0", "ell1", "ellfree", "round_done",
                "dve", "dvc", "dvg", "carrier", "ex_in", "ex_out", "init", "epochs")}
            gat = [S[f"gat{u}"] for u in range(NBUF)]
            sca = [S[f"sca{u}"] for u in range(NBUF)]
            els = [S["ell0"], S["ell1"]]
            xls = [S["xl0"], S["xl1"]]
            yst = [S[f"yst{t}"] for t in range(4)]
            HALF = "(t p k) c -> p t (k c)"

            with nc.Block() as block:
                @block.sync
                def _(sp):
                    for dst, src in ((lo[:, :], hist_keys[0]), (hi[:, :], hist_keys[1])):
                        sp.dma_start(dst, src).then_inc(S["keys"], 16)
                    sp.dma_start(last[:, :], table[NODES - 1].partition_broadcast(P)).then_inc(S["small"], 16)
                    nr = sp.value_load(counts[0:1, 2:3], min_val=1, max_val=EDGES // K)
                    ne = sp.value_load(counts[0:1, 0:1], min_val=1, max_val=EPOCHS)
                    sp.wait_ge(S["consts"], 3)
                    sl = slots.rearrange(HALF, p=P, k=K)
                    with sp.Fori(0, nr) as ro:
                        for g in range(GROUPS):
                            sp.dma_start(sl[:, g * GT:(g + 1) * GT],
                                         fill[:, :, :].rearrange("p k c -> p (k c)").unsqueeze(1).to_broadcast([P, GT, K * ROW])
                                         ).then_inc(S["filled"], 16)
                        with sp.Fori(0, ne) as ep:
                            sp.wait_ge(S["lists_free"], ro * ne + ep + 1)
                            sp.sem_inc(S["carrier"], 1)
                            for dst, src in ((slotf, lists[0]), (node_s, lists[1]), (rank, lists[2])):
                                sp.dma_start(dst[:, :], src[:, bass.ds(ep * COLS, COLS)]).then_inc(S["lists"], 16)
                        sp.wait_ge(S["scattered"], ro + 1)
                        for g in range(GROUPS):
                            u = g % 2
                            sp.wait_ge(S["ellfree"], ro * GROUPS + g + 1)
                            sp.dma_start(ell[:, u].rearrange("p (t n) -> p t n", t=GT),
                                         sl[:, g * GT:(g + 1) * GT]).then_inc(els[u], 16)
                        sp.wait_ge(S["ellfree"], ro * GROUPS + GROUPS + 2)
                        sp.sem_inc(S["carrier"], 1)

                @block.gpsimd
                def _(pool):
                    nc.gpsimd.memset(ones[:, :], 1.0).then_inc(S["consts"], 1)
                    nc.gpsimd.memset(fill[:, :, 0:GAT], 0.0).then_inc(S["consts"], 1)
                    nc.gpsimd.memset(fill[:, :, GAT:ROW], EMPTY).then_inc(S["consts"], 1)
                    nc.gpsimd.memset(zeros[:, :], 0.0).then_inc(S["consts"], 1)
                    nc.gpsimd.iota(bins_i[:, :, :], pattern=[[1, P], [0, HB]], base=0,
                                   channel_multiplier=0).then_inc(S["consts"], 1)
                    nc.gpsimd.memset(round_lo[:, :], 0.0).then_inc(S["consts"], 1)
                    pool.sem_inc(S["lists_free"], 1)
                    nr = pool.value_load(counts[0:1, 2:3], min_val=1, max_val=EDGES // K)
                    ne = pool.value_load(counts[0:1, 0:1], min_val=1, max_val=EPOCHS)
                    IT = COLS // 8 // NBUF
                    NPE = 9
                    NPR = 1
                    first = sca[0].num

                    def gathers(u):
                        for k in range(8):
                            nc.gpsimd.indirect_dma_start(
                                out=rows[:, u, k], out_offset=None, in_=table,
                                in_offset=bass.IndirectOffsetOnAxis(ap=src8[:, u, k:k + 1].bitcast(U32), axis=0)
                            ).then_inc(gat[u], 16)

                    def scatters(u):
                        for k in range(8):
                            nc.gpsimd.indirect_dma_start(
                                out=slots, out_offset=bass.IndirectOffsetOnAxis(ap=slot8[:, u, k:k + 1].bitcast(U32), axis=0),
                                in_=rows[:, u, k], in_offset=None, bounds_check=CAP - 1, oob_is_err=False
                            ).then_inc(sca[u], 16)

                    pool.wait_ge(S["consts"], 6)
                    with pool.Fori(0, nr) as ro:
                        with pool.Fori(0, ne) as ep:
                            q = ro * ne + ep
                            k = 0

                            def link(ins):
                                nonlocal k
                                k += 1
                                ins.then_inc(S["pool"], 1)
                                pool.wait_ge(S["pool"], q * NPE + ro + k)
                                pool.sem_inc(S["carrier"], 1)
                            for u in range(NBUF):
                                pool.dma_start(prime[:, u], counts_dram[0:1, :]).then_inc(sca[u], 16)
                            pool.wait_ge(S["lists"], 48 * (q + 1))
                            pool.sem_inc(S["carrier"], 1)
                            g_ts, g_tt = nc.gpsimd.tensor_scalar, nc.gpsimd.tensor_tensor
                            link(g_ts(rank[:, :], rank[:, :], round_lo[:, 0:1], None, ALU.subtract))
                            link(g_ts(ok[:, :], rank[:, :], 0.0, None, ALU.is_ge))
                            link(g_ts(ok2[:, :], rank[:, :], float(K), None, ALU.is_lt))
                            link(g_tt(ok[:, :], ok[:, :], ok2[:, :], ALU.mult))
                            link(g_ts(slotf[:, :], slotf[:, :], round_lo[:, 0:1], None, ALU.subtract))
                            link(g_tt(slotf[:, :], slotf[:, :], ok[:, :], ALU.mult))
                            link(g_ts(ok[:, :], ok[:, :], -OUTSIDE, OUTSIDE, ALU.mult, ALU.add))
                            link(g_tt(slotf[:, :], slotf[:, :], ok[:, :], ALU.add))
                            link(nc.gpsimd.tensor_copy(slot_i[:, :], slotf[:, :]))
                            assert k == NPE
                            pool.wait_ge(S["filled"], (ro + 1) * 16 * GROUPS)
                            pool.sem_inc(S["carrier"], 1)
                            with pool.Fori(0, IT) as it:
                                for u in range(NBUF):
                                    pool.wait_ge(sca[u], 128 * it + 16)
                                    pool.sem_inc(S["carrier"], 1)
                                    c8 = bass.ds((it * NBUF + u) * 8, 8)
                                    nc.gpsimd.tensor_copy(src8[:, u], node_s[:, c8].bitcast(I32)).then_inc(S["pidx"], 1)
                                    nc.gpsimd.tensor_copy(slot8[:, u], slot_i[:, c8]).then_inc(S["pidx"], 1)
                                    pool.wait_ge(S["pidx"], (q * IT + it) * 2 * NBUF + 2 * u + 2)
                                    pool.sem_inc(S["carrier"], 1)
                                    gathers(u)
                                    if u:
                                        pool.wait_ge(gat[u - 1], 128 * it + 128)
                                        pool.sem_inc(S["carrier"], 1)
                                        scatters(u - 1)
                                pool.wait_ge(gat[NBUF - 1], 128 * it + 128)
                                pool.sem_inc(S["carrier"], 1)
                                scatters(NBUF - 1)
                            for u in range(NBUF):
                                pool.wait_ge(sca[u], 128 * IT + 16)
                            pool.sem_inc(S["carrier"], 1)
                            pool.dma_reset(range(gat[0].num, gat[0].num + 2 * NBUF))
                            pool.sem_clear(range(gat[0].num, gat[0].num + 2 * NBUF))
                            pool.sem_inc(S["lists_free"], 1)
                        nc.gpsimd.tensor_scalar(round_lo[:, :], round_lo[:, :], float(K), None, ALU.add).then_inc(S["pool"], 1)
                        pool.wait_ge(S["pool"], (ro * ne + ne) * NPE + ro + 1)
                        pool.sem_inc(S["scattered"], 1)

                @block.vector
                def _(dve):
                    cnt = [0]

                    def link(ins):
                        cnt[0] += 1
                        ins.then_inc(S["dve"], 1)
                        dve.wait_ge(S["dve"], cnt[0])

                    def bt(ap):
                        return ap.unsqueeze(2).to_broadcast([P, TILES, GH])

                    def lrelu(dst, src):
                        return nc.vector.scalar_tensor_tensor(out=dst, in0=src, scalar=GAT_SLOPE, in1=src,
                                                              op0=ALU.mult, op1=ALU.max)

                    dve.wait_ge(S["consts"], 6)
                    link(nc.vector.tensor_copy(bins[:, :, :], bins_i[:, :, :]))
                    dve.wait_ge(S["keys"], 32)
                    with dve.Fori(0, EPP // HB // 2) as i:
                        for u in (0, 1):
                            c = bass.ds((2 * i + u) * HB, HB)
                            dve.wait_ge(S["free"], 2 * i + u + 1)
                            nc.vector.tensor_tensor(oh_lo[:, u], lo[:, c].unsqueeze(1).to_broadcast([P, P, HB]),
                                                    bins[:, :, :], ALU.is_equal).then_inc(S["made"], 1)
                            nc.vector.tensor_tensor(oh_hi[:, u], hi[:, c].unsqueeze(1).to_broadcast([P, HI, HB]),
                                                    bins[:, 0:HI, :], ALU.is_equal).then_inc(S["made"], 1)
                    dve.wait_ge(S["hist"], 1)
                    link(nc.vector.tensor_copy(nclamp[:, :], ps_hist[:, 0:HI]))
                    dve.wait_ge(S["small"], 16)
                    zc = t4b
                    link(nc.vector.tensor_tensor(t4[:, :, :], asrc, adst, ALU.add))
                    link(lrelu(t4[:, :, :], t4[:, :, :]))
                    link(nc.vector.tensor_tensor(zc[:, :, :], adst,
                                                 last[:, GAT:ROW].unsqueeze(1).to_broadcast([P, TILES, GH]), ALU.add))
                    link(lrelu(zc[:, :, :], zc[:, :, :]))
                    link(nc.vector.tensor_scalar(has[:, :], nclamp[:, :], 0.0, None, ALU.is_gt))
                    link(nc.vector.tensor_tensor(m0[:, :, :], zc[:, :, :], bt(has[:, :]), ALU.mult))
                    link(nc.vector.tensor_scalar(has[:, :], has[:, :], 1.0, -EMPTY, ALU.subtract, ALU.mult))
                    link(nc.vector.tensor_tensor(m0[:, :, :], m0[:, :, :], bt(has[:, :]), ALU.add))
                    link(nc.vector.tensor_tensor(m0[:, :, :], m0[:, :, :], t4[:, :, :], ALU.max))
                    link(nc.vector.tensor_tensor(t4[:, :, :], t4[:, :, :], m0[:, :, :], ALU.subtract))
                    link(nc.vector.tensor_tensor(zc[:, :, :], zc[:, :, :], m0[:, :, :], ALU.subtract))
                    link(nc.vector.tensor_scalar(zc[:, :, :], zc[:, :, :], 0.0, None, ALU.min))
                    dve.sem_inc(S["init"], 1)
                    dve.wait_ge(S["init"], 3)
                    link(nc.vector.tensor_tensor(zc[:, :, :], zc[:, :, :], bt(nclamp[:, :]), ALU.mult))
                    link(nc.vector.tensor_tensor(den[:, :, :], zc[:, :, :], t4[:, :, :], ALU.add))
                    for h in range(GH):
                        q = slice(h * GE, (h + 1) * GE)
                        link(nc.vector.tensor_tensor(num[:, :, q], hg_all[:, :, q], t4[:, :, h:h + 1].to_broadcast([P, TILES, GE]), ALU.mult))
                        link(nc.vector.tensor_tensor(prod[:, 0:TILES * GE].rearrange("p (t e) -> p t e", t=TILES),
                                                     last[:, q].unsqueeze(1).to_broadcast([P, TILES, GE]),
                                                     zc[:, :, h:h + 1].to_broadcast([P, TILES, GE]), ALU.mult))
                        link(nc.vector.tensor_tensor(num[:, :, q], num[:, :, q],
                                                     prod[:, 0:TILES * GE].rearrange("p (t e) -> p t e", t=TILES), ALU.add))
                    nr = dve.value_load(counts[0:1, 2:3], min_val=1, max_val=EDGES // K)
                    dve.sem_inc(S["ellfree"], 2)
                    NG = 14 * GROUPS
                    with dve.Fori(0, nr) as ro:
                        gk = 0

                        def link(ins):
                            nonlocal gk
                            gk += 1
                            ins.then_inc(S["dvg"], 1)
                            dve.wait_ge(S["dvg"], ro * NG + gk)
                        for g in range(GROUPS):
                            u = g % 2
                            gt = slice(g * GT, (g + 1) * GT)
                            E3 = ell[:, u].rearrange("p (t k c) -> p t k c", t=GT, k=K)
                            Ef = ell[:, u].rearrange("p (n c) -> p n c", c=ROW)
                            zk4 = zk[:, :].rearrange("p (t k h) -> p t k h", t=GT, k=K)
                            zl4 = zl[:, :].rearrange("p (t k h) -> p t k h", t=GT, k=K)

                            def over_k(ap):
                                return ap.unsqueeze(2).to_broadcast([P, GT, K, GH])
                            dve.wait_ge(els[u], ro * (16 * GROUPS // 2) + 16 * (g // 2 + 1))
                            link(nc.vector.tensor_tensor(zk4, E3[:, :, :, GAT:ROW], over_k(adst[:, gt]), ALU.add))
                            link(lrelu(zl[:, :], zk[:, :]))
                            link(nc.vector.tensor_reduce(mx[:, :, :], zl4.rearrange("p t k h -> p t h k"), AX.X, ALU.max))
                            link(nc.vector.tensor_tensor(m1[:, :, :], mx[:, :, :], m0[:, gt], ALU.max))
                            link(nc.vector.tensor_tensor(sc[:, :, :], m0[:, gt], m1[:, :, :], ALU.subtract))
                            link(nc.vector.tensor_copy(m0[:, gt], m1[:, :, :]))
                            link(nc.vector.tensor_tensor(zk4, zl4, over_k(m1[:, :, :]), ALU.subtract))
                            dve.sem_inc(S["ex_in"], 1)
                            dve.wait_ge(S["ex_out"], ro * GROUPS + g + 1)
                            link(nc.vector.tensor_reduce(mx[:, :, :], zk4.rearrange("p t k h -> p t h k"), AX.X, ALU.add))
                            link(nc.vector.tensor_tensor(den[:, gt], den[:, gt], sc[:, :, :], ALU.mult))
                            link(nc.vector.tensor_tensor(den[:, gt], den[:, gt], mx[:, :, :], ALU.add))
                            link(nc.vector.tensor_tensor(prod[:, :].rearrange("p (n h e) -> p n h e", h=GH, e=GE),
                                                         Ef[:, :, 0:GAT].rearrange("p n (h e) -> p n h e", h=GH),
                                                         zk[:, :].rearrange("p (n h) -> p n h", h=GH).unsqueeze(3)
                                                         .to_broadcast([P, GT * K, GH, GE]), ALU.mult))
                            dve.sem_inc(S["ellfree"], 1)
                            link(nc.vector.tensor_reduce(part[:, :, :], prod[:, :].rearrange("p (t k f) -> p t f k", t=GT, k=K),
                                                         AX.X, ALU.add))
                            n4 = num[:, gt].rearrange("p t (h e) -> p t h e", h=GH)
                            link(nc.vector.tensor_tensor(n4, n4, sc[:, :, :].unsqueeze(3).to_broadcast([P, GT, GH, GE]), ALU.mult))
                            link(nc.vector.tensor_tensor(num[:, gt], num[:, gt], part[:, :, :], ALU.add))
                        assert gk == NG, gk

                @block.tensor
                def _(pe):
                    pe.sem_inc(S["free"], 2)
                    pe.wait_ge(S["consts"], 6)
                    nc.tensor.matmul(ps_hist[:, 0:HI], zeros[:, :], zeros[:, 0:HI], start=True, stop=False,
                                     skip_group_check=True)
                    pe.wait_ge(S["wl"], 64)
                    HPG = EPP // HB // (NODES // MG)

                    def hist_batch(g, n):
                        u = n % 2
                        pe.wait_ge(S["made"], 2 * (g * HPG + n + 1))
                        for c in range(HB):
                            mm = nc.tensor.matmul(ps_hist[:, 0:HI], oh_lo[:, u, :, c], oh_hi[:, u, :, c], start=False,
                                                  stop=False, skip_group_check=True)
                        mm.then_inc(S["free"], 1)

                    with pe.Fori(0, NODES // MG // 2) as i:
                        for u in (0, 1):
                            g = 2 * i + u
                            pe.wait_ge(xls[u], 16 * (i + 1))
                            for c in range(GE * 2):
                                pe.wait_ge(S["gelu"], g * 8 + c + 1)
                                mm = nc.tensor.matmul(ps1[c % 4][:, :], w1[:, c // 2, (c % 2) * P:(c % 2 + 1) * P], xg[:, u],
                                                      start=True, stop=True)
                                mm.then_inc(S["l1"], 1)
                                hist_batch(g, c)
                            pe.wait_ge(S["gelu"], g * 8 + 8 + 4)
                            for t in range(4):
                                pe.wait_ge(S["ysb"], g * 4 + t + 1)
                                for e in range(GE):
                                    nc.tensor.matmul(ps2[t % 2][:, e * DIM:(e + 1) * DIM], ones[:, :],
                                                     b2[:, e * DIM:(e + 1) * DIM], start=True, stop=False)
                                    for c in (0, 1):
                                        mm = nc.tensor.matmul(ps2[t % 2][:, e * DIM:(e + 1) * DIM], hh[:, 2 * e + c, t * P:(t + 1) * P],
                                                              w2[:, e, c], start=False, stop=(c == 1))
                                mm.then_inc(S["l2"], 1)
                                hist_batch(g, 8 + 2 * t)
                                hist_batch(g, 9 + 2 * t)
                    nc.tensor.matmul(ps_hist[:, 0:HI], zeros[:, :], zeros[:, 0:HI], start=False, stop=True,
                                     skip_group_check=True).then_inc(S["hist"], 1)

                @block.scalar
                def _(act):
                    for dst, src in ((w1[:, :, :], w["W1"].rearrange("e d h -> d e h")), (b1[:, :], w["b1T"]),
                                     (w2[:, :, :, :].rearrange("p e c o -> p (e c) o"),
                                      w["W2"].rearrange("e (c p) o -> p (e c) o", p=P)),
                                     (b2[:, :], w["b2"].rearrange("e o -> (e o)").unsqueeze(0))):
                        act.dma_start(dst, src).then_inc(S["wl"], 16)
                    for t in range(4):
                        act.dma_start(prime[:, NBUF + t], counts_dram[0:1, :]).then_inc(yst[t], 16)
                    act.sem_inc(S["gelu"], 4)
                    act.sem_inc(S["l2"], 4)
                    act.sem_inc(S["ysb"], 2)
                    for u in (0, 1):
                        act.dma_start(xg[:, u], xT_dram[:, u * MG:(u + 1) * MG]).then_inc(xls[u], 16)
                    act.wait_ge(S["wl"], 64)
                    def groups(i, more):
                        for u in (0, 1):
                            g = 2 * i + u
                            for c in range(GE * 2):
                                act.wait_ge(S["l1"], g * 8 + c + 1)
                                if c == 0:
                                    act.wait_ge(S["l2"], g * 4 + 4)
                                nc.scalar.activation(hh[:, c], ps1[c % 4][:, :], ACT.Gelu, bias=b1[:, c:c + 1]).then_inc(S["gelu"], 1)
                            if more:
                                act.dma_start(xg[:, u], xT_dram[:, bass.ds((g + 2) * MG, MG)]).then_inc(xls[u], 16)
                            for t in range(4):
                                act.wait_ge(S["l2"], g * 4 + t + 5)
                                act.wait_ge(yst[t], 16 * g + 16)
                                nc.scalar.copy(yb[:, t], ps2[t % 2][:, :]).then_inc(S["ysb"], 1)
                                act.wait_ge(S["ysb"], g * 4 + t + 3)
                                act.dma_start(Y[bass.ds(g * 4 + t, 1)].squeeze(0) if more else Y[g * 4 + t],
                                              yb[:, t]).then_inc(yst[t], 16)

                    pairs = NODES // MG // 2
                    with act.Fori(0, pairs - 1) as i:
                        groups(i, True)
                    groups(pairs - 1, False)
                    act.wait_ge(S["init"], 1)
                    nc.scalar.activation(t4[:, :, :], t4[:, :, :], ACT.Exp).then_inc(S["init"], 1)
                    nc.scalar.activation(t4b[:, :, :], t4b[:, :, :], ACT.Exp).then_inc(S["init"], 1)
                    for t in range(4):
                        act.wait_ge(yst[t], 16 * (NODES // MG) + 16)
                    nr = act.value_load(counts[0:1, 2:3], min_val=1, max_val=EDGES // K)
                    with act.Fori(0, nr) as ro:
                        for g in range(GROUPS):
                            act.wait_ge(S["ex_in"], ro * GROUPS + g + 1)
                            nc.scalar.activation(sc[:, :, :], sc[:, :, :], ACT.Exp)
                            nc.scalar.activation(zk[:, :], zk[:, :], ACT.Exp).then_inc(S["ex_out"], 1)

        with ExitStack() as c2:
            def sb2(name, shape, dt=F32):
                return c2.enter_context(nc.sbuf_tensor("m2_" + name, shape, dt))
            bg = sb2("bg", [P, GAT])
            gam = sb2("gam", [P, GAT])
            bet = sb2("bet", [P, GAT])
            a1 = sb2("a1", [P, TILES, GAT])
            a2 = sb2("a2", [P, TILES, GAT])
            r1 = sb2("r1", [P, TILES])
            r2 = sb2("r2", [P, TILES])
            hf = sb2("hf", [P, TILES])
            s4 = sb2("s4", [P, TILES, GE])
            rk = sb2("rk", [P, TILES, GE])
            cmp = sb2("cmp", [P, TILES])
            g4 = sb2("g4", [P, TILES, GE])
            NY = 8
            NG = 4
            yl = sb2("yl", [P, NY, GE * DIM])
            S2 = {n: c2.enter_context(nc.semaphore("m2_" + n)) for n in
                  ("ld", "carrier", "dve", "pw", "pwd", "ex", "exd", "y0", "y1", "y2", "y3", "y4", "y5", "y6", "y7", "yfree", "comb", "od", "stored")}
            ys = [S2[f"y{t}"] for t in range(NY)]
            xo = out.rearrange("(t b) n d -> (b n) t d", b=2)
            OG = 8
            with nc.Block() as block:
                @block.sync
                def _(sp):
                    for dst, src in ((bg, w["b_gat"]), (gam, w["gamma"]), (bet, w["beta"])):
                        sp.dma_start(dst[:, :], src.partition_broadcast(P)).then_inc(S2["ld"], 16)
                    with sp.Fori(0, TILES // NY) as i:
                        for t in range(NY):
                            sp.wait_ge(S2["yfree"], i * NY + t + 1)
                            sp.sem_inc(S2["carrier"], 1)
                            sp.dma_start(yl[:, t], Y[bass.ds(i * NY + t, 1)].squeeze(0)).then_inc(ys[t], 16)
                    for t in range(NY):
                        sp.wait_ge(ys[t], 16 * (TILES // NY))

                @block.gpsimd
                def _(pool):
                    nc.gpsimd.memset(hf[:, :], -0.5).then_inc(S2["pw"], 1)
                    pool.wait_ge(S2["pw"], 2)
                    nc.gpsimd.tensor_tensor(r2[:, :], r1[:, :], hf[:, :], ALU.pow).then_inc(S2["pwd"], 1)

                @block.scalar
                def _(act):
                    act.wait_ge(S2["ex"], 1)
                    nc.scalar.activation(g4[:, :, :], g4[:, :, :], ACT.Exp).then_inc(S2["exd"], 1)
                    with act.Fori(0, TILES // OG) as i:
                        act.wait_ge(S2["comb"], OG * i + OG)
                        act.dma_start(xo[:, bass.ds(i * OG, OG)], x_all[:, bass.ds(i * OG, OG)]).then_inc(S2["stored"], 16)
                    act.wait_ge(S2["stored"], 16 * (TILES // OG))

                @block.vector
                def _(dve):
                    cnt = [0]

                    def link(ins):
                        cnt[0] += 1
                        ins.then_inc(S2["dve"], 1)
                        dve.wait_ge(S2["dve"], cnt[0])
                    tt, ts, red = nc.vector.tensor_tensor, nc.vector.tensor_scalar, nc.vector.tensor_reduce

                    def f16(ap):
                        return ap.unsqueeze(2).to_broadcast([P, TILES, GAT])

                    def row(ap):
                        return ap[:, :].unsqueeze(1).to_broadcast([P, TILES, GAT])
                    dve.wait_ge(S2["ld"], 48)
                    link(ts(den[:, :, :], den[:, :, :], 1e-16, None, ALU.add))
                    link(nc.vector.reciprocal(den[:, :, :], den[:, :, :]))
                    for h in range(GH):
                        q = slice(h * GE, (h + 1) * GE)
                        link(tt(a1[:, :, q], num[:, :, q], den[:, :, h:h + 1].to_broadcast([P, TILES, GE]), ALU.mult))
                    link(tt(a1[:, :, :], a1[:, :, :], row(bg), ALU.add))
                    link(red(r1[:, :], a1[:, :, :], AX.X, ALU.add))
                    link(ts(r1[:, :], r1[:, :], 1.0 / GAT, None, ALU.mult))
                    link(tt(a1[:, :, :], a1[:, :, :], f16(r1[:, :]), ALU.subtract))
                    link(tt(a2[:, :, :], a1[:, :, :], a1[:, :, :], ALU.mult))
                    link(red(r1[:, :], a2[:, :, :], AX.X, ALU.add))
                    link(ts(r1[:, :], r1[:, :], 1.0 / GAT, EPS, ALU.mult, ALU.add))
                    dve.sem_inc(S2["pw"], 1)
                    dve.wait_ge(S2["pwd"], 1)
                    link(tt(a1[:, :, :], a1[:, :, :], f16(r2[:, :]), ALU.mult))
                    link(tt(a1[:, :, :], a1[:, :, :], row(gam), ALU.mult))
                    link(tt(a1[:, :, :], a1[:, :, :], row(bet), ALU.add))
                    link(red(s4[:, :, :], a1[:, :, :].rearrange("p t (h e) -> p t e h", h=GH), AX.X, ALU.add))
                    link(ts(s4[:, :, :], s4[:, :, :], 1.0 / GH, None, ALU.mult))
                    link(nc.vector.memset(rk[:, :, :], 0.0))
                    for e in range(GE):
                        for o in range(GE):
                            if o != e:
                                link(tt(cmp[:, :], s4[:, :, o], s4[:, :, e], ALU.is_ge if o < e else ALU.is_gt))
                                link(tt(rk[:, :, e], rk[:, :, e], cmp[:, :], ALU.add))
                    link(red(r1[:, :], s4[:, :, :], AX.X, ALU.max))
                    link(tt(g4[:, :, :], s4[:, :, :], r1[:, :].unsqueeze(2).to_broadcast([P, TILES, GE]), ALU.subtract))
                    dve.sem_inc(S2["ex"], 1)
                    dve.wait_ge(S2["exd"], 1)
                    link(nc.vector.scalar_tensor_tensor(out=g4[:, :, :], in0=rk[:, :, :], scalar=2.0, in1=g4[:, :, :],
                                                        op0=ALU.is_lt, op1=ALU.mult))
                    link(red(r1[:, :], g4[:, :, :], AX.X, ALU.add))
                    link(nc.vector.reciprocal(r1[:, :], r1[:, :]))
                    link(tt(g4[:, :, :], g4[:, :, :], r1[:, :].unsqueeze(2).to_broadcast([P, TILES, GE]), ALU.mult))
                    dve.sem_inc(S2["yfree"], NY)
                    with dve.Fori(0, TILES // NY) as i:
                        for half in range(NY // NG):
                            tiles = range(half * NG, (half + 1) * NG)
                            for e in range(GE):
                                for t in tiles:
                                    if e == 0:
                                        dve.wait_ge(ys[t], 16 * (i + 1))
                                    else:
                                        dve.wait_ge(S2["od"], (i * NY + half * NG) * (GE - 1) + (e - 1) * NG + t % NG + 1)
                                    xt = x_all[:, bass.ds(i * NY + t, 1), :].squeeze(1)
                                    gs = g4[:, bass.ds(i * NY + t, 1), e:e + 1].squeeze(1)
                                    nc.vector.scalar_tensor_tensor(
                                        out=xt, in0=yl[:, t, e * DIM:(e + 1) * DIM], scalar=gs, in1=xt, op0=ALU.mult,
                                        op1=ALU.add).then_inc(S2["od"] if e < GE - 1 else S2["comb"], 1)
                            dve.wait_ge(S2["comb"], i * NY + (half + 1) * NG)
                            dve.sem_inc(S2["yfree"], NG)


_ARGS = ("x", "adj", "adjT", "fcT", "fp", "fcbT", "q_w", "k_w", "q_b", "k_b", "fp_b", "WiT", "biT", "WoT", "bo", "gWT",
         "gb", "Wgat", "att_src", "att_dst", "route", "WsT", "bsT", "WrT", "brT", "b_gat", "gamma", "beta", "W1", "b1T",
         "W2", "b2", "edges")


def program(nc, w, out):
    lists = nc.dram_tensor("edge_lists", [3, P, LIST], F32).ap()
    hist_keys = nc.dram_tensor("hist_keys", [2, P, EPP], BF16).ap()
    counts = nc.dram_tensor("loop_counts", [P, 4], I32).ap()
    xT = nc.dram_tensor("features_T", [P, NODES], F32).ap()
    table = nc.dram_tensor("gat_table", [NODES, ROW], F32).ap()
    sort_edges(nc, w["edges"], hist_keys, lists, counts)
    with ExitStack() as ctx:
        x_all = ctx.enter_context(nc.sbuf_tensor("x_all", [P, TILES, DIM], F32))
        hg_all = ctx.enter_context(nc.sbuf_tensor("hg_all", [P, TILES, COLS24], F32))
        node_layers(nc, w, x_all, hg_all, xT, table)
        edge_and_expert_layers(nc, w, x_all, hg_all, xT, table, hist_keys, lists, counts, out)


def kernel(**inputs):
    import numpy as np
    import concourse.bacc as bacc
    from concourse.bass_utils import run_bass_kernel_spmd

    g = {k: np.asarray(v) for k, v in inputs.items()}

    def lay(a):
        return np.ascontiguousarray(a)

    C = HID // P
    host = {
        "x": g["x"], "adj": g["adj"], "adjT": lay(g["adj"].transpose(0, 2, 1)),
        "fcT": lay(g["L0_gnn_fc_w"].T), "fp": g["L0_gnn_fp_w"],
        "fcbT": lay(g["L0_gnn_fc_b"].reshape(HEADS, DIM).T),
        "q_w": g["L0_gnn_q_w"], "k_w": g["L0_gnn_k_w"], "q_b": g["L0_gnn_q_b"], "k_b": g["L0_gnn_k_b"],
        "fp_b": g["L0_gnn_fp_b"],
        "WiT": lay(g["L0_ffn_Wi"].T), "biT": lay(g["L0_ffn_bi"].reshape(C, P).T),
        "WoT": lay(g["L0_ffn_Wo"].T), "bo": g["L0_ffn_bo"],
        "gWT": lay(g["L1_gnn_W"].T), "gb": g["L1_gnn_b"], "Wgat": g["L1_ffn_W_gat"],
        "att_src": lay(g["L1_ffn_att_src"].reshape(-1)), "att_dst": lay(g["L1_ffn_att_dst"].reshape(-1)),
        "route": g["L0_ffn_route_id"],
        "WsT": lay(g["L0_ffn_Ws"][:, 0].transpose(0, 2, 1).reshape(LAYERS, C, P, HID).transpose(2, 0, 1, 3)
                   .reshape(P, LAYERS * C * HID)),
        "bsT": lay(g["L0_ffn_bs"].reshape(LAYERS, C, P).transpose(2, 0, 1).reshape(P, LAYERS * C)),
        "WrT": lay(g["L0_ffn_Wr"].transpose(1, 0, 3, 2).reshape(EXP0, LAYERS, C, P, HID).transpose(0, 3, 1, 2, 4)
                   .reshape(EXP0, P, LAYERS * C * HID)),
        "brT": lay(g["L0_ffn_br"].reshape(LAYERS, EXP0, C, P).transpose(1, 3, 0, 2).reshape(EXP0, P, LAYERS * C)),
        "b_gat": g["L1_ffn_b_gat"], "gamma": g["L1_ffn_ln_gamma"], "beta": g["L1_ffn_ln_beta"],
        "W1": g["L1_ffn_W1"], "b1T": lay(g["L1_ffn_b1"].reshape(GE * C, P).T), "W2": g["L1_ffn_W2"],
        "b2": g["L1_ffn_b2"], "edges": g["L1_ffn_edge_index"],
    }
    nc = bacc.Bacc("TRN2", target_bir_lowering=False, num_devices=1)
    arrays, w = {}, {}
    for name in _ARGS:
        arrays["in_" + name] = host[name]
        w[name] = nc.dram_tensor("in_" + name, host[name].shape, mybir.dt.from_np(host[name].dtype),
                                 kind="ExternalInput").ap()
    out = nc.dram_tensor("out_x", (TILES * 2, NB, DIM), F32, kind="ExternalOutput").ap()
    program(nc, w, out)
    got = run_bass_kernel_spmd(nc, [arrays], core_ids=[0])
    return got.results[0]["out_x"]
```

```python
from contextlib import ExitStack
import concourse.bass as bass
from concourse import mybir
F32 = mybir.dt.float32
BF16 = mybir.dt.bfloat16
I32 = mybir.dt.int32
U32 = mybir.dt.uint32
ALU = mybir.AluOpType
ACT = mybir.ActivationFunctionType
AX = mybir.AxisListType
P = 128

NODES = 8192
HI = NODES // P
EDGES = 524288
EPP = EDGES // P
SEGS = 4
SEG = EPP // SEGS
ROUNDS = 11
SLOTS = 8 * ROUNDS
COLS = SEGS * SLOTS
EPOCHS = -(-SEG // SLOTS)
LIST = EPOCHS * COLS
BATCH = 8
BPE = COLS // BATCH
HALF = BATCH // 2
PAIRS = BATCH // 2
QB = 4
HB = 16
TAG = 0x20000000
K = 16
SB = 13
HID = 256
EXP0 = 16
LAYERS = 2
WROW = LAYERS * 2 * HID + LAYERS * 2
NW = 4
RECORD = 3
TURN_COLS = 16
CHUNK = 6
PLACED = NODES // P * CHUNK
NOWHERE = 1 << 20
NO_RANK = float(1 << 20)
COUNTS = 3 + EPOCHS


def clear(nc, sems, pool_dma=()):
    with nc.Block() as block:
        @block.gpsimd
        def _(pool):
            for s in pool_dma:
                pool.dma_reset(range(s.num, s.num + 1))
            for s in sems:
                pool.sem_clear(s)


def fields(flat, j, dt=None):
    flat = flat if dt is None else flat.bitcast(dt)
    return flat.rearrange("p (c k) -> p c k", k=RECORD)[:, :, j]


def sort_edges(nc, edge_index, hist_keys, lists, counts_out, records, place, w, expert_w):

    with ExitStack() as ctx:
        def sb(name, shape, dt=F32):
            return ctx.enter_context(nc.sbuf_tensor("e_" + name, shape, dt))

        def ps(name, shape, dt=F32):
            return ctx.enter_context(nc.psum_tensor("e_" + name, shape, dt))

        def sem(name):
            sems.append(ctx.enter_context(nc.semaphore("e_" + name)))
            return sems[-1]
        sems = []

        src = sb("src", [P, SEG], I32)
        dst = sb("dst", [P, SEG], I32)
        key = sb("key", [P, EPP])
        keyi = key[:, :].bitcast(I32)
        mask = sb("mask", [P, SEG])
        lo = sb("lo", [P, EPP], BF16)
        hi = sb("hi", [P, EPP], BF16)
        tmp = sb("tmp", [P, SEG], I32)
        counts = sb("counts", [P, SEGS])
        countmax = sb("countmax", [P, SEGS])
        edge_steps = sb("edge_steps", [P, EPOCHS])
        top = sb("top", [P, 1])
        n_epochs_f = sb("n_epochs_f", [P, 1])
        n_epochs = sb("n_epochs", [P, COUNTS], I32)
        all_ones = sb("all_ones", [P, P], BF16)
        index = sb("index", [P, COLS])
        per_seg = sb("per_seg", [P, SEGS])
        per_seg_b = sb("per_seg_b", [P, SEGS], BF16)
        sums = sb("sums", [P, 2, SEGS])
        start = sb("start", [P, SEGS])
        total = sb("total", [P, 1])
        total_i = sb("total_i", [P, 1], I32)
        page = sb("page", [P, COLS * RECORD])
        top_rank = sb("top_rank", [P, 2])
        rounds_i = sb("rounds_i", [P, 2], I32)
        iota_i = sb("iota_i", [P, P], I32)
        iota = sb("iota", [P, P], BF16)
        ident = sb("ident", [P, P], BF16)
        ident_hi = sb("ident_hi", [P, P], BF16)
        later = sb("later", [P, P], BF16)
        zeros = sb("zeros", [P, P], BF16)
        bins = sb("bins", [P, P, BATCH], BF16)
        ones = sb("ones", [P, HI], BF16)
        oh_lo = sb("oh_lo", [P, QB, P, BATCH], BF16)
        oh_hi = sb("oh_hi", [P, QB, HI, BATCH], BF16)
        picked = sb("picked", [P, COLS])
        picked_i = picked[:, :].bitcast(I32)
        dec = sb("dec", [P, COLS], I32)
        dec2 = sb("dec2", [P, COLS], I32)
        node_d = sb("node_d", [P, LIST + 2 * BATCH])
        node_lo = sb("node_lo", [P, LIST + 2 * BATCH], BF16)
        node_hi = sb("node_hi", [P, LIST + 2 * BATCH], BF16)
        node_s = sb("node_s", [P, LIST], I32)
        rank = sb("rank", [P, LIST])
        slotf = sb("slotf", [P, LIST])
        lo8 = sb("lo8", [P, QB, BATCH], BF16)
        hi8 = sb("hi8", [P, QB, BATCH], BF16)
        same = sb("same", [P, 2, BATCH, P], BF16)
        loT = sb("loT", [P, 2, BATCH, P])
        loTb = sb("loTb", [P, 2, PAIRS, P], BF16)
        hist = sb("hist", [P, 2, HI])
        first = sb("first", [P, 2, PAIRS, HI], BF16)
        masked = sb("masked", [P, 2, BATCH, HI])

        ps_hist = ps("ps_hist", [P, 512])
        ps_row = ps("ps_row", [P, 2, BATCH, P])
        ps_base = ps("ps_base", [P, 2, BATCH, HI])
        ps_turn = ps("ps_turn", [P, 512])
        ps_loT = ps_turn[:, 0:256].bitcast(BF16).rearrange("p (k e) -> p k e", k=HALF)
        ps_first = ps_turn[:, 256:512].rearrange("p (j h) -> p j h", j=PAIRS)

        loaded = [sem(f"loaded{s}") for s in range(SEGS)]
        consts = sem("consts")
        decoded = sem("decoded")
        chain = sem("chain")
        counted = sem("counted")
        maxed = sem("maxed")
        stored = sem("stored")
        steps = [0]

        with nc.Block() as block:
            @block.sync
            def _(sp):
                for s in range(SEGS):
                    if s:
                        sp.wait_ge(decoded, s)
                    e = edge_index.rearrange("two (p e) -> two p e", p=P)
                    sp.dma_start(src[:, :], e[0, :, s * SEG:(s + 1) * SEG]).then_inc(loaded[s], 16)
                    sp.dma_start(dst[:, :], e[1, :, s * SEG:(s + 1) * SEG]).then_inc(loaded[s], 16)
                sp.wait_ge(decoded, SEGS)
                sp.dma_start(hist_keys[0], lo[:, :]).then_inc(stored, 16)
                sp.dma_start(hist_keys[1], hi[:, :]).then_inc(stored, 16)
                sp.wait_ge(stored, 32)

            @block.gpsimd
            def _(pool):
                nc.gpsimd.iota(iota_i[:, :], pattern=[[1, P]], base=0, channel_multiplier=0).then_inc(consts, 1)
                nc.gpsimd.iota(edge_steps[:, :], pattern=[[SLOTS, EPOCHS]], base=0, channel_multiplier=0,
                               allow_small_or_imprecise_dtypes=True).then_inc(consts, 1)
                nc.gpsimd.memset(ident[:, :], 0.0).then_inc(consts, 1)
                nc.gpsimd.memset(ident_hi[:, :], 0.0).then_inc(consts, 1)
                nc.gpsimd.memset(later[:, :], 1.0).then_inc(consts, 1)
                nc.gpsimd.memset(zeros[:, :], 0.0).then_inc(consts, 1)
                nc.gpsimd.memset(rank[:, :], 0.0).then_inc(consts, 1)
                nc.gpsimd.memset(ones[:, :], 1.0).then_inc(consts, 1)
                nc.gpsimd.memset(all_ones[:, :], 1.0).then_inc(consts, 1)
                nc.gpsimd.memset(place[:, :], NOWHERE).then_inc(consts, 1)
                nc.gpsimd.memset(records[:, :], 0.0).then_inc(consts, 1)
                nc.gpsimd.iota(index[:, :].rearrange("p (s c) -> p s c", s=SEGS), pattern=[[0, SEGS], [1, SLOTS]], base=0,
                               channel_multiplier=0, allow_small_or_imprecise_dtypes=True).then_inc(consts, 1)
                pool.wait_ge(consts, 12)
                nc.gpsimd.tensor_copy(iota[:, :], iota_i[:, :]).then_inc(consts, 1)
                for m, v in ((ident, 1.0), (ident_hi, float(P))):
                    nc.gpsimd.affine_select(out=m[:, :], in_=m[:, :], compare_op=ALU.not_equal, fill=v, base=0,
                                            pattern=[[-1, P]], channel_multiplier=1).then_inc(consts, 1)
                nc.gpsimd.affine_select(out=later[:, :], in_=later[:, :], compare_op=ALU.is_gt, fill=0.0,
                                        base=0, pattern=[[1, P]], channel_multiplier=-1).then_inc(consts, 1)
                pool.wait_ge(consts, 16)
                nc.gpsimd.tensor_copy(bins[:, :, :], iota[:, :].unsqueeze(2).to_broadcast([P, P, BATCH])
                                      ).then_inc(consts, 1)
                pool.wait_ge(counted, 1)
                nc.gpsimd.partition_all_reduce(countmax[:, :], counts[:, :], P, bass.bass_isa.ReduceOp.max).then_inc(maxed, 1)

            @block.vector
            def _(dve):
                def link(ins):
                    steps[0] += 1
                    ins.then_inc(chain, 1)
                    dve.wait_ge(chain, steps[0])

                for s in range(SEGS):
                    q = slice(s * SEG, (s + 1) * SEG)
                    dve.wait_ge(loaded[s], 32)
                    link(nc.vector.tensor_scalar(dst[:, :], dst[:, :], float(NODES), None, ALU.min))
                    link(nc.vector.tensor_scalar(src[:, :], src[:, :], float(NODES - 1), None, ALU.min))
                    link(nc.vector.tensor_scalar(mask[:, :], dst[:, :], float(NODES), None, ALU.is_lt))
                    link(nc.vector.scalar_tensor_tensor(out=mask[:, :], in0=src[:, :], scalar=float(NODES - 1),
                                                        in1=mask[:, :], op0=ALU.is_lt, op1=ALU.mult))
                    link(nc.vector.tensor_reduce(counts[:, s:s + 1], mask[:, :], AX.X, ALU.add))
                    link(nc.vector.tensor_scalar(tmp[:, :], dst[:, :], SB, TAG, ALU.logical_shift_left, ALU.bitwise_or))
                    link(nc.vector.tensor_tensor(keyi[:, q], tmp[:, :], src[:, :], ALU.bitwise_or))
                    link(nc.vector.tensor_tensor(key[:, q], key[:, q], mask[:, :], ALU.mult))
                    link(nc.vector.tensor_scalar(tmp[:, :], dst[:, :], P - 1, None, ALU.bitwise_and))
                    link(nc.vector.tensor_copy(lo[:, q], tmp[:, :]))
                    link(nc.vector.tensor_scalar(tmp[:, :], dst[:, :], 7, None, ALU.logical_shift_right))
                    link(nc.vector.tensor_scalar(mask[:, :], src[:, :], float(NODES - 1), 256.0, ALU.is_lt, ALU.mult))
                    link(nc.vector.tensor_tensor(hi[:, q], tmp[:, :], mask[:, :], ALU.add))
                    dve.sem_inc(decoded, 1)
                dve.sem_inc(counted, 1)
                dve.wait_ge(consts, 17)
                dve.wait_ge(maxed, 1)
                link(nc.vector.tensor_reduce(top[:, :], countmax[:, :], AX.X, ALU.max))
                link(nc.vector.tensor_scalar(edge_steps[:, :], edge_steps[:, :], top[:, 0:1], None, ALU.is_lt))
                link(nc.vector.tensor_reduce(n_epochs_f[:, :], edge_steps[:, :], AX.X, ALU.add))
                link(nc.vector.tensor_scalar(n_epochs_f[:, :], n_epochs_f[:, :], 1.0, None, ALU.max))
                link(nc.vector.tensor_copy(n_epochs[:, 0:1], n_epochs_f[:, :]))
                link(nc.vector.tensor_scalar(n_epochs[:, 1:2], n_epochs_f[:, :], float(BPE // QB), None, ALU.mult))
        carrier = sem("carrier")
        chain2 = sem("chain2")
        shared_w = ctx.enter_context(nc.sbuf_tensor("e_shared_w", [P, WROW], F32))
        routed_w = ctx.enter_context(nc.sbuf_tensor("e_routed_w", [P, NW, WROW], F32))
        ident32 = ctx.enter_context(nc.sbuf_tensor("e_ident32", [P, P], F32))
        w_loaded = [sem(f"w_loaded{u}") for u in range(NW)]
        w_stored = [sem(f"w_stored{u}") for u in range(NW)]
        shared_loaded = sem("shared_loaded")
        shared_done = sem("shared_done")
        w_sum = sem("w_sum")
        with nc.Block() as block:
            @block.sync
            def _(sp):
                sp.dma_start(shared_w[:, 0:LAYERS * 2 * HID], w["WsT"]).then_inc(shared_loaded, 16)
                sp.dma_start(shared_w[:, LAYERS * 2 * HID:WROW], w["bsT"]).then_inc(shared_loaded, 16)
                for e in range(EXP0 + 2):
                    if e < EXP0:
                        u = e % NW
                        if e >= NW:
                            sp.wait_ge(w_stored[u], 16 * (e // NW))
                        sp.dma_start(routed_w[:, u, 0:LAYERS * 2 * HID], w["WrT"][e]).then_inc(w_loaded[u], 16)
                        sp.dma_start(routed_w[:, u, LAYERS * 2 * HID:WROW], w["brT"][e]).then_inc(w_loaded[u], 16)
                    if e >= 2:
                        sp.wait_ge(w_sum, e - 1)
                        sp.dma_start(expert_w[e - 2], routed_w[:, (e - 2) % NW]).then_inc(w_stored[(e - 2) % NW], 16)
                for u in range(NW):
                    sp.wait_ge(w_stored[u], 16 * (EXP0 // NW))

            @block.gpsimd
            def _(pool):
                nc.gpsimd.memset(ident32[:, :], 0.0).then_inc(shared_done, 1)
                pool.wait_ge(shared_done, 1)
                nc.gpsimd.affine_select(out=ident32[:, :], in_=ident32[:, :], compare_op=ALU.not_equal, fill=1.0, base=0,
                                        pattern=[[-1, P]], channel_multiplier=1).then_inc(shared_done, 1)
                pool.wait_ge(shared_loaded, 32)
                for k in range(LAYERS * 2):
                    q = k * HID + (k % 2) * P
                    pool.wait_ge(shared_done, 2 + k)
                    nc.gpsimd.tensor_tensor(shared_w[:, q:q + P], shared_w[:, q:q + P], ident32[:, :],
                                            ALU.add).then_inc(shared_done, 1)
                pool.wait_ge(shared_done, 2 + LAYERS * 2)
                for e in range(EXP0):
                    u = e % NW
                    pool.wait_ge(w_loaded[u], 32 * (e // NW + 1))
                    nc.gpsimd.tensor_tensor(routed_w[:, u], routed_w[:, u], shared_w[:, :], ALU.add).then_inc(w_sum, 1)

            @block.vector
            def _(dve):
                ne = dve.value_load(n_epochs[0:1, 0:1], min_val=1, max_val=EPOCHS)
                N2 = 2 * ROUNDS + 9
                nc.vector.memset(node_d[:, :], float(NODES)).then_inc(chain2, 1)
                nc.vector.memset(node_s[:, :], 0).then_inc(chain2, 1)
                nc.vector.memset(node_lo[:, :], 0.0).then_inc(chain2, 1)
                nc.vector.memset(node_hi[:, :], float(HI)).then_inc(chain2, 1)
                dve.wait_ge(chain2, 4)
                with dve.Fori(0, ne) as ep:
                    k = 4
                    for r in range(ROUNDS):
                        for s in range(SEGS):
                            m8 = picked[:, s * SLOTS + 8 * r:s * SLOTS + 8 * r + 8]
                            ins = nc.vector.max(out=m8, in_=key[:, s * SEG:(s + 1) * SEG])
                        ins.then_inc(chain2, 1)
                        k += 1
                        dve.wait_ge(chain2, ep * N2 + k)
                        dve.sem_inc(carrier, 1)
                        for s in range(SEGS):
                            m8 = picked[:, s * SLOTS + 8 * r:s * SLOTS + 8 * r + 8]
                            sl = key[:, s * SEG:(s + 1) * SEG]
                            ins = nc.vector.match_replace(out=sl, in_to_replace=m8, in_values=sl, imm_value=0.0)
                        ins.then_inc(chain2, 1)
                        k += 1
                        dve.wait_ge(chain2, ep * N2 + k)
                        dve.sem_inc(carrier, 1)
                    q = bass.ds(ep * COLS, COLS)

                    def link(ins):
                        nonlocal k
                        k += 1
                        ins.then_inc(chain2, 1)
                        dve.wait_ge(chain2, ep * N2 + k)
                    link(nc.vector.tensor_scalar(node_s[:, q], picked_i, NODES - 1, None, ALU.bitwise_and))
                    link(nc.vector.tensor_scalar(dec[:, :], picked_i, SB, NODES - 1, ALU.logical_shift_right,
                                                 ALU.bitwise_and))
                    link(nc.vector.tensor_scalar(dec2[:, :], picked[:, :], 0.0, float(NODES), ALU.is_equal, ALU.mult))
                    link(nc.vector.tensor_tensor(node_d[:, q], dec[:, :], dec2[:, :], ALU.add))
                    dve.sem_inc(carrier, 1)
                    link(nc.vector.tensor_copy(dec[:, :], node_d[:, q]))
                    link(nc.vector.tensor_scalar(dec2[:, :], dec[:, :], P - 1, None, ALU.bitwise_and))
                    link(nc.vector.tensor_copy(node_lo[:, q], dec2[:, :]))
                    link(nc.vector.tensor_scalar(dec2[:, :], dec[:, :], 7, None, ALU.logical_shift_right))
                    nc.vector.tensor_copy(node_hi[:, q], dec2[:, :]).then_inc(chain2, 1)
                    dve.wait_ge(chain2, ep * N2 + N2 + 4)
                    assert k + 1 == N2 + 4, k

        oh_ready = sem("oh_ready")
        same_ready = sem("same_ready")
        AHEAD = 2 * PAIRS
        loT_ps = sem("loT_ps")
        loT_sb = sem("loT_sb")
        rows = sem("rows")
        rows_free = sem("rows_free")
        hist_sb = sem("hist_sb")
        hist_up = sem("hist_up")
        base_ready = sem("base_ready")
        base_free = sem("base_free")
        ranked = sem("ranked")
        rchain = sem("rchain")
        seg_counts = sem("seg_counts")
        seg_sums = sem("seg_sums")
        place_chain = sem("place_chain")
        page_ready = sem("page_ready")
        page_free = sem("page_free")
        lstored = sem("lstored")
        rstored = sem("rstored")
        topped = sem("topped")
        last_steps = sem("last_steps")
        with nc.Block() as block:
            @block.sync
            def _(sp):
                ne = sp.value_load(n_epochs[0:1, 0:1], min_val=1, max_val=EPOCHS)
                with sp.Fori(0, ne) as ep:
                    sp.wait_ge(page_ready, ep + 1)
                    sp.dma_start(lists[bass.ds(ep, 1)].squeeze(0), page[:, :]).then_inc(lstored, 16)
                    sp.wait_ge(lstored, 16 * ep + 16)
                    sp.sem_inc(page_free, 1)
                sp.wait_ge(ranked, 1)
                sp.dma_start(lists[0], page[:, :]).then_inc(rstored, 16)
                sp.wait_ge(ranked, 2)
                sp.dma_start(counts_out, n_epochs[:, :]).then_inc(rstored, 16)
                sp.wait_ge(rstored, 32)

            @block.gpsimd
            def _(pool):
                pool.wait_ge(topped, 1)
                nc.gpsimd.partition_all_reduce(top_rank[:, 1:2], top_rank[:, 0:1], P,
                                               bass.bass_isa.ReduceOp.max).then_inc(topped, 1)

            @block.tensor
            def _(pe):
                n = pe.value_load(n_epochs[0:1, 1:2], min_val=1, max_val=EPOCHS * BPE // QB)
                pe.wait_ge(seg_counts, 1)
                nc.tensor.matmul(ps_base[:, 0, 0, 0:SEGS], later[:, :], per_seg_b[:, :], start=True, stop=True)
                nc.tensor.matmul(ps_base[:, 0, 1, 0:SEGS], all_ones[:, :], per_seg_b[:, :], start=True,
                                 stop=True).then_inc(seg_sums, 1)
                pe.sem_inc(hist_up, AHEAD)
                nc.tensor.matmul(ps_hist[:, 0:HI], zeros[:, :], zeros[:, 0:HI], start=True, stop=False,
                                 skip_group_check=True).then_inc(hist_up, 1)

                def transposed(b, h):
                    if h == 0:
                        for j in range(PAIRS):
                            nc.tensor.matmul(ps_first[:, j], oh_lo[:, b, :, 2 * j], oh_hi[:, b, :, 2 * j], start=True,
                                             stop=True)
                    for k in range(HALF):
                        mm = nc.tensor.transpose(ps_loT[:, k], oh_lo[:, b, :, h * HALF + k], ident[:, :])
                    mm.then_inc(loT_ps, 1)

                def row(b, q, k):
                    nc.tensor.matmul(ps_row[:, q, k], lo8[:, b, k:k + 1].to_broadcast([P, P]), ident[:, :],
                                     start=True, stop=False)
                    return nc.tensor.matmul(ps_row[:, q, k], hi8[:, b, k:k + 1].to_broadcast([P, P]), ident_hi[:, :],
                                            start=False, stop=True)

                pe.wait_ge(oh_ready, 1)
                for h in (0, 1):
                    if h:
                        pe.wait_ge(loT_sb, 1)
                    transposed(0, h)
                for k in range(BATCH):
                    mm = row(0, 0, k)
                mm.then_inc(rows, 1)
                with pe.Fori(0, n) as i:
                    for b in range(QB):
                        g = QB * i + b
                        u = b % 2
                        pe.wait_ge(oh_ready, g + 2)
                        pe.wait_ge(rows_free, g + 2)
                        pe.wait_ge(base_free, g + 1)
                        for k in range(BATCH):
                            if k % HALF == 0:
                                pe.wait_ge(loT_sb, 2 * g + 2 + k // HALF)
                                transposed((b + 1) % QB, k // HALF)
                            nm = row((b + 1) % QB, 1 - u, k)
                            if k == BATCH - 1:
                                nm.then_inc(rows, 1)
                            j = k // 2
                            if k % 2 == 0:
                                pe.wait_ge(hist_sb, g * PAIRS + j + 1)
                            nc.tensor.matmul(ps_base[:, u, k], loT[:, u, k], hist[:, j % 2], start=(k == 0), stop=False,
                                             skip_group_check=True)
                            mm = nc.tensor.matmul(ps_hist[:, 0:HI], oh_lo[:, b, :, k], oh_hi[:, b, :, k], start=False,
                                                  stop=False, skip_group_check=True)
                            if k % 2:
                                mm.then_inc(hist_up, 1)
                                nc.tensor.matmul(ps_base[:, u, k], loTb[:, u, j], first[:, u, j], start=False, stop=False,
                                                 skip_group_check=True)
                        pe.wait_ge(same_ready, g + 1)
                        for k in range(BATCH):
                            mm = nc.tensor.matmul(ps_base[:, u, k], same[:, u, k], ones[:, :], start=False, stop=True,
                                                  skip_group_check=True)
                        mm.then_inc(base_ready, 1)

            @block.scalar
            def _(act):
                n = act.value_load(n_epochs[0:1, 1:2], min_val=1, max_val=EPOCHS * BPE // QB)

                def transposed_copy(q, h):
                    half = slice(h * HALF, (h + 1) * HALF)
                    nc.scalar.copy(loT[:, q, half], ps_loT)

                def second_copy(q, h):
                    if h == 0:
                        nc.scalar.copy(first[:, q], ps_first)
                    nc.scalar.copy(loTb[:, q, h * HALF // 2:(h + 1) * HALF // 2],
                                   ps_loT.rearrange("p (j two) e -> p j two e", two=2)[:, :, 1]).then_inc(loT_sb, 1)

                for h in (0, 1):
                    act.wait_ge(loT_ps, h + 1)
                    transposed_copy(0, h)
                    second_copy(0, h)
                with act.Fori(0, n) as i:
                    for b in range(QB):
                        g = QB * i + b
                        for j in range(PAIRS):
                            act.wait_ge(hist_up, g * PAIRS + j + 1 + AHEAD)
                            nc.scalar.copy(hist[:, j % 2], ps_hist[:, 0:HI]).then_inc(hist_sb, 1)
                            h = j // 2
                            if j % 2 == 0:
                                act.wait_ge(loT_ps, 2 * (g + 1) + h + 1)
                                transposed_copy(1 - b % 2, h)
                            else:
                                second_copy(1 - b % 2, h)

            @block.vector
            def _(dve):
                n = dve.value_load(n_epochs[0:1, 1:2], min_val=1, max_val=EPOCHS * BPE // QB)
                dve.sem_inc(rows_free, 2)
                dve.sem_inc(page_free, 1)

                first_steps = [0]

                def link0(ins):
                    first_steps[0] += 1
                    ins.then_inc(place_chain, 1)
                    dve.wait_ge(place_chain, first_steps[0])
                valid0, pos, low, high = (slotf[:, k * COLS:(k + 1) * COLS] for k in range(4))
                tt, ts = nc.vector.tensor_tensor, nc.vector.tensor_scalar

                def segs(ap):
                    return ap.rearrange("p (s c) -> p s c", s=SEGS)
                link0(ts(valid0, node_d[:, 0:COLS], float(NODES), None, ALU.is_lt))
                link0(nc.vector.tensor_reduce(per_seg[:, :], segs(valid0), AX.X, ALU.add))
                link0(nc.vector.tensor_copy(per_seg_b[:, :], per_seg[:, :]))
                dve.sem_inc(seg_counts, 1)
                dve.wait_ge(seg_sums, 1)
                link0(nc.vector.tensor_copy(sums[:, :, :], ps_base[:, 0, 0:2, 0:SEGS]))
                dve.sem_inc(base_free, 2)
                link0(nc.vector.tensor_reduce(start[:, 0:1], sums[:, 0], AX.X, ALU.add))
                for k in range(1, SEGS):
                    link0(tt(start[:, k:k + 1], start[:, k - 1:k], per_seg[:, k - 1:k], ALU.add))
                link0(tt(segs(pos), segs(index[:, :]), start[:, :].unsqueeze(2).to_broadcast([P, SEGS, SLOTS]), ALU.add))
                link0(nc.vector.tensor_copy(high.bitcast(I32), pos))
                link0(ts(low.bitcast(I32), high.bitcast(I32), P - 1, None, ALU.bitwise_and))
                link0(ts(high.bitcast(I32), high.bitcast(I32), 7, None, ALU.logical_shift_right))
                link0(ts(pos, low.bitcast(I32), float(COLS), None, ALU.mult))
                link0(nc.vector.tensor_copy(low, high.bitcast(I32)))
                link0(tt(pos, pos, low, ALU.add))
                link0(ts(valid0, valid0, -float(NOWHERE), float(NOWHERE), ALU.mult, ALU.add))
                link0(tt(pos, pos, valid0, ALU.add))
                link0(nc.vector.tensor_copy(place[:, 0:COLS], pos))
                link0(nc.vector.tensor_reduce(total[:, :], sums[:, 1], AX.X, ALU.add))
                link0(ts(total[:, :], total[:, :], float(P * TURN_COLS - 1), float(P * TURN_COLS), ALU.add, ALU.max))
                link0(nc.vector.tensor_copy(total_i[:, :], total[:, :]))
                link0(nc.vector.memset(n_epochs[:, 4:COUNTS], COLS // TURN_COLS))
                link0(ts(n_epochs[:, 3:4], total_i[:, :], (P * TURN_COLS).bit_length() - 1, None, ALU.logical_shift_right))
                NR = 4 * QB

                def onehots(g, b):
                    c = bass.ds(g * BATCH, BATCH)
                    nc.vector.tensor_tensor(oh_lo[:, b], node_lo[:, c].unsqueeze(1).to_broadcast([P, P, BATCH]),
                                            bins[:, :, :], ALU.is_equal)
                    nc.vector.tensor_copy(lo8[:, b], node_lo[:, c])
                    nc.vector.tensor_copy(hi8[:, b], node_hi[:, c])
                    nc.vector.tensor_tensor(oh_hi[:, b], node_hi[:, c].unsqueeze(1).to_broadcast([P, HI, BATCH]),
                                            bins[:, 0:HI], ALU.is_equal).then_inc(oh_ready, 1)

                onehots(0, 0)
                onehots(1, 1)
                with dve.Fori(0, n) as i:
                    for b in range(QB):
                        g = QB * i + b
                        u = b % 2
                        k = b * 4

                        def link(ins):
                            nonlocal k
                            k += 1
                            ins.then_inc(rchain, 1)
                            dve.wait_ge(rchain, i * NR + k)
                        c = bass.ds(g * BATCH, BATCH)
                        dve.wait_ge(rows, g + 1)
                        link(nc.vector.tensor_tensor(same[:, u], ps_row[:, u],
                                                     node_d[:, c].unsqueeze(2).to_broadcast([P, BATCH, P]), ALU.is_equal))
                        dve.sem_inc(rows_free, 1)
                        link(nc.vector.tensor_tensor(same[:, u], same[:, u],
                                                     later[:, :].unsqueeze(1).to_broadcast([P, BATCH, P]), ALU.mult))
                        dve.sem_inc(same_ready, 1)
                        dve.wait_ge(hist_up, g * PAIRS + AHEAD - PAIRS + 1)
                        onehots(g + 2, (b + 2) % QB)
                        dve.wait_ge(base_ready, g + 1)
                        link(nc.vector.tensor_tensor(masked[:, u], ps_base[:, u],
                                                     oh_hi[:, b].rearrange("p h k -> p k h"), ALU.mult))
                        dve.sem_inc(base_free, 1)
                        link(nc.vector.tensor_reduce(rank[:, c], masked[:, u], AX.X, ALU.add))
                valid = node_d[:, 0:LIST]
                seq = [0]

                def link(ins):
                    seq[0] += 1
                    ins.then_inc(last_steps, 1)
                    dve.wait_ge(last_steps, seq[0])
                link(nc.vector.scalar_tensor_tensor(out=slotf[:, :], in0=node_d[:, 0:LIST], scalar=float(K), in1=rank[:, :],
                                                    op0=ALU.mult, op1=ALU.add))
                link(nc.vector.tensor_scalar(valid, node_d[:, 0:LIST], float(NODES), None, ALU.is_lt))
                link(nc.vector.tensor_tensor(valid, valid, rank[:, :], ALU.mult))
                link(nc.vector.tensor_reduce(top_rank[:, 0:1], valid, AX.X, ALU.max))
                dve.sem_inc(topped, 1)
                c0 = slice(0, COLS)
                link(nc.vector.tensor_copy(fields(records[:, 0:COLS * RECORD], 0, I32), node_s[:, c0]))
                link(nc.vector.tensor_copy(fields(records[:, 0:COLS * RECORD], 1), slotf[:, c0]))
                link(nc.vector.tensor_copy(fields(records[:, 0:COLS * RECORD], 2), rank[:, c0]))
                ne = dve.value_load(n_epochs[0:1, 0:1], min_val=1, max_val=EPOCHS)
                with dve.Fori(0, ne) as ep:
                    dve.wait_ge(page_free, ep + 1)
                    dve.sem_inc(carrier, 1)
                    q = bass.ds(ep * COLS, COLS)
                    nc.vector.tensor_copy(fields(page[:, :], 0, I32), node_s[:, q])
                    nc.vector.tensor_copy(fields(page[:, :], 1), slotf[:, q])
                    nc.vector.tensor_copy(fields(page[:, :], 2), rank[:, q]).then_inc(page_ready, 1)
                dve.wait_ge(page_free, ne + 1)
                dve.sem_inc(carrier, 1)
                link(nc.vector.memset(page[:, :], 0.0))
                link(nc.vector.memset(fields(page[:, :], 2), NO_RANK))
                dve.sem_inc(ranked, 1)
                dve.wait_ge(topped, 2)
                link(nc.vector.tensor_copy(rounds_i[:, 0:1], top_rank[:, 1:2]))
                link(nc.vector.tensor_scalar(rounds_i[:, 1:2], rounds_i[:, 0:1], 4, None, ALU.logical_shift_right))
                link(nc.vector.tensor_scalar(n_epochs[:, 2:3], rounds_i[:, 1:2], 1.0, None, ALU.add))
                dve.sem_inc(ranked, 1)
        clear(nc, sems)

TILES = NODES // P
UN = 4
SHIFT = (0,3,6,9)
DIM = 128
HEADS = 8
NB = 64
EPS = 1e-5
NEG = 1e9
SLOPE = 0.01
GH = 4
GE = 4
GAT = GH * GE
ROW = GAT + GH
COLS24 = GAT + 2 * GH


def node_layers(nc, w, x_all, hg_all, xT_dram, table, records, place, lists, wdram):
    with ExitStack() as ctx:
        def sb(name, shape, dt=F32):
            return ctx.enter_context(nc.sbuf_tensor("n_" + name, shape, dt))

        def ps(name, shape, dt=F32):
            return ctx.enter_context(nc.psum_tensor("n_" + name, shape, dt))

        def sem(name):
            sems.append(ctx.enter_context(nc.semaphore("n_" + name)))
            return sems[-1]
        sems = []

        M = sb("M", [P, HEADS, DIM])
        kw = sb("kw", [P, 32])
        qw = sb("qw", [P, 32])
        cb = sb("cb", [1, DIM])
        head_c = sb("head_c", [1, HEADS])
        wiT = sb("wiT", [P, HID])
        bi = sb("bi", [P, 2])
        woT = sb("woT", [P, 2, DIM])
        bo = sb("bo", [1, DIM])
        gW = sb("gW", [P, DIM])
        gb = sb("gb", [1, DIM])
        w24 = sb("w24", [P, COLS24])
        ident = sb("ident", [P, P])
        ones = sb("ones", [1, P])
        half = sb("half", [P, UN])
        route = sb("route", [1, TILES], I32)
        adj = sb("adj", [P, TILES, NB])
        BD = sb("BD", [P, TILES, P])
        deg = sb("deg", [P, TILES])
        dinv = sb("dinv", [P, TILES])
        A = [ps(f"A{u}", [P, 512]) for u in range(UN)]
        Z = [ps(f"Z{u}", [P, 512]) for u in range(UN)]

        with ExitStack() as tctx:
            def tsb(name, shape, dt=F32):
                return tctx.enter_context(nc.sbuf_tensor("s_" + name, shape, dt))

            def tsem(name):
                tsems.append(tctx.enter_context(nc.semaphore("s_" + name)))
                return tsems[-1]
            tsems = []
            fcT = tsb("fcT", [P, HEADS, DIM])
            fp = tsb("fp", [P, HEADS, DIM])
            fcb = tsb("fcb", [P, HEADS])
            qk = tsb("qk", [P, 4])
            small = tsb("small", [1, 2 * DIM])
            att = tsb("att", [P, 2, GAT])
            attw = tsb("attw", [P, 2, GAT])
            pos = tsb("pos", [P, TILES])
            pos_mask = tsb("pos_mask", [P, TILES])
            ld = tsem("ld")
            ldb = tsem("ldb")
            lda = tsem("lda")
            chain = tsem("chain")
            consts = tsem("consts")
            summed = tsem("summed")
            folded = tsem("folded")
            powed = tsem("powed")
            k = [0]
            NLD = 18

            with nc.Block() as block:
                @block.sync
                def _(sp):
                    for dst, src in (
                        (fcT[:, :, :], w["fcT"].rearrange("(h c) d -> c h d", c=DIM)),
                        (fp[:, :, :], w["fp"].rearrange("(h c) d -> c h d", c=DIM)),
                        (fcb[:, :], w["fcbT"]),
                        (qk[:, 0:1], w["q_w"]), (qk[:, 1:2], w["k_w"]),
                        (small[:, 0:DIM], w["fp_b"].unsqueeze(0)),
                        (small[:, DIM:DIM + 1], w["q_b"].unsqueeze(0)),
                        (small[:, DIM + 1:DIM + 2], w["k_b"].unsqueeze(0)),
                        (wiT[:, :], w["WiT"]), (bi[:, :], w["biT"]),
                        (woT[:, :, :], w["WoT"].rearrange("(c p) o -> p c o", p=P)),
                        (bo[:, :], w["bo"].unsqueeze(0)),
                        (gW[:, :], w["gWT"]), (gb[:, :], w["gb"].unsqueeze(0)),
                        (w24[:, 0:GAT], w["Wgat"]),
                        (att[:, 0], w["att_src"].partition_broadcast(P)),
                        (att[:, 1], w["att_dst"].partition_broadcast(P)),
                        (route[:, :], w["route"].unsqueeze(0)),
                    ):
                        sp.dma_start(dst, src).then_inc(ld, 16)
                    sp.wait_ge(consts, 8)
                    for b in (0, 1):
                        sp.dma_start(BD[b * NB:(b + 1) * NB, :, b * NB:(b + 1) * NB],
                                     w["adjT"].rearrange("(t b) m i -> b m t i", b=2)[b]).then_inc(ldb, 16)
                    sp.dma_start(x_all[:, :, :], w["x"].rearrange("(t b) n d -> (b n) t d", b=2)).then_inc(ldb, 16)
                    sp.wait_ge(ldb, 48)

                @block.scalar
                def _(act):
                    act.dma_start(adj[:, :, :], w["adj"].rearrange("(t b) i j -> (b i) t j", b=2)).then_inc(lda, 16)

                @block.gpsimd
                def _(pool):
                    nc.gpsimd.memset(ident[:, :], 0.0).then_inc(consts, 1)
                    nc.gpsimd.memset(ones[:, :], 1.0).then_inc(consts, 1)
                    nc.gpsimd.memset(half[:, :], -0.5).then_inc(consts, 1)
                    nc.gpsimd.memset(pos[:, :], -0.5).then_inc(consts, 1)
                    nc.gpsimd.memset(kw[:, :], 0.0).then_inc(consts, 1)
                    nc.gpsimd.memset(qw[:, :], 0.0).then_inc(consts, 1)
                    nc.gpsimd.memset(BD[:, :, :], 0.0).then_inc(consts, 1)
                    pool.wait_ge(consts, 7)
                    nc.gpsimd.affine_select(out=ident[:, :], in_=ident[:, :], compare_op=ALU.not_equal, fill=1.0,
                                            base=0, pattern=[[-1, P]], channel_multiplier=1).then_inc(consts, 1)
                    pool.wait_ge(summed, 1)
                    nc.gpsimd.tensor_tensor(dinv[:, :], deg[:, :], pos[:, :], ALU.pow).then_inc(powed, 1)

                @block.vector
                def _(dve):
                    def link(ins):
                        k[0] += 1
                        ins.then_inc(chain, 1)
                        dve.wait_ge(chain, k[0])
                    dve.wait_ge(ld, 16 * NLD)
                    dve.wait_ge(consts, 8)
                    link(nc.vector.tensor_tensor(qk[:, 2:3], qk[:, 0:1], qk[:, 1:2], ALU.add))
                    link(nc.vector.tensor_tensor(small[:, DIM + 2:DIM + 3], small[:, DIM:DIM + 1],
                                                 small[:, DIM + 1:DIM + 2], ALU.add))
                    for s in (0, 1):
                        link(nc.vector.tensor_tensor(attw[:, s], w24[:, 0:GAT], att[:, s], ALU.mult))
                        link(nc.vector.tensor_reduce(w24[:, GAT + s * GH:GAT + (s + 1) * GH],
                                                     attw[:, s].rearrange("p (h e) -> p h e", h=GH), AX.X, ALU.add))
                    dve.sem_inc(folded, 1)
                    dve.wait_ge(lda, 16)
                    link(nc.vector.tensor_reduce(dinv[:, :], adj[:, :, :], AX.X, ALU.add))
                    link(nc.vector.tensor_scalar(deg[:, :], dinv[:, :], 1e-30, None, ALU.max))
                    link(nc.vector.tensor_scalar(pos_mask[:, :], dinv[:, :], 0.0, None, ALU.not_equal))
                    dve.sem_inc(summed, 1)
                    dve.wait_ge(powed, 1)
                    link(nc.vector.tensor_tensor(dinv[:, :], dinv[:, :], pos_mask[:, :], ALU.mult))
                    link(nc.vector.tensor_scalar(adj[:, :, :], adj[:, :, :], 1.0, NEG, ALU.subtract, ALU.mult))
                    dve.wait_ge(folded, 2)
                    link(nc.vector.tensor_copy(M[:, 0:4], A[0][:, :].rearrange("p (h d) -> p h d", h=4)))
                    link(nc.vector.tensor_copy(M[:, 4:8], A[1][:, :].rearrange("p (h d) -> p h d", h=4)))
                    qkp = Z[0][:, 0:16].rearrange("p (h s) -> p h s", s=2)
                    link(nc.vector.tensor_copy(qw[:, 0:HEADS], qkp[:, :, 0]))
                    link(nc.vector.tensor_copy(kw[:, 0:HEADS], qkp[:, :, 1]))
                    link(nc.vector.tensor_tensor(cb[:, :], Z[1][0:1, 0:DIM], small[:, 0:DIM], ALU.add))
                    link(nc.vector.tensor_scalar(head_c[:, :], Z[1][0:1, DIM:DIM + HEADS], small[:, DIM + 2:DIM + 3],
                                                 None, ALU.add))

                @block.tensor
                def _(pe):
                    pe.wait_ge(folded, 1)
                    for h in range(HEADS):
                        nc.tensor.matmul(A[h // 4][:, (h % 4) * DIM:(h % 4 + 1) * DIM], fcT[:, h], fp[:, h],
                                         start=True, stop=True)
                        nc.tensor.matmul(Z[0][:, 2 * h:2 * h + 2], fcT[:, h], qk[:, 0:2], start=True, stop=True)
                    for h in range(HEADS):
                        nc.tensor.matmul(Z[1][0:1, 0:DIM], fcb[:, h:h + 1], fp[:, h], start=(h == 0),
                                         stop=(h == HEADS - 1))
                    nc.tensor.matmul(Z[1][0:1, DIM:DIM + HEADS], qk[:, 2:3], fcb[:, :], start=True,
                                     stop=True).then_inc(folded, 1)

            clear(nc, tsems)

        f = sb("f", [P, UN, DIM])
        fT = sb("fT", [P, UN, P])
        stats = sb("stats", [P, UN, 6])
        mv = sb("mv", [P, UN, 2])
        ve = sb("ve", [P, UN])
        rstd = sb("rstd", [P, UN])
        delta = sb("delta", [64, HEADS])
        kd = sb("kd", [P, UN, HEADS, NB])
        sel = sb("sel", [P, UN, P])
        z = sb("z", [P, UN, HEADS, NB])
        z2 = sb("z2", [P, UN, HEADS, NB])
        zmax = sb("zmax", [P, UN, HEADS])
        zsum = sb("zsum", [P, UN, HEADS])
        atT = sb("atT", [P, UN, HEADS // 2, P])
        f_swapped = sb("f_swapped", [P, UN, DIM])
        UT = sb("UT", [P, UN, HEADS, 2, NB])
        s_ = sb("s_", [P, UN, DIM])
        h1 = sb("h1", [P, UN, 2, P])
        h2 = sb("h2", [P, UN, 2, P])
        wbuf = sb("wbuf", [P, UN, WROW])
        dcol = sb("dcol", [P, UN])
        srow = sb("srow", [1, UN, P])
        prime = sb("prime", [1, UN, TILES], I32)
        prime2 = sb("prime2", [1, UN, TILES], I32)
        chunk = sb("chunk", [P, UN, CHUNK * RECORD])
        chunk_place = sb("chunk_place", [P, UN, CHUNK], I32)
        list0 = lists.rearrange("e p (c k) -> (e p c) k", k=RECORD)[0:P * COLS]
        VT = sb("VT", [P, UN, P])
        NCH = 21
        LN0, SM_A, SM_B, GATE, LN1, ADD_OUT, LN2, ADD_GNN, LN3 = 0, 2, 5, 7, 10, 12, 13, 17, 19
        TURNS = TILES // UN

        def per_tile(names):
            return {n: [sem(f"{n}{u}") for u in range(UN)] for n in names}

        S = per_tile((
            "dve", "var", "rstd", "f", "swapped", "fT_ps", "fT", "xT", "kq", "q_in_sel", "kd", "scores", "shifted", "exp",
            "attn", "attn_T_ps", "attn_T", "U_ps", "UT", "y", "gate_in", "gate", "H1", "h1", "L1", "h2", "L2", "h3",
            "weights", "weights_used", "chunk", "moved", "ffn_out", "V_ps", "V", "gnn", "hg", "hg_out"))
        init = sem("init")
        consts2 = sem("consts2")
        carrier = sem("carrier")
        stored = sem("stored")

        STAGES = ("stats0", "norm0", "transpose0", "kq", "scores", "softmax", "normalise", "attn_T", "U", "y", "gate",
                  "norm1", "transpose1", "H1", "L1", "L2", "ffn_out", "norm2", "V", "gnn", "add_gnn",
                  "norm3", "transpose2", "hg")
        N = len(STAGES)

        def in_order(eng, stages):
            def step(k, i, u, turn_ok):
                name = STAGES[k % N]
                if name in stages and turn_ok(k // N):
                    stages[name](i + k // N, u)
            for k in range(-max(SHIFT), 0):
                for u in range(UN):
                    if k + SHIFT[u] >= 0:
                        step(k + SHIFT[u], 0, u, lambda t: True)
            with eng.Fori(0, TURNS - 1) as i:
                for k in range(N):
                    for u in range(UN):
                        step(k + SHIFT[u], i, u, lambda t: True)
            for k in range(N):
                for u in range(UN):
                    step(k + SHIFT[u], TURNS - 1, u, lambda t: t == 0)

        def heads_of(u, parity):
            return UT[:, u].rearrange("p (m t) b j -> p t b m j", t=2)[:, parity]

        def tile_of(ap, i, u):
            return ap[:, bass.ds(UN * i + u, 1)]

        with nc.Block() as block:
            @block.sync
            def _(sp):
                for u in range(UN):
                    sp.dma_start(prime[:, u], w["route"].unsqueeze(0)).then_inc(S["xT"][u], 16)

                def load_weights(i, u):
                    sp.wait_ge(S["weights_used"][u], i + 1)
                    e = sp.value_load(route[0:1, bass.ds(UN * i + u, 1)], min_val=0, max_val=EXP0 - 1)
                    sp.dma_start(wbuf[:, u, :], wdram[bass.ds(e, 1)].squeeze(0)).then_inc(S["weights"][u], 16)

                def store_xT(i, u):
                    sp.wait_ge(S["fT"][u], 3 * i + 3)
                    sp.dma_start(xT_dram[:, bass.ds((UN * i + u) * P, P)], fT[:, u]).then_inc(S["xT"][u], 16)

                def swap_graphs(i, u):
                    sp.wait_ge(S["f"][u], 4 * i + 1)
                    for b in (0, 1):
                        sp.dma_start(f_swapped[(1 - b) * NB:(2 - b) * NB, u], f[b * NB:(b + 1) * NB, u]
                                     ).then_inc(S["swapped"][u], 16)
                in_order(sp, {"norm0": swap_graphs, "scores": load_weights, "transpose2": store_xT})
                for u in range(UN):
                    sp.wait_ge(S["xT"][u], 16 * TURNS + 16)
                    sp.wait_ge(S["hg_out"][u], TURNS)
                sp.dma_start(table.rearrange("(t p) c -> p t c", p=P), hg_all[:, :, 0:ROW]).then_inc(stored, 16)
                sp.wait_ge(stored, 16)

            @block.gpsimd
            def _(pool):
                nc.gpsimd.memset(kd[:, :, :, :], 0.0).then_inc(consts2, 1)
                nc.gpsimd.memset(sel[:, :, :], 0.0).then_inc(consts2, 1)
                nc.gpsimd.memset(delta[:, :], 0.0).then_inc(consts2, 1)
                pool.wait_ge(consts2, 3)
                for b in (0, 1):
                    nc.gpsimd.affine_select(out=delta[32 * b:32 * b + 32, :], in_=delta[32 * b:32 * b + 32, :],
                                            compare_op=ALU.not_equal, fill=1.0, base=0, pattern=[[-1, HEADS]],
                                            channel_multiplier=1).then_inc(consts2, 1)
                for u in range(UN):
                    nc.gpsimd.affine_select(out=kd[64:96, u], in_=kd[64:96, u], compare_op=ALU.not_equal, fill=1.0,
                                            base=0, pattern=[[-1, HEADS], [0, NB]],
                                            channel_multiplier=1).then_inc(consts2, 1)
                    for b in (0, 1):
                        nc.gpsimd.memset(sel[32 * b:32 * b + 32, u, b * NB:(b + 1) * NB], 1.0).then_inc(consts2, 1)
                    nc.gpsimd.memset(sel[96:97, u, :], 1.0).then_inc(consts2, 1)

                def inv_std(ln):
                    def stage(i, u):
                        pool.wait_ge(S["var"][u], 4 * i + ln + 1)
                        nc.gpsimd.tensor_tensor(rstd[:, u:u + 1], ve[:, u:u + 1], half[:, u:u + 1],
                                                ALU.pow).then_inc(S["rstd"][u], 1)
                    return stage

                for u in range(UN):
                    pool.dma_start(prime2[:, u], w["route"].unsqueeze(0)).then_inc(S["moved"][u], 16)

                def next_chunk(i, u):
                    pool.wait_ge(S["moved"][u], 16 * CHUNK * i + 16)
                    pool.sem_inc(carrier, 1)
                    c = (UN * i + u) * CHUNK
                    nc.gpsimd.tensor_copy(chunk_place[:, u], place[:, bass.ds(c, CHUNK)]).then_inc(S["chunk"][u], 1)
                    nc.gpsimd.tensor_copy(chunk[:, u].bitcast(I32),
                                          records[:, bass.ds(c * RECORD, CHUNK * RECORD)].bitcast(I32)
                                          ).then_inc(S["chunk"][u], 1)

                def move(k):
                    def stage(i, u):
                        pool.wait_ge(S["chunk"][u], 2 * i + 2)
                        pool.sem_inc(carrier, 1)
                        nc.gpsimd.indirect_dma_start(
                            out=list0, out_offset=bass.IndirectOffsetOnAxis(ap=chunk_place[:, u, k:k + 1].bitcast(U32), axis=0),
                            in_=chunk[:, u, k * RECORD:(k + 1) * RECORD], in_offset=None, bounds_check=P * COLS - 1,
                            oob_is_err=False).then_inc(S["moved"][u], 16)
                    return stage
                moves = ("kq", "scores", "softmax", "normalise", "attn_T", "U")
                assert len(moves) == CHUNK
                in_order(pool, {"stats0": inv_std(0), "norm0": next_chunk, "gate": inv_std(1), "ffn_out": inv_std(2),
                                "add_gnn": inv_std(3), **{name: move(k) for k, name in enumerate(moves)}})
                for u in range(UN):
                    pool.wait_ge(S["moved"][u], 16 * CHUNK * TURNS + 16)

            @block.vector
            def _(dve):
                dve.wait_ge(consts2, 5 + 4 * UN)
                for u in range(UN):
                    nc.vector.tensor_copy(kd[96:97, u], head_c[:, :].unsqueeze(2).to_broadcast([1, HEADS, NB])
                                          ).then_inc(init, 1)
                dve.wait_ge(init, UN)

                def linker(i, u, before):
                    n = before

                    def link(ins):
                        nonlocal n
                        n += 1
                        ins.then_inc(S["dve"][u], 1)
                        dve.wait_ge(S["dve"][u], i * NCH + n)
                    return link

                def bc(ap):
                    return ap.unsqueeze(2).to_broadcast([P, HEADS, NB])

                def stats_of(i, u, before):
                    link = linker(i, u, before)
                    xt = tile_of(x_all, i, u).squeeze(1)
                    dve.sem_inc(carrier, 1)
                    link(nc.vector.bn_stats(stats[:, u], xt))
                    dve.sem_inc(carrier, 1)
                    link(nc.vector.bn_aggr(mv[:, u], stats[:, u]))
                    nc.vector.tensor_scalar(ve[:, u:u + 1], mv[:, u, 1:2], EPS, None, ALU.add).then_inc(S["var"][u], 1)

                def norm(ln):
                    def stage(i, u):
                        xt = tile_of(x_all, i, u).squeeze(1)
                        dve.wait_ge(S["rstd"][u], 4 * i + ln + 1)
                        r = rstd[:, u:u + 1]
                        if ln == 2:
                            link = linker(i, u, LN2 + 2)
                            link(nc.vector.tensor_copy(dcol[:, u:u + 1], tile_of(dinv, i, u)))
                            link(nc.vector.tensor_tensor(ve[:, u:u + 1], r, dcol[:, u:u + 1], ALU.mult))
                            r = ve[:, u:u + 1]
                        nc.vector.tensor_scalar(f[:, u], xt, mv[:, u, 0:1], r, ALU.subtract,
                                                ALU.mult).then_inc(S["f"][u], 1)
                    return stage

                def spread_keys(i, u):
                    dve.wait_ge(S["kq"][u], i + 1)
                    nc.vector.tensor_tensor(kd[0:64, u], A[u][0:64, 256:256 + NB].unsqueeze(1).to_broadcast([64, HEADS, NB]),
                                            delta[:, :].unsqueeze(2).to_broadcast([64, HEADS, NB]),
                                            ALU.mult).then_inc(S["kd"][u], 1)

                def softmax_shift(i, u):
                    link = linker(i, u, SM_A)
                    dve.wait_ge(S["scores"][u], i + 1)
                    m = tile_of(adj, i, u).to_broadcast([P, HEADS, NB])
                    link(nc.vector.tensor_tensor(z[:, u], Z[u][:, :].rearrange("p (h j) -> p h j", h=HEADS), m, ALU.add))
                    link(nc.vector.scalar_tensor_tensor(out=z2[:, u], in0=z[:, u], scalar=SLOPE, in1=z[:, u],
                                                        op0=ALU.mult, op1=ALU.max))
                    link(nc.vector.tensor_reduce(zmax[:, u], z2[:, u], AX.X, ALU.max))
                    nc.vector.tensor_tensor(z[:, u], z2[:, u], bc(zmax[:, u]), ALU.subtract).then_inc(S["shifted"][u], 1)

                def softmax_divide(i, u):
                    link = linker(i, u, SM_B)
                    dve.wait_ge(S["exp"][u], i + 1)
                    link(nc.vector.tensor_reduce(zsum[:, u], z2[:, u], AX.X, ALU.add))
                    link(nc.vector.reciprocal(zsum[:, u], zsum[:, u]))
                    nc.vector.tensor_tensor(z[:, u], z2[:, u], bc(zsum[:, u]), ALU.mult).then_inc(S["attn"][u], 1)

                def copy_U1(i, u):
                    dve.wait_ge(S["U_ps"][u], i + 1)
                    nc.vector.tensor_copy(heads_of(u, 1), A[u][:, :].rearrange("p (b m j) -> p b m j", b=2, j=NB)
                                          ).then_inc(S["UT"][u], 1)

                def gate_in(i, u):
                    dve.wait_ge(S["y"][u], i + 1)
                    nc.vector.tensor_tensor(s_[:, u], A[u][:, 0:DIM], f[:, u], ALU.add).then_inc(S["gate_in"][u], 1)

                def gate_add(i, u):
                    link = linker(i, u, GATE)
                    xt = tile_of(x_all, i, u).squeeze(1)
                    dve.wait_ge(S["gate"][u], i + 1)
                    link(nc.vector.tensor_scalar(s_[:, u], s_[:, u], 1.0, None, ALU.add))
                    link(nc.vector.reciprocal(s_[:, u], s_[:, u]))
                    link(nc.vector.tensor_tensor(xt, xt, s_[:, u], ALU.add))
                    stats_of(i, u, LN1)

                def ffn_add(i, u):
                    link = linker(i, u, ADD_OUT)
                    xt = tile_of(x_all, i, u).squeeze(1)
                    dve.wait_ge(S["ffn_out"][u], i + 1)
                    link(nc.vector.tensor_tensor(xt, xt, A[u][:, 0:DIM], ALU.add))
                    stats_of(i, u, LN2)

                def gnn_add(i, u):
                    link = linker(i, u, ADD_GNN)
                    xt = tile_of(x_all, i, u).squeeze(1)
                    dve.wait_ge(S["gnn"][u], i + 1)
                    link(nc.vector.tensor_scalar(s_[:, u], A[u][:, 384:512], dcol[:, u:u + 1], 0.0, ALU.mult, ALU.max))
                    link(nc.vector.tensor_tensor(xt, xt, s_[:, u], ALU.add))
                    stats_of(i, u, LN3)

                def keep_hg(i, u):
                    dve.wait_ge(S["hg"][u], i + 1)
                    nc.vector.tensor_copy(tile_of(hg_all, i, u).squeeze(1), A[u][:, 0:COLS24]).then_inc(S["hg_out"][u], 1)

                in_order(dve, {
                    "stats0": lambda i, u: stats_of(i, u, LN0), "norm0": norm(0), "kq": spread_keys,
                    "softmax": softmax_shift, "normalise": softmax_divide, "U": copy_U1, "y": gate_in, "gate": gate_add,
                    "norm1": norm(1), "ffn_out": ffn_add,
                    "norm2": norm(2), "add_gnn": gnn_add, "norm3": norm(3),
                    "hg": keep_hg})

            @block.scalar
            def _(act):
                def copy_fT(k):
                    def stage(i, u):
                        act.wait_ge(S["fT_ps"][u], 3 * i + k + 1)
                        if k == 0:
                            act.wait_ge(S["xT"][u], 16 * i + 16)
                        nc.scalar.copy(fT[:, u], A[u][:, 0:P]).then_inc(S["fT"][u], 1)
                    return stage

                def copy_q(i, u):
                    act.wait_ge(S["kq"][u], i + 1)
                    nc.scalar.copy(sel[64:96, u], A[u][64:96, 256:384]).then_inc(S["q_in_sel"][u], 1)

                def exp(i, u):
                    act.wait_ge(S["shifted"][u], i + 1)
                    nc.scalar.activation(z2[:, u], z[:, u], ACT.Exp).then_inc(S["exp"][u], 1)

                def copy_attn_T(i, u):
                    act.wait_ge(S["attn_T_ps"][u], i + 1)
                    nc.scalar.copy(atT[:, u], Z[u][:, :].rearrange("p (m e) -> p m e", e=P)).then_inc(S["attn_T"][u], 1)

                def copy_U0(i, u):
                    act.wait_ge(S["U_ps"][u], i + 1)
                    nc.scalar.copy(heads_of(u, 0), Z[u][:, :].rearrange("p (b m j) -> p b m j", b=2, j=NB)
                                   ).then_inc(S["UT"][u], 1)

                def gate(i, u):
                    act.wait_ge(S["gate_in"][u], i + 1)
                    nc.scalar.activation(s_[:, u], s_[:, u], ACT.Exp, scale=-1.0).then_inc(S["gate"][u], 1)

                def relu_in(i, u):
                    act.wait_ge(S["H1"][u], i + 1)
                    for c in (0, 1):
                        ins = nc.scalar.activation(h1[:, u, c], Z[u][:, c * P:(c + 1) * P], ACT.Relu, bias=bi[:, c:c + 1])
                    ins.then_inc(S["h1"][u], 1)

                def relu(l, src, dst, ready, done):
                    def stage(i, u):
                        act.wait_ge(S[ready][u], i + 1)
                        act.wait_ge(S["weights"][u], 16 * (i + 1))
                        for c in (0, 1):
                            q = LAYERS * 2 * HID + l * 2 + c
                            ins = nc.scalar.activation(dst[:, u, c], src[u][:, c * P:(c + 1) * P], ACT.Relu,
                                                       bias=wbuf[:, u, q:q + 1])
                        ins.then_inc(S[done][u], 1)
                    return stage

                def copy_V(i, u):
                    act.wait_ge(S["V_ps"][u], i + 1)
                    nc.scalar.copy(VT[:, u], A[u][:, 128:256])
                    nc.scalar.copy(srow[:, u], A[u][0:1, 256:384]).then_inc(S["V"][u], 1)

                in_order(act, {
                    "transpose0": copy_fT(0), "kq": copy_q, "softmax": exp, "attn_T": copy_attn_T, "U": copy_U0, "y": gate,
                    "transpose1": copy_fT(1), "H1": relu_in, "L1": relu(0, A, h2, "L1", "h2"),
                    "L2": relu(1, Z, h1, "L2", "h3"), "V": copy_V, "transpose2": copy_fT(2)})

            @block.tensor
            def _(pe):
                for u in range(UN):
                    pe.sem_inc(S["weights_used"][u], 1)
                pe.wait_ge(init, UN)
                pe.wait_ge(consts2, 5 + 4 * UN)

                def transpose(k):
                    def stage(i, u):
                        pe.wait_ge(S["f"][u], 4 * i + (1, 2, 4)[k])
                        nc.tensor.transpose(A[u][:, 0:P], f[:, u], ident[:, :]).then_inc(S["fT_ps"][u], 1)
                    return stage

                def kq(i, u):
                    pe.wait_ge(S["fT"][u], 3 * i + 1)
                    for b in (0, 1):
                        nc.tensor.matmul(A[u][32 * b:32 * b + 32, 256:256 + NB], kw[:, :],
                                         fT[:, u, b * NB:(b + 1) * NB], start=True, stop=True)
                    nc.tensor.matmul(A[u][64:96, 256:384], qw[:, :], fT[:, u], start=True, stop=True).then_inc(S["kq"][u], 1)

                def scores(i, u):
                    pe.wait_ge(S["kd"][u], i + 1)
                    pe.wait_ge(S["q_in_sel"][u], i + 1)
                    nc.tensor.matmul(Z[u][:, :], sel[:, u], kd[:, u].rearrange("p h j -> p (h j)"), start=True,
                                     stop=True).then_inc(S["scores"][u], 1)

                def attn_T(i, u):
                    pe.wait_ge(S["attn"][u], i + 1)
                    for m in range(HEADS // 2):
                        mm = nc.tensor.transpose(Z[u][:, m * P:(m + 1) * P],
                                                 z[:, u, 2 * m:2 * m + 2].rearrange("p h j -> p (h j)"), ident[:, :])
                    mm.then_inc(S["attn_T_ps"][u], 1)

                def attend(i, u):
                    pe.wait_ge(S["attn_T"][u], i + 1)
                    pe.wait_ge(S["swapped"][u], 32 * i + 32)
                    for par in (0, 1):
                        q = slice(par * NB, (par + 1) * NB)
                        for b in (0, 1):
                            src = f if par == b else f_swapped
                            mm = nc.tensor.matmul((Z, A)[par][u][:, b * 256:(b + 1) * 256], src[q, u],
                                                  atT[q, u, :, b * NB:(b + 1) * NB], start=True, stop=True)
                    mm.then_inc(S["U_ps"][u], 1)

                def project(i, u):
                    pe.wait_ge(S["UT"][u], 2 * i + 2)
                    nc.tensor.matmul(A[u][:, 0:DIM], ones[:, :], cb[:, :], start=True, stop=False)
                    for h in range(HEADS):
                        mm = nc.tensor.matmul(A[u][:, 0:DIM], UT[:, u, h].rearrange("p b j -> p (b j)"), M[:, h],
                                              start=False, stop=(h == HEADS - 1))
                    mm.then_inc(S["y"][u], 1)

                def ffn_in(i, u):
                    pe.wait_ge(S["fT"][u], 3 * i + 2)
                    for c in (0, 1):
                        mm = nc.tensor.matmul(Z[u][:, c * P:(c + 1) * P], wiT[:, c * P:(c + 1) * P], fT[:, u],
                                              start=True, stop=True)
                    mm.then_inc(S["H1"][u], 1)

                def expert(l, dst, src, ready, done):
                    def stage(i, u):
                        pe.wait_ge(S[ready][u], i + 1)
                        pe.wait_ge(S["weights"][u], 16 * (i + 1))
                        for m in (0, 1):
                            for k in (0, 1):
                                q = (l * 2 + k) * HID + m * P
                                mm = nc.tensor.matmul(dst[u][:, m * P:(m + 1) * P], wbuf[:, u, q:q + P],
                                                      src[:, u, k], start=(k == 0), stop=(k == 1))
                        mm.then_inc(S[done][u], 1)
                    return stage

                def ffn_out(i, u):
                    pe.wait_ge(S["h3"][u], i + 1)
                    pe.sem_inc(S["weights_used"][u], 1)
                    nc.tensor.matmul(A[u][:, 0:DIM], ones[:, :], bo[:, :], start=True, stop=False)
                    for c in (0, 1):
                        mm = nc.tensor.matmul(A[u][:, 0:DIM], h1[:, u, c], woT[:, c], start=False, stop=(c == 1))
                    mm.then_inc(S["ffn_out"][u], 1)

                def neighbours(i, u):
                    pe.wait_ge(S["f"][u], 4 * i + 3)
                    bd = tile_of(BD, i, u).squeeze(1)
                    nc.tensor.matmul(A[u][:, 128:256], f[:, u], bd, start=True, stop=True)
                    nc.tensor.matmul(A[u][0:1, 256:384], dcol[:, u:u + 1], bd, start=True, stop=True).then_inc(S["V_ps"][u], 1)

                def gnn(i, u):
                    pe.wait_ge(S["V"][u], i + 1)
                    nc.tensor.matmul(A[u][:, 384:512], VT[:, u], gW[:, :], start=True, stop=False)
                    nc.tensor.matmul(A[u][:, 384:512], srow[:, u], gb[:, :], start=False, stop=True).then_inc(S["gnn"][u], 1)

                def gat_features(i, u):
                    pe.wait_ge(S["fT"][u], 3 * i + 3)
                    nc.tensor.matmul(A[u][:, 0:COLS24], fT[:, u], w24[:, :], start=True, stop=True).then_inc(S["hg"][u], 1)

                in_order(pe, {
                    "transpose0": transpose(0), "kq": kq, "scores": scores, "attn_T": attn_T, "U": attend, "y": project,
                    "transpose1": transpose(1), "H1": ffn_in, "L1": expert(0, A, h1, "h1", "L1"),
                    "L2": expert(1, Z, h2, "h2", "L2"), "ffn_out": ffn_out, "V": neighbours, "gnn": gnn,
                    "transpose2": transpose(2), "hg": gat_features})
        clear(nc, sems, S["moved"])

CAP = NODES * K
OUTSIDE = float(4 * CAP)
EMPTY = -1e30
GT = 8
GROUPS = TILES // GT
NBUF = 4
GB = TURN_COLS // NBUF
MG = 512
GAT_SLOPE = 0.2


def edge_and_expert_layers(nc, w, x_all, hg_all, xT_dram, table, hist_keys, lists, counts_dram, out):
    with ExitStack() as ctx:
        def sb(name, shape, dt=F32):
            return ctx.enter_context(nc.sbuf_tensor("m_" + name, shape, dt))

        def sem(name):
            return ctx.enter_context(nc.semaphore("m_" + name))

        slots = nc.dram_tensor("m_slots", [CAP, ROW], F32).ap()
        Y = nc.dram_tensor("m_Y", [TILES, P, GE * DIM], F32).ap()
        counts = sb("counts", [P, COUNTS], I32)
        m0 = sb("m0", [P, TILES, GH])
        den = sb("den", [P, TILES, GH])
        num = sb("num", [P, TILES, GAT])
        t4 = sb("t4", [P, TILES, GH])
        t4b = sb("t4b", [P, TILES, GH])
        asrc = hg_all[:, :, GAT:GAT + GH]
        adst = hg_all[:, :, GAT + GH:GAT + 2 * GH]
        cload = sem("cload")
        with nc.Block() as block:
            @block.sync
            def _(sp):
                sp.dma_start(counts[:, :], counts_dram).then_inc(cload, 16)
                sp.wait_ge(cload, 16)

        with ExitStack() as c1:
            def sb1(name, shape, dt=F32):
                return c1.enter_context(nc.sbuf_tensor("m1_" + name, shape, dt))

            ps1 = [c1.enter_context(nc.psum_tensor(f"m1_p{k}", [P, 512], F32)) for k in range(4)]
            ps2 = [c1.enter_context(nc.psum_tensor(f"m1_q{k}", [P, 512], F32)) for k in range(2)]
            ps_hist = c1.enter_context(nc.psum_tensor("m1_hist", [P, 512], F32))
            page = sb1("page", [P, COLS * RECORD])
            slotf = sb1("slotf", [P, COLS])
            node_s = fields(page[:, :], 0, I32)
            page_slot = fields(page[:, :], 1)
            rank = fields(page[:, :], 2)
            ok = sb1("ok", [P, COLS])
            ok2 = sb1("ok2", [P, COLS])
            slot_i = sb1("slot_i", [P, COLS], I32)
            lo = sb1("lo", [P, EPP], BF16)
            hi = sb1("hi", [P, EPP], BF16)
            bins_i = sb1("bins_i", [P, P, HB], I32)
            bins = sb1("bins", [P, P, HB], BF16)
            oh_lo = sb1("oh_lo", [P, 2, P, HB], BF16)
            oh_hi = sb1("oh_hi", [P, 2, HI, HB], BF16)
            zeros = sb1("zeros", [P, P], BF16)
            w1 = sb1("w1", [P, GE, HID])
            b1 = sb1("b1", [P, GE * 2])
            w2 = sb1("w2", [P, GE, 2, DIM])
            b2 = sb1("b2", [1, GE * DIM])
            ones = sb1("ones", [1, P])
            xg = sb1("xg", [P, 2, MG])
            hh = sb1("hh", [P, GE * 2, MG])
            yb = sb1("yb", [P, 4, GE * DIM])
            prime = sb1("prime", [1, 4 + NBUF, COUNTS], I32)
            fill = sb1("fill", [P, K, ROW])
            nclamp = sb1("nclamp", [P, TILES])
            last = sb1("last", [P, ROW])
            has = sb1("has", [P, TILES])
            round_lo = sb1("round_lo", [P, 1])
            src8 = sb1("src8", [P, NBUF, GB], I32)
            slot8 = sb1("slot8", [P, NBUF, GB], I32)
            rows = sb1("rows", [P, NBUF, GB, ROW])
            ell = sb1("ell", [P, 2, GT * K * ROW])
            zk = sb1("zk", [P, GT * K * GH])
            zl = sb1("zl", [P, GT * K * GH])
            mx = sb1("mx", [P, GT, GH])
            m1 = sb1("m1", [P, GT, GH])
            sc = sb1("sc", [P, GT, GH])
            prod = sb1("prod", [P, GT * K * GAT])
            part = sb1("part", [P, GT, GAT])

            S = {n: c1.enter_context(nc.semaphore("m1_" + n)) for n in (
                "wl", "small", "consts", "xl0", "xl1", "l1", "gelu", "l2", "ysb", "yst0", "yst1", "yst2", "yst3",
                "filled", "keys", "lists", "lists_free", "pool", "pidx", "gat0", "gat1", "gat2", "gat3", "sca0", "sca1", "sca2", "sca3", "scattered", "made", "free", "hist", "ell0", "ell1", "ellfree",
                "dve", "dvg", "carrier", "ex_in", "ex_out", "init")}
            gat = [S[f"gat{u}"] for u in range(NBUF)]
            sca = [S[f"sca{u}"] for u in range(NBUF)]
            els = [S["ell0"], S["ell1"]]
            xls = [S["xl0"], S["xl1"]]
            yst = [S[f"yst{t}"] for t in range(4)]
            HALF = "(t p k) c -> p t (k c)"

            with nc.Block() as block:
                @block.sync
                def _(sp):
                    for dst, src in ((lo[:, :], hist_keys[0]), (hi[:, :], hist_keys[1])):
                        sp.dma_start(dst, src).then_inc(S["keys"], 16)
                    sp.dma_start(last[:, :], table[NODES - 1].partition_broadcast(P)).then_inc(S["small"], 16)
                    nr = sp.value_load(counts[0:1, 2:3], min_val=1, max_val=EDGES // K)
                    ne = sp.value_load(counts[0:1, 0:1], min_val=1, max_val=EPOCHS)
                    sp.wait_ge(S["consts"], 3)
                    sl = slots.rearrange(HALF, p=P, k=K)
                    with sp.Fori(0, nr) as ro:
                        for g in range(GROUPS):
                            sp.dma_start(sl[:, g * GT:(g + 1) * GT],
                                         fill[:, :, :].rearrange("p k c -> p (k c)").unsqueeze(1).to_broadcast([P, GT, K * ROW])
                                         ).then_inc(S["filled"], 16)
                        with sp.Fori(0, ne) as ep:
                            sp.wait_ge(S["lists_free"], ro * ne + ep + 1)
                            sp.sem_inc(S["carrier"], 1)
                            sp.dma_start(page[:, :], lists[bass.ds(ep, 1)].squeeze(0)).then_inc(S["lists"], 16)
                        sp.wait_ge(S["scattered"], ro + 1)
                        for g in range(GROUPS):
                            u = g % 2
                            sp.wait_ge(S["ellfree"], ro * GROUPS + g + 1)
                            sp.dma_start(ell[:, u].rearrange("p (t n) -> p t n", t=GT),
                                         sl[:, g * GT:(g + 1) * GT]).then_inc(els[u], 16)
                        sp.wait_ge(S["ellfree"], ro * GROUPS + GROUPS + 2)
                        sp.sem_inc(S["carrier"], 1)

                @block.gpsimd
                def _(pool):
                    nc.gpsimd.memset(ones[:, :], 1.0).then_inc(S["consts"], 1)
                    nc.gpsimd.memset(fill[:, :, 0:GAT], 0.0).then_inc(S["consts"], 1)
                    nc.gpsimd.memset(fill[:, :, GAT:ROW], EMPTY).then_inc(S["consts"], 1)
                    nc.gpsimd.memset(zeros[:, :], 0.0).then_inc(S["consts"], 1)
                    nc.gpsimd.iota(bins_i[:, :, :], pattern=[[1, P], [0, HB]], base=0,
                                   channel_multiplier=0).then_inc(S["consts"], 1)
                    nc.gpsimd.memset(round_lo[:, :], 0.0).then_inc(S["consts"], 1)
                    pool.sem_inc(S["lists_free"], 1)
                    nr = pool.value_load(counts[0:1, 2:3], min_val=1, max_val=EDGES // K)
                    ne = pool.value_load(counts[0:1, 0:1], min_val=1, max_val=EPOCHS)
                    NPE = 9

                    def gathers(u):
                        for k in range(GB):
                            nc.gpsimd.indirect_dma_start(
                                out=rows[:, u, k], out_offset=None, in_=table,
                                in_offset=bass.IndirectOffsetOnAxis(ap=src8[:, u, k:k + 1].bitcast(U32), axis=0)
                            ).then_inc(gat[u], 16)

                    def scatters(u):
                        for k in range(GB):
                            nc.gpsimd.indirect_dma_start(
                                out=slots, out_offset=bass.IndirectOffsetOnAxis(ap=slot8[:, u, k:k + 1].bitcast(U32), axis=0),
                                in_=rows[:, u, k], in_offset=None, bounds_check=CAP - 1, oob_is_err=False
                            ).then_inc(sca[u], 16)

                    pool.wait_ge(S["consts"], 6)
                    with pool.Fori(0, nr) as ro:
                        with pool.Fori(0, ne) as ep:
                            q = ro * ne + ep
                            k = 0

                            def link(ins):
                                nonlocal k
                                k += 1
                                ins.then_inc(S["pool"], 1)
                                pool.wait_ge(S["pool"], q * NPE + ro + k)
                                pool.sem_inc(S["carrier"], 1)
                            for u in range(NBUF):
                                pool.dma_start(prime[:, u], counts_dram[0:1, :]).then_inc(sca[u], 16)
                            pool.wait_ge(S["lists"], 16 * (q + 1))
                            pool.sem_inc(S["carrier"], 1)
                            g_ts, g_tt = nc.gpsimd.tensor_scalar, nc.gpsimd.tensor_tensor
                            link(g_ts(rank, rank, round_lo[:, 0:1], None, ALU.subtract))
                            link(g_ts(ok[:, :], rank, 0.0, None, ALU.is_ge))
                            link(g_ts(ok2[:, :], rank, float(K), None, ALU.is_lt))
                            link(g_tt(ok[:, :], ok[:, :], ok2[:, :], ALU.mult))
                            link(g_ts(slotf[:, :], page_slot, round_lo[:, 0:1], None, ALU.subtract))
                            link(g_tt(slotf[:, :], slotf[:, :], ok[:, :], ALU.mult))
                            link(g_ts(ok[:, :], ok[:, :], -OUTSIDE, OUTSIDE, ALU.mult, ALU.add))
                            link(g_tt(slotf[:, :], slotf[:, :], ok[:, :], ALU.add))
                            link(nc.gpsimd.tensor_copy(slot_i[:, :], slotf[:, :]))
                            assert k == NPE
                            pool.wait_ge(S["filled"], (ro + 1) * 16 * GROUPS)
                            pool.sem_inc(S["carrier"], 1)
                            turns = pool.value_load(counts[0:1, bass.ds(ep + 3, 1)], min_val=1, max_val=COLS // TURN_COLS)
                            with pool.Fori(0, turns) as it:
                                for u in range(NBUF):
                                    pool.wait_ge(sca[u], 16 * GB * it + 16)
                                    pool.sem_inc(S["carrier"], 1)
                                    c8 = bass.ds((it * NBUF + u) * GB, GB)
                                    nc.gpsimd.tensor_copy(src8[:, u], node_s[:, c8]).then_inc(S["pidx"], 1)
                                    nc.gpsimd.tensor_copy(slot8[:, u], slot_i[:, c8]).then_inc(S["pidx"], 1)
                                    pool.wait_ge(S["pidx"], it * 2 * NBUF + 2 * u + 2)
                                    pool.sem_inc(S["carrier"], 1)
                                    gathers(u)
                                    if u:
                                        pool.wait_ge(gat[u - 1], 16 * GB * (it + 1))
                                        pool.sem_inc(S["carrier"], 1)
                                        scatters(u - 1)
                                pool.wait_ge(gat[NBUF - 1], 16 * GB * (it + 1))
                                pool.sem_inc(S["carrier"], 1)
                                scatters(NBUF - 1)
                            for u in range(NBUF):
                                pool.wait_ge(sca[u], turns * (16 * GB) + 16)
                            pool.sem_inc(S["carrier"], 1)
                            pool.dma_reset(range(gat[0].num, gat[0].num + 2 * NBUF))
                            pool.sem_clear(range(gat[0].num, gat[0].num + 2 * NBUF))
                            pool.sem_clear(S["pidx"])
                            pool.sem_inc(S["lists_free"], 1)
                        nc.gpsimd.tensor_scalar(round_lo[:, :], round_lo[:, :], float(K), None, ALU.add).then_inc(S["pool"], 1)
                        pool.wait_ge(S["pool"], (ro * ne + ne) * NPE + ro + 1)
                        pool.sem_inc(S["scattered"], 1)

                @block.vector
                def _(dve):
                    cnt = [0]

                    def link(ins):
                        cnt[0] += 1
                        ins.then_inc(S["dve"], 1)
                        dve.wait_ge(S["dve"], cnt[0])

                    def bt(ap):
                        return ap.unsqueeze(2).to_broadcast([P, TILES, GH])

                    def lrelu(dst, src):
                        return nc.vector.scalar_tensor_tensor(out=dst, in0=src, scalar=GAT_SLOPE, in1=src,
                                                              op0=ALU.mult, op1=ALU.max)

                    dve.wait_ge(S["consts"], 6)
                    link(nc.vector.tensor_copy(bins[:, :, :], bins_i[:, :, :]))
                    dve.wait_ge(S["keys"], 32)
                    with dve.Fori(0, EPP // HB // 2) as i:
                        for u in (0, 1):
                            c = bass.ds((2 * i + u) * HB, HB)
                            dve.wait_ge(S["free"], 2 * i + u + 1)
                            nc.vector.tensor_tensor(oh_lo[:, u], lo[:, c].unsqueeze(1).to_broadcast([P, P, HB]),
                                                    bins[:, :, :], ALU.is_equal).then_inc(S["made"], 1)
                            nc.vector.tensor_tensor(oh_hi[:, u], hi[:, c].unsqueeze(1).to_broadcast([P, HI, HB]),
                                                    bins[:, 0:HI, :], ALU.is_equal).then_inc(S["made"], 1)
                    dve.wait_ge(S["hist"], 1)
                    link(nc.vector.tensor_copy(nclamp[:, :], ps_hist[:, 0:HI]))
                    dve.wait_ge(S["small"], 16)
                    zc = t4b
                    link(nc.vector.tensor_tensor(t4[:, :, :], asrc, adst, ALU.add))
                    link(lrelu(t4[:, :, :], t4[:, :, :]))
                    link(nc.vector.tensor_tensor(zc[:, :, :], adst,
                                                 last[:, GAT:ROW].unsqueeze(1).to_broadcast([P, TILES, GH]), ALU.add))
                    link(lrelu(zc[:, :, :], zc[:, :, :]))
                    link(nc.vector.tensor_scalar(has[:, :], nclamp[:, :], 0.0, None, ALU.is_gt))
                    link(nc.vector.tensor_tensor(m0[:, :, :], zc[:, :, :], bt(has[:, :]), ALU.mult))
                    link(nc.vector.tensor_scalar(has[:, :], has[:, :], 1.0, -EMPTY, ALU.subtract, ALU.mult))
                    link(nc.vector.tensor_tensor(m0[:, :, :], m0[:, :, :], bt(has[:, :]), ALU.add))
                    link(nc.vector.tensor_tensor(m0[:, :, :], m0[:, :, :], t4[:, :, :], ALU.max))
                    link(nc.vector.tensor_tensor(t4[:, :, :], t4[:, :, :], m0[:, :, :], ALU.subtract))
                    link(nc.vector.tensor_tensor(zc[:, :, :], zc[:, :, :], m0[:, :, :], ALU.subtract))
                    link(nc.vector.tensor_scalar(zc[:, :, :], zc[:, :, :], 0.0, None, ALU.min))
                    dve.sem_inc(S["init"], 1)
                    dve.wait_ge(S["init"], 3)
                    link(nc.vector.tensor_tensor(zc[:, :, :], zc[:, :, :], bt(nclamp[:, :]), ALU.mult))
                    link(nc.vector.tensor_tensor(den[:, :, :], zc[:, :, :], t4[:, :, :], ALU.add))
                    for h in range(GH):
                        q = slice(h * GE, (h + 1) * GE)
                        link(nc.vector.tensor_tensor(num[:, :, q], hg_all[:, :, q], t4[:, :, h:h + 1].to_broadcast([P, TILES, GE]), ALU.mult))
                        link(nc.vector.tensor_tensor(prod[:, 0:TILES * GE].rearrange("p (t e) -> p t e", t=TILES),
                                                     last[:, q].unsqueeze(1).to_broadcast([P, TILES, GE]),
                                                     zc[:, :, h:h + 1].to_broadcast([P, TILES, GE]), ALU.mult))
                        link(nc.vector.tensor_tensor(num[:, :, q], num[:, :, q],
                                                     prod[:, 0:TILES * GE].rearrange("p (t e) -> p t e", t=TILES), ALU.add))
                    nr = dve.value_load(counts[0:1, 2:3], min_val=1, max_val=EDGES // K)
                    dve.sem_inc(S["ellfree"], 2)
                    NG = 14 * GROUPS
                    with dve.Fori(0, nr) as ro:
                        gk = 0

                        def link(ins):
                            nonlocal gk
                            gk += 1
                            ins.then_inc(S["dvg"], 1)
                            dve.wait_ge(S["dvg"], ro * NG + gk)
                        for g in range(GROUPS):
                            u = g % 2
                            gt = slice(g * GT, (g + 1) * GT)
                            E3 = ell[:, u].rearrange("p (t k c) -> p t k c", t=GT, k=K)
                            Ef = ell[:, u].rearrange("p (n c) -> p n c", c=ROW)
                            zk4 = zk[:, :].rearrange("p (t k h) -> p t k h", t=GT, k=K)
                            zl4 = zl[:, :].rearrange("p (t k h) -> p t k h", t=GT, k=K)

                            def over_k(ap):
                                return ap.unsqueeze(2).to_broadcast([P, GT, K, GH])
                            dve.wait_ge(els[u], ro * (16 * GROUPS // 2) + 16 * (g // 2 + 1))
                            link(nc.vector.tensor_tensor(zk4, E3[:, :, :, GAT:ROW], over_k(adst[:, gt]), ALU.add))
                            link(lrelu(zl[:, :], zk[:, :]))
                            link(nc.vector.tensor_reduce(mx[:, :, :], zl4.rearrange("p t k h -> p t h k"), AX.X, ALU.max))
                            link(nc.vector.tensor_tensor(m1[:, :, :], mx[:, :, :], m0[:, gt], ALU.max))
                            link(nc.vector.tensor_tensor(sc[:, :, :], m0[:, gt], m1[:, :, :], ALU.subtract))
                            link(nc.vector.tensor_copy(m0[:, gt], m1[:, :, :]))
                            link(nc.vector.tensor_tensor(zk4, zl4, over_k(m1[:, :, :]), ALU.subtract))
                            dve.sem_inc(S["ex_in"], 1)
                            dve.wait_ge(S["ex_out"], ro * GROUPS + g + 1)
                            link(nc.vector.tensor_reduce(mx[:, :, :], zk4.rearrange("p t k h -> p t h k"), AX.X, ALU.add))
                            link(nc.vector.tensor_tensor(den[:, gt], den[:, gt], sc[:, :, :], ALU.mult))
                            link(nc.vector.tensor_tensor(den[:, gt], den[:, gt], mx[:, :, :], ALU.add))
                            link(nc.vector.tensor_tensor(prod[:, :].rearrange("p (n h e) -> p n h e", h=GH, e=GE),
                                                         Ef[:, :, 0:GAT].rearrange("p n (h e) -> p n h e", h=GH),
                                                         zk[:, :].rearrange("p (n h) -> p n h", h=GH).unsqueeze(3)
                                                         .to_broadcast([P, GT * K, GH, GE]), ALU.mult))
                            dve.sem_inc(S["ellfree"], 1)
                            link(nc.vector.tensor_reduce(part[:, :, :], prod[:, :].rearrange("p (t k f) -> p t f k", t=GT, k=K),
                                                         AX.X, ALU.add))
                            n4 = num[:, gt].rearrange("p t (h e) -> p t h e", h=GH)
                            link(nc.vector.tensor_tensor(n4, n4, sc[:, :, :].unsqueeze(3).to_broadcast([P, GT, GH, GE]), ALU.mult))
                            link(nc.vector.tensor_tensor(num[:, gt], num[:, gt], part[:, :, :], ALU.add))
                        assert gk == NG, gk

                @block.tensor
                def _(pe):
                    pe.sem_inc(S["free"], 2)
                    pe.wait_ge(S["consts"], 6)
                    nc.tensor.matmul(ps_hist[:, 0:HI], zeros[:, :], zeros[:, 0:HI], start=True, stop=False,
                                     skip_group_check=True)
                    pe.wait_ge(S["wl"], 64)
                    HPG = EPP // HB // (NODES // MG)

                    def hist_batch(g, n):
                        u = n % 2
                        pe.wait_ge(S["made"], 2 * (g * HPG + n + 1))
                        for c in range(HB):
                            mm = nc.tensor.matmul(ps_hist[:, 0:HI], oh_lo[:, u, :, c], oh_hi[:, u, :, c], start=False,
                                                  stop=False, skip_group_check=True)
                        mm.then_inc(S["free"], 1)

                    with pe.Fori(0, NODES // MG // 2) as i:
                        for u in (0, 1):
                            g = 2 * i + u
                            pe.wait_ge(xls[u], 16 * (i + 1))
                            for c in range(GE * 2):
                                pe.wait_ge(S["gelu"], g * 8 + c + 1)
                                mm = nc.tensor.matmul(ps1[c % 4][:, :], w1[:, c // 2, (c % 2) * P:(c % 2 + 1) * P], xg[:, u],
                                                      start=True, stop=True)
                                mm.then_inc(S["l1"], 1)
                                hist_batch(g, c)
                            pe.wait_ge(S["gelu"], g * 8 + 8 + 4)
                            for t in range(4):
                                pe.wait_ge(S["ysb"], g * 4 + t + 1)
                                for e in range(GE):
                                    nc.tensor.matmul(ps2[t % 2][:, e * DIM:(e + 1) * DIM], ones[:, :],
                                                     b2[:, e * DIM:(e + 1) * DIM], start=True, stop=False)
                                    for c in (0, 1):
                                        mm = nc.tensor.matmul(ps2[t % 2][:, e * DIM:(e + 1) * DIM], hh[:, 2 * e + c, t * P:(t + 1) * P],
                                                              w2[:, e, c], start=False, stop=(c == 1))
                                mm.then_inc(S["l2"], 1)
                                hist_batch(g, 8 + 2 * t)
                                hist_batch(g, 9 + 2 * t)
                    nc.tensor.matmul(ps_hist[:, 0:HI], zeros[:, :], zeros[:, 0:HI], start=False, stop=True,
                                     skip_group_check=True).then_inc(S["hist"], 1)

                @block.scalar
                def _(act):
                    for dst, src in ((w1[:, :, :], w["W1"].rearrange("e d h -> d e h")), (b1[:, :], w["b1T"]),
                                     (w2[:, :, :, :].rearrange("p e c o -> p (e c) o"),
                                      w["W2"].rearrange("e (c p) o -> p (e c) o", p=P)),
                                     (b2[:, :], w["b2"].rearrange("e o -> (e o)").unsqueeze(0))):
                        act.dma_start(dst, src).then_inc(S["wl"], 16)
                    for t in range(4):
                        act.dma_start(prime[:, NBUF + t], counts_dram[0:1, :]).then_inc(yst[t], 16)
                    act.sem_inc(S["gelu"], 4)
                    act.sem_inc(S["l2"], 4)
                    act.sem_inc(S["ysb"], 2)
                    for u in (0, 1):
                        act.dma_start(xg[:, u], xT_dram[:, u * MG:(u + 1) * MG]).then_inc(xls[u], 16)
                    act.wait_ge(S["wl"], 64)
                    def groups(i, more):
                        for u in (0, 1):
                            g = 2 * i + u
                            for c in range(GE * 2):
                                act.wait_ge(S["l1"], g * 8 + c + 1)
                                if c == 0:
                                    act.wait_ge(S["l2"], g * 4 + 4)
                                nc.scalar.activation(hh[:, c], ps1[c % 4][:, :], ACT.Gelu, bias=b1[:, c:c + 1]).then_inc(S["gelu"], 1)
                            if more:
                                act.dma_start(xg[:, u], xT_dram[:, bass.ds((g + 2) * MG, MG)]).then_inc(xls[u], 16)
                            for t in range(4):
                                act.wait_ge(S["l2"], g * 4 + t + 5)
                                act.wait_ge(yst[t], 16 * g + 16)
                                nc.scalar.copy(yb[:, t], ps2[t % 2][:, :]).then_inc(S["ysb"], 1)
                                act.wait_ge(S["ysb"], g * 4 + t + 3)
                                act.dma_start(Y[bass.ds(g * 4 + t, 1)].squeeze(0) if more else Y[g * 4 + t],
                                              yb[:, t]).then_inc(yst[t], 16)

                    pairs = NODES // MG // 2
                    with act.Fori(0, pairs - 1) as i:
                        groups(i, True)
                    groups(pairs - 1, False)
                    act.wait_ge(S["init"], 1)
                    nc.scalar.activation(t4[:, :, :], t4[:, :, :], ACT.Exp).then_inc(S["init"], 1)
                    nc.scalar.activation(t4b[:, :, :], t4b[:, :, :], ACT.Exp).then_inc(S["init"], 1)
                    for t in range(4):
                        act.wait_ge(yst[t], 16 * (NODES // MG) + 16)
                    nr = act.value_load(counts[0:1, 2:3], min_val=1, max_val=EDGES // K)
                    with act.Fori(0, nr) as ro:
                        for g in range(GROUPS):
                            act.wait_ge(S["ex_in"], ro * GROUPS + g + 1)
                            nc.scalar.activation(sc[:, :, :], sc[:, :, :], ACT.Exp)
                            nc.scalar.activation(zk[:, :], zk[:, :], ACT.Exp).then_inc(S["ex_out"], 1)

        with ExitStack() as c2:
            def sb2(name, shape, dt=F32):
                return c2.enter_context(nc.sbuf_tensor("m2_" + name, shape, dt))
            bg = sb2("bg", [P, GAT])
            gam = sb2("gam", [P, GAT])
            bet = sb2("bet", [P, GAT])
            a1 = sb2("a1", [P, TILES, GAT])
            a2 = sb2("a2", [P, TILES, GAT])
            r1 = sb2("r1", [P, TILES])
            r2 = sb2("r2", [P, TILES])
            hf = sb2("hf", [P, TILES])
            s4 = sb2("s4", [P, TILES, GE])
            rk = sb2("rk", [P, TILES, GE])
            cmp = sb2("cmp", [P, TILES])
            g4 = sb2("g4", [P, TILES, GE])
            NG = 4
            NY = 8
            yl = sb2("yl", [P, NY, NG, GE * DIM])
            S2 = {n: c2.enter_context(nc.semaphore("m2_" + n)) for n in
                  ("ld", "carrier", "dve", "pw", "pwd", "ex", "exd", "y0", "y1", "y2", "y3", "y4", "y5", "y6", "y7", "yfree", "comb", "od", "stored")}
            ys = [S2[f"y{t}"] for t in range(NY)]
            xo = out.rearrange("(t b) n d -> (b n) t d", b=2)
            OG = 8
            with nc.Block() as block:
                @block.sync
                def _(sp):
                    for dst, src in ((bg, w["b_gat"]), (gam, w["gamma"]), (bet, w["beta"])):
                        sp.dma_start(dst[:, :], src.partition_broadcast(P)).then_inc(S2["ld"], 16)
                    with sp.Fori(0, TILES // NY // NG) as i:
                        for g in range(NY):
                            sp.wait_ge(S2["yfree"], i * NY + g + 1)
                            sp.sem_inc(S2["carrier"], 1)
                            sp.dma_start(yl[:, g], Y[bass.ds((i * NY + g) * NG, NG)].rearrange("t p o -> p t o")
                                         ).then_inc(ys[g], 16)
                    for g in range(NY):
                        sp.wait_ge(ys[g], 16 * (TILES // NY // NG))

                @block.gpsimd
                def _(pool):
                    nc.gpsimd.memset(hf[:, :], -0.5).then_inc(S2["pw"], 1)
                    pool.wait_ge(S2["pw"], 2)
                    nc.gpsimd.tensor_tensor(r2[:, :], r1[:, :], hf[:, :], ALU.pow).then_inc(S2["pwd"], 1)

                @block.scalar
                def _(act):
                    act.wait_ge(S2["ex"], 1)
                    nc.scalar.activation(g4[:, :, :], g4[:, :, :], ACT.Exp).then_inc(S2["exd"], 1)
                    with act.Fori(0, TILES // OG) as i:
                        act.wait_ge(S2["comb"], OG * i + OG)
                        act.dma_start(xo[:, bass.ds(i * OG, OG)], x_all[:, bass.ds(i * OG, OG)]).then_inc(S2["stored"], 16)
                    act.wait_ge(S2["stored"], 16 * (TILES // OG))

                @block.vector
                def _(dve):
                    cnt = [0]

                    def link(ins):
                        cnt[0] += 1
                        ins.then_inc(S2["dve"], 1)
                        dve.wait_ge(S2["dve"], cnt[0])
                    tt, ts, red = nc.vector.tensor_tensor, nc.vector.tensor_scalar, nc.vector.tensor_reduce

                    def f16(ap):
                        return ap.unsqueeze(2).to_broadcast([P, TILES, GAT])

                    def row(ap):
                        return ap[:, :].unsqueeze(1).to_broadcast([P, TILES, GAT])
                    dve.sem_inc(S2["yfree"], NY)
                    dve.wait_ge(S2["ld"], 48)
                    link(ts(den[:, :, :], den[:, :, :], 1e-16, None, ALU.add))
                    link(nc.vector.reciprocal(den[:, :, :], den[:, :, :]))
                    for h in range(GH):
                        q = slice(h * GE, (h + 1) * GE)
                        link(tt(a1[:, :, q], num[:, :, q], den[:, :, h:h + 1].to_broadcast([P, TILES, GE]), ALU.mult))
                    link(tt(a1[:, :, :], a1[:, :, :], row(bg), ALU.add))
                    link(red(r1[:, :], a1[:, :, :], AX.X, ALU.add))
                    link(ts(r1[:, :], r1[:, :], 1.0 / GAT, None, ALU.mult))
                    link(tt(a1[:, :, :], a1[:, :, :], f16(r1[:, :]), ALU.subtract))
                    link(tt(a2[:, :, :], a1[:, :, :], a1[:, :, :], ALU.mult))
                    link(red(r1[:, :], a2[:, :, :], AX.X, ALU.add))
                    link(ts(r1[:, :], r1[:, :], 1.0 / GAT, EPS, ALU.mult, ALU.add))
                    dve.sem_inc(S2["pw"], 1)
                    dve.wait_ge(S2["pwd"], 1)
                    link(tt(a1[:, :, :], a1[:, :, :], f16(r2[:, :]), ALU.mult))
                    link(tt(a1[:, :, :], a1[:, :, :], row(gam), ALU.mult))
                    link(tt(a1[:, :, :], a1[:, :, :], row(bet), ALU.add))
                    link(red(s4[:, :, :], a1[:, :, :].rearrange("p t (h e) -> p t e h", h=GH), AX.X, ALU.add))
                    link(ts(s4[:, :, :], s4[:, :, :], 1.0 / GH, None, ALU.mult))
                    link(nc.vector.memset(rk[:, :, :], 0.0))
                    for e in range(GE):
                        for o in range(GE):
                            if o != e:
                                link(tt(cmp[:, :], s4[:, :, o], s4[:, :, e], ALU.is_ge if o < e else ALU.is_gt))
                                link(tt(rk[:, :, e], rk[:, :, e], cmp[:, :], ALU.add))
                    link(red(r1[:, :], s4[:, :, :], AX.X, ALU.max))
                    link(tt(g4[:, :, :], s4[:, :, :], r1[:, :].unsqueeze(2).to_broadcast([P, TILES, GE]), ALU.subtract))
                    dve.sem_inc(S2["ex"], 1)
                    dve.wait_ge(S2["exd"], 1)
                    link(nc.vector.scalar_tensor_tensor(out=g4[:, :, :], in0=rk[:, :, :], scalar=2.0, in1=g4[:, :, :],
                                                        op0=ALU.is_lt, op1=ALU.mult))
                    link(red(r1[:, :], g4[:, :, :], AX.X, ALU.add))
                    link(nc.vector.reciprocal(r1[:, :], r1[:, :]))
                    link(tt(g4[:, :, :], g4[:, :, :], r1[:, :].unsqueeze(2).to_broadcast([P, TILES, GE]), ALU.mult))
                    with dve.Fori(0, TILES // NY // NG) as i:
                        for g in range(NY):
                            dve.wait_ge(ys[g], 16 * (i + 1))
                            dve.sem_inc(S2["carrier"], 1)
                            tiles = bass.ds((i * NY + g) * NG, NG)
                            x4, gates = x_all[:, tiles, :], g4[:, tiles, :]
                            for e in range(GE):
                                for t in range(NG):
                                    if e:
                                        dve.wait_ge(S2["od"], (i * NY + g) * NG * (GE - 1) + (e - 1) * NG + t + 1)
                                    xt, gs = x4[:, t], gates[:, t, e:e + 1]
                                    nc.vector.scalar_tensor_tensor(
                                        out=xt, in0=yl[:, g, t, e * DIM:(e + 1) * DIM], scalar=gs, in1=xt, op0=ALU.mult,
                                        op1=ALU.add).then_inc(S2["od"] if e < GE - 1 else S2["comb"], 1)
                            dve.wait_ge(S2["comb"], (i * NY + g + 1) * NG)
                            dve.sem_inc(S2["yfree"], 1)


_ARGS = ("x", "adj", "adjT", "fcT", "fp", "fcbT", "q_w", "k_w", "q_b", "k_b", "fp_b", "WiT", "biT", "WoT", "bo", "gWT",
         "gb", "Wgat", "att_src", "att_dst", "route", "WsT", "bsT", "WrT", "brT", "b_gat", "gamma", "beta", "W1", "b1T",
         "W2", "b2", "edges")


def program(nc, w, out):
    lists = nc.dram_tensor("edge_lists", [EPOCHS, P, COLS * RECORD], F32).ap()
    hist_keys = nc.dram_tensor("hist_keys", [2, P, EPP], BF16).ap()
    counts = nc.dram_tensor("loop_counts", [P, COUNTS], I32).ap()
    expert_w = nc.dram_tensor("expert_weights", [EXP0, P, WROW], F32).ap()
    xT = nc.dram_tensor("features_T", [P, NODES], F32).ap()
    table = nc.dram_tensor("gat_table", [NODES, ROW], F32).ap()
    with ExitStack() as ctx:
        records = ctx.enter_context(nc.sbuf_tensor("first_records", [P, PLACED * RECORD], F32))
        place = ctx.enter_context(nc.sbuf_tensor("first_places", [P, PLACED], I32))
        sort_edges(nc, w["edges"], hist_keys, lists, counts, records, place, w, expert_w)
        x_all = ctx.enter_context(nc.sbuf_tensor("x_all", [P, TILES, DIM], F32))
        hg_all = ctx.enter_context(nc.sbuf_tensor("hg_all", [P, TILES, COLS24], F32))
        node_layers(nc, w, x_all, hg_all, xT, table, records, place, lists, expert_w)
        edge_and_expert_layers(nc, w, x_all, hg_all, xT, table, hist_keys, lists, counts, out)


def kernel(**inputs):
    import numpy as np
    import concourse.bacc as bacc
    from concourse.bass_utils import run_bass_kernel_spmd

    g = {k: np.asarray(v) for k, v in inputs.items()}

    def lay(a):
        return np.ascontiguousarray(a)

    C = HID // P
    host = {
        "x": g["x"], "adj": g["adj"], "adjT": lay(g["adj"].transpose(0, 2, 1)),
        "fcT": lay(g["L0_gnn_fc_w"].T), "fp": g["L0_gnn_fp_w"],
        "fcbT": lay(g["L0_gnn_fc_b"].reshape(HEADS, DIM).T),
        "q_w": g["L0_gnn_q_w"], "k_w": g["L0_gnn_k_w"], "q_b": g["L0_gnn_q_b"], "k_b": g["L0_gnn_k_b"],
        "fp_b": g["L0_gnn_fp_b"],
        "WiT": lay(g["L0_ffn_Wi"].T), "biT": lay(g["L0_ffn_bi"].reshape(C, P).T),
        "WoT": lay(g["L0_ffn_Wo"].T), "bo": g["L0_ffn_bo"],
        "gWT": lay(g["L1_gnn_W"].T), "gb": g["L1_gnn_b"], "Wgat": g["L1_ffn_W_gat"],
        "att_src": lay(g["L1_ffn_att_src"].reshape(-1)), "att_dst": lay(g["L1_ffn_att_dst"].reshape(-1)),
        "route": g["L0_ffn_route_id"],
        "WsT": lay(g["L0_ffn_Ws"][:, 0].transpose(0, 2, 1).reshape(LAYERS, C, P, HID).transpose(2, 0, 1, 3)
                   .reshape(P, LAYERS * C * HID)),
        "bsT": lay(g["L0_ffn_bs"].reshape(LAYERS, C, P).transpose(2, 0, 1).reshape(P, LAYERS * C)),
        "WrT": lay(g["L0_ffn_Wr"].transpose(1, 0, 3, 2).reshape(EXP0, LAYERS, C, P, HID).transpose(0, 3, 1, 2, 4)
                   .reshape(EXP0, P, LAYERS * C * HID)),
        "brT": lay(g["L0_ffn_br"].reshape(LAYERS, EXP0, C, P).transpose(1, 3, 0, 2).reshape(EXP0, P, LAYERS * C)),
        "b_gat": g["L1_ffn_b_gat"], "gamma": g["L1_ffn_ln_gamma"], "beta": g["L1_ffn_ln_beta"],
        "W1": g["L1_ffn_W1"], "b1T": lay(g["L1_ffn_b1"].reshape(GE * C, P).T), "W2": g["L1_ffn_W2"],
        "b2": g["L1_ffn_b2"], "edges": g["L1_ffn_edge_index"],
    }
    nc = bacc.Bacc("TRN2", target_bir_lowering=False, num_devices=1)
    arrays, w = {}, {}
    for name in _ARGS:
        arrays["in_" + name] = host[name]
        w[name] = nc.dram_tensor("in_" + name, host[name].shape, mybir.dt.from_np(host[name].dtype),
                                 kind="ExternalInput").ap()
    out = nc.dram_tensor("out_x", (TILES * 2, NB, DIM), F32, kind="ExternalOutput").ap()
    program(nc, w, out)
    got = run_bass_kernel_spmd(nc, [arrays], core_ids=[0])
    return got.results[0]["out_x"]
```
